# Optimizing a Trainium2 kernel written in Bass

```python
import numpy as np
import jax
import jax.numpy as jnp

def _softmax(x, axis=-1):
    return jax.nn.softmax(x, axis=axis)

def _gelu(x):
    return jax.nn.gelu(x, approximate=True)

def _silu(x):
    return jax.nn.silu(x)

def _sigmoid(x):
    return jax.nn.sigmoid(x)

def _layernorm(x, axis=-1, eps=1e-05):
    m = jnp.mean(x, axis=axis, keepdims=True)
    v = jnp.var(x, axis=axis, keepdims=True)
    return (x - m) / jnp.sqrt(v + eps)

def _scatter_add(tgt, idx, src, axis=0):
    return tgt.at[idx].add(src)

def _segment_sum(src, seg, n):
    return jax.ops.segment_sum(src, seg, n)
kernel_name = 'mk_sandwich_d2_jaxref_r8_c09c84'

def setup_inputs(seed: int=0):
    np.random.seed(seed)
    _w = jnp.asarray

    def _L0_attn_setup():
        import math
        import jax, jax.numpy as jnp
        import numpy as np
        EPS = 1e-06
        NEG = -1000000000.0

        def rms_norm(x):
            return x * jax.lax.rsqrt(jnp.mean(x * x, axis=-1, keepdims=True) + EPS)

        def apply_rope(x, cos, sin):
            d2 = x.shape[-1] // 2
            x1, x2 = (x[..., :d2], x[..., d2:])
            c = cos[None, None, :, :]
            s = sin[None, None, :, :]
            return jnp.concatenate([x1 * c - x2 * s, x2 * c + x1 * s], axis=-1)
        key = jax.random.key(seed)
        k1, k2, k3 = jax.random.split(key, 3)
        B, T, C = (2, 256, 128)
        H, D = (16, 64)
        dim_inner = H * D
        x = jax.random.normal(k1, (B, T, C), dtype=jnp.float32)
        w_qkv = jax.random.normal(k2, (3 * dim_inner, C), dtype=jnp.float32) * (1.0 / math.sqrt(C))
        w_out = jax.random.normal(k3, (C, dim_inner), dtype=jnp.float32) * (1.0 / math.sqrt(dim_inner))
        return {'x': x, 'w_qkv': w_qkv, 'w_out': w_out}
    _L0_attn_in = _L0_attn_setup()

    def _L0_ffn_setup():
        import jax, jax.numpy as jnp
        import numpy as np
        LN_EPS = 1e-05

        def layer_norm(x, g, b):
            mu = jnp.mean(x, axis=-1, keepdims=True)
            var = jnp.var(x, axis=-1, keepdims=True)
            return (x - mu) / jnp.sqrt(var + LN_EPS) * g + b

        def balanced_assignment(scores):
            T, E = scores.shape
            C = T // E
            taken = jnp.zeros((T,), dtype=bool)
            parts = []
            for e in range(E):
                s = jnp.where(taken, -jnp.inf, scores[:, e])
                _, idx = jax.lax.top_k(s, C)
                parts.append(idx)
                taken = taken.at[idx].set(True)
            return jnp.concatenate(parts)
        key = jax.random.key(seed)
        ks = jax.random.split(key, 4)
        B, S, D, F, E = (4, 256, 128, 512, 8)
        return {'x': jax.random.normal(ks[0], (B, S, D), dtype=jnp.float32), 'centroids': jax.random.normal(ks[1], (E, D), dtype=jnp.float32) * 0.1, 'ln_g': jnp.ones((D,), dtype=jnp.float32), 'ln_b': jnp.zeros((D,), dtype=jnp.float32), 'w1': jax.random.normal(ks[2], (E, D, F), dtype=jnp.float32) * 0.02, 'b1': jnp.zeros((E, F), dtype=jnp.float32), 'w2': jax.random.normal(ks[3], (E, F, D), dtype=jnp.float32) * 0.02, 'b2': jnp.zeros((E, D), dtype=jnp.float32)}
    _L0_ffn_in = _L0_ffn_setup()

    def _L1_attn_setup():
        import jax, jax.numpy as jnp
        import numpy as np
        BATCH, SEQ, DIM, NH = (4, 256, 128, 16)
        HD = DIM // NH

        def _rope_cos_sin(seq_len, head_dim, dtype=jnp.float32):
            inv_freq = 1.0 / 10000.0 ** (jnp.arange(0, head_dim, 2, dtype=dtype) / head_dim)
            t = jnp.arange(seq_len, dtype=dtype)
            freqs = jnp.outer(t, inv_freq)
            emb = jnp.concatenate([freqs, freqs], axis=-1)
            return (jnp.cos(emb), jnp.sin(emb))

        def _apply_rope(x, cos, sin):
            d2 = x.shape[-1] // 2
            x1, x2 = (x[..., :d2], x[..., d2:])
            c = cos[None, None, :, :d2]
            s = sin[None, None, :, :d2]
            return jnp.concatenate([x1 * c - x2 * s, x1 * s + x2 * c], axis=-1)
        key = jax.random.key(seed)
        ks = jax.random.split(key, 3)
        x = jax.random.normal(ks[0], (BATCH, SEQ, DIM), dtype=jnp.float32)
        Wqkv = jax.random.normal(ks[1], (DIM, 3 * DIM), dtype=jnp.float32) * (1.0 / np.sqrt(DIM))
        bqkv = jnp.zeros((3 * DIM,), dtype=jnp.float32)
        Wout = jax.random.normal(ks[2], (DIM, DIM), dtype=jnp.float32) * (1.0 / np.sqrt(DIM))
        bout = jnp.zeros((DIM,), dtype=jnp.float32)
        return {'x': x, 'Wqkv': Wqkv, 'bqkv': bqkv, 'Wout': Wout, 'bout': bout}
    _L1_attn_in = _L1_attn_setup()

    def _L1_ffn_setup():
        import jax, jax.numpy as jnp
        import numpy as np
        B, S, D_MODEL, D_FF = (4, 256, 128, 512)

        def _quantum_transform(hidden, theta, w_real, w_imag):
            imag = w_imag * jnp.sin(theta + hidden * 0.1)
            quantum_phase = jnp.cos(theta) * w_real + jnp.sin(theta) * w_imag
            return hidden + quantum_phase * imag * 0.1
        key = jax.random.key(seed)
        ks = jax.random.split(key, 8)
        return {'x': jax.random.normal(ks[0], (B, S, D_MODEL), dtype=jnp.float32), 'W1': jax.random.normal(ks[1], (D_MODEL, D_FF), dtype=jnp.float32) * (1.0 / np.sqrt(D_MODEL)), 'b1': jnp.zeros((D_FF,), dtype=jnp.float32), 'quantum_phases': jax.random.normal(ks[2], (D_FF,), dtype=jnp.float32) * (2.0 * np.pi), 'quantum_weights_real': jax.random.normal(ks[3], (D_FF,), dtype=jnp.float32) * 0.1, 'quantum_weights_imag': jax.random.normal(ks[4], (D_FF,), dtype=jnp.float32) * 0.1, 'W2': jax.random.normal(ks[5], (D_FF, D_MODEL), dtype=jnp.float32) * (1.0 / np.sqrt(D_FF)), 'b2': jnp.zeros((D_MODEL,), dtype=jnp.float32)}
    _L1_ffn_in = _L1_ffn_setup()
    _d = {'L0_attn_x': _L0_attn_in['x'], 'L0_attn_w_qkv': _L0_attn_in['w_qkv'], 'L0_attn_w_out': _L0_attn_in['w_out'], 'L0_ffn_centroids': _L0_ffn_in['centroids'], 'L0_ffn_ln_g': _L0_ffn_in['ln_g'], 'L0_ffn_ln_b': _L0_ffn_in['ln_b'], 'L0_ffn_w1': _L0_ffn_in['w1'], 'L0_ffn_b1': _L0_ffn_in['b1'], 'L0_ffn_w2': _L0_ffn_in['w2'], 'L0_ffn_b2': _L0_ffn_in['b2'], 'L1_attn_Wqkv': _L1_attn_in['Wqkv'], 'L1_attn_bqkv': _L1_attn_in['bqkv'], 'L1_attn_Wout': _L1_attn_in['Wout'], 'L1_attn_bout': _L1_attn_in['bout'], 'L1_ffn_W1': _L1_ffn_in['W1'], 'L1_ffn_b1': _L1_ffn_in['b1'], 'L1_ffn_quantum_phases': _L1_ffn_in['quantum_phases'], 'L1_ffn_quantum_weights_real': _L1_ffn_in['quantum_weights_real'], 'L1_ffn_quantum_weights_imag': _L1_ffn_in['quantum_weights_imag'], 'L1_ffn_W2': _L1_ffn_in['W2'], 'L1_ffn_b2': _L1_ffn_in['b2']}
    _x0 = _d['L0_attn_x']
    _d['L0_attn_x'] = jax.random.normal(jax.random.fold_in(jax.random.key(seed), 1), (16, 512, 128), dtype=_x0.dtype)
    del _x0
    return _d

def reference(L0_attn_x, L0_attn_w_qkv, L0_attn_w_out, L0_ffn_centroids, L0_ffn_ln_g, L0_ffn_ln_b, L0_ffn_w1, L0_ffn_b1, L0_ffn_w2, L0_ffn_b2, L1_attn_Wqkv, L1_attn_bqkv, L1_attn_Wout, L1_attn_bout, L1_ffn_W1, L1_ffn_b1, L1_ffn_quantum_phases, L1_ffn_quantum_weights_real, L1_ffn_quantum_weights_imag, L1_ffn_W2, L1_ffn_b2):

    def _L0_attn_ref(x, w_qkv, w_out):
        import math
        import jax, jax.numpy as jnp
        import numpy as np
        EPS = 1e-06
        NEG = -1000000000.0

        def rms_norm(x):
            return x * jax.lax.rsqrt(jnp.mean(x * x, axis=-1, keepdims=True) + EPS)

        def apply_rope(x, cos, sin):
            d2 = x.shape[-1] // 2
            x1, x2 = (x[..., :d2], x[..., d2:])
            c = cos[None, None, :, :]
            s = sin[None, None, :, :]
            return jnp.concatenate([x1 * c - x2 * s, x2 * c + x1 * s], axis=-1)
        H, D, window_size = (16, 64, 32)
        B, T, C = x.shape
        xn = rms_norm(x)
        qkv = xn @ w_qkv.T
        q, k, v = jnp.split(qkv, 3, axis=-1)
        q = q.reshape(B, T, H, D).transpose(0, 2, 1, 3)
        k = k.reshape(B, T, H, D).transpose(0, 2, 1, 3)
        v = v.reshape(B, T, H, D).transpose(0, 2, 1, 3)
        inv_freq = 1.0 / 10000.0 ** (jnp.arange(0, D, 2, dtype=jnp.float32) / D)
        freqs = jnp.outer(jnp.arange(T, dtype=jnp.float32), inv_freq)
        cos, sin = (jnp.cos(freqs), jnp.sin(freqs))
        q = apply_rope(q, cos, sin)
        k = apply_rope(k, cos, sin)
        scale = 1.0 / math.sqrt(D)
        attn = jnp.einsum('bhqd,bhkd->bhqk', q, k) * scale
        q_pos = jnp.arange(T)[:, None]
        k_pos = jnp.arange(T)[None, :]
        mask = (q_pos >= k_pos) & (q_pos - k_pos <= window_size)
        attn = jnp.where(mask[None, None], attn, NEG)
        attn = jax.nn.softmax(attn.astype(jnp.float32), axis=-1).astype(q.dtype)
        out = jnp.einsum('bhqk,bhkd->bhqd', attn, v)
        out = out.transpose(0, 2, 1, 3).reshape(B, T, H * D)
        return out @ w_out.T

    def _L0_ffn_ref(x, centroids, ln_g, ln_b, w1, b1, w2, b2):
        import jax, jax.numpy as jnp
        import numpy as np
        LN_EPS = 1e-05

        def layer_norm(x, g, b):
            mu = jnp.mean(x, axis=-1, keepdims=True)
            var = jnp.var(x, axis=-1, keepdims=True)
            return (x - mu) / jnp.sqrt(var + LN_EPS) * g + b

        def balanced_assignment(scores):
            T, E = scores.shape
            C = T // E
            taken = jnp.zeros((T,), dtype=bool)
            parts = []
            for e in range(E):
                s = jnp.where(taken, -jnp.inf, scores[:, e])
                _, idx = jax.lax.top_k(s, C)
                parts.append(idx)
                taken = taken.at[idx].set(True)
            return jnp.concatenate(parts)
        D = x.shape[-1]
        feat = x.reshape(-1, D)
        T = feat.shape[0]
        E = centroids.shape[0]
        C = T // E
        norm = layer_norm(feat, ln_g, ln_b)
        scores = jax.lax.stop_gradient(norm @ centroids.T)
        sort_by_expert = balanced_assignment(scores)
        routed = feat[sort_by_expert].reshape(E, C, D)
        h = layer_norm(routed, ln_g, ln_b)
        h = jax.nn.gelu(jnp.einsum('ecd,edf->ecf', h, w1) + b1[:, None, :])
        h = jnp.einsum('ecf,efd->ecd', h, w2) + b2[:, None, :]
        out = routed + h
        inv = jnp.zeros((T,), dtype=jnp.int32).at[sort_by_expert].set(jnp.arange(T, dtype=jnp.int32))
        return out.reshape(T, D)[inv].reshape(x.shape)

    def _L1_attn_ref(x, Wqkv, bqkv, Wout, bout):
        import jax, jax.numpy as jnp
        import numpy as np
        BATCH, SEQ, DIM, NH = (4, 256, 128, 16)
        HD = DIM // NH

        def _rope_cos_sin(seq_len, head_dim, dtype=jnp.float32):
            inv_freq = 1.0 / 10000.0 ** (jnp.arange(0, head_dim, 2, dtype=dtype) / head_dim)
            t = jnp.arange(seq_len, dtype=dtype)
            freqs = jnp.outer(t, inv_freq)
            emb = jnp.concatenate([freqs, freqs], axis=-1)
            return (jnp.cos(emb), jnp.sin(emb))

        def _apply_rope(x, cos, sin):
            d2 = x.shape[-1] // 2
            x1, x2 = (x[..., :d2], x[..., d2:])
            c = cos[None, None, :, :d2]
            s = sin[None, None, :, :d2]
            return jnp.concatenate([x1 * c - x2 * s, x1 * s + x2 * c], axis=-1)
        b, s, dim = x.shape
        qkv = x @ Wqkv + bqkv
        qkv = qkv.reshape(b, s, 3, NH, HD).transpose(2, 0, 3, 1, 4)
        q, k, v = (qkv[0], qkv[1], qkv[2])
        cos, sin = _rope_cos_sin(s, HD, x.dtype)
        q = _apply_rope(q, cos, sin)
        k = _apply_rope(k, cos, sin)
        scale = HD ** (-0.5)
        scores = jnp.einsum('bhqd,bhkd->bhqk', q, k) * scale
        attn = jax.nn.softmax(scores, axis=-1)
        attn = jnp.nan_to_num(attn, nan=0.0)
        out = jnp.einsum('bhqk,bhkd->bhqd', attn, v)
        out = out.transpose(0, 2, 1, 3).reshape(b, s, dim)
        return out @ Wout + bout

    def _L1_ffn_ref(x, W1, b1, quantum_phases, quantum_weights_real, quantum_weights_imag, W2, b2):
        import jax, jax.numpy as jnp
        import numpy as np
        B, S, D_MODEL, D_FF = (4, 256, 128, 512)

        def _quantum_transform(hidden, theta, w_real, w_imag):
            imag = w_imag * jnp.sin(theta + hidden * 0.1)
            quantum_phase = jnp.cos(theta) * w_real + jnp.sin(theta) * w_imag
            return hidden + quantum_phase * imag * 0.1
        hidden = jnp.einsum('bsd,df->bsf', x, W1) + b1
        q = _quantum_transform(hidden, quantum_phases, quantum_weights_real, quantum_weights_imag)
        act = jax.nn.relu(q)
        return jnp.einsum('bsf,fd->bsd', act, W2) + b2
    x = L0_attn_x
    x = x + _layernorm(_L0_attn_ref(_layernorm(x, axis=-1), L0_attn_w_qkv, L0_attn_w_out), axis=-1)
    x = x + _layernorm(_L0_ffn_ref(_layernorm(x, axis=-1), L0_ffn_centroids, L0_ffn_ln_g, L0_ffn_ln_b, L0_ffn_w1, L0_ffn_b1, L0_ffn_w2, L0_ffn_b2), axis=-1)
    x = x + _layernorm(_L1_attn_ref(_layernorm(x, axis=-1), L1_attn_Wqkv, L1_attn_bqkv, L1_attn_Wout, L1_attn_bout), axis=-1)
    x = x + _layernorm(_L1_ffn_ref(_layernorm(x, axis=-1), L1_ffn_W1, L1_ffn_b1, L1_ffn_quantum_phases, L1_ffn_quantum_weights_real, L1_ffn_quantum_weights_imag, L1_ffn_W2, L1_ffn_b2), axis=-1)
    return x

_drawn_inputs = setup_inputs


def setup_inputs(seed=0):
    import zlib

    import numpy as np

    out = dict(_drawn_inputs(seed))
    spreads = {'L0_ffn_ln_g': (1.0, 0.59),
     'L0_ffn_ln_b': (0.0, 2.0),
     'L0_ffn_b1': (0.0, 0.731),
     'L0_ffn_b2': (0.0, 0.1),
     'L1_attn_bqkv': (0.0, 0.1),
     'L1_attn_bout': (0.0, 0.1),
     'L1_ffn_b1': (0.0, 0.331),
     'L1_ffn_b2': (0.0, 0.1)}
    factors = {'L1_ffn_quantum_phases': 28.806,
     'L1_ffn_quantum_weights_real': 60.708,
     'L1_ffn_quantum_weights_imag': 23.304}
    for name, (base, spread) in spreads.items():
        noise = np.random.default_rng([zlib.crc32(name.encode()), seed]).standard_normal(out[name].shape)
        drawn = base * np.exp(spread * noise) if base else spread * noise
        out[name] = jnp.asarray(drawn.astype(out[name].dtype))
    for name, factor in factors.items():
        out[name] = (out[name] * factor).astype(out[name].dtype)
    return out
```

```python
from contextlib import ExitStack

import numpy as np

import concourse.bass as bass
from concourse import mybir

F32 = mybir.dt.float32
F32R = mybir.dt.float32r
BF16 = mybir.dt.bfloat16
I32 = mybir.dt.int32
ALU = mybir.AluOpType
ACT = mybir.ActivationFunctionType
AX_X = mybir.AxisListType.X
MASKED = -1e30
L0_HEAD = 64
L0_WINDOW = 32
L0_BLOCK = 96
L1_HEADS = 16


def l0_attention(nc, x_in, w_l0, wo_l0, rope_l0, masks_q, masks_k, ident_in, x1):
    NB, T, C = x_in.shape
    NT = T // 128
    HD = 64
    PAIRS = wo_l0.shape[0] // 128
    HALF = 4 * 128
    WIN = 32
    QB = 96
    NJ = -(-T // QB)
    QP = NJ * QB
    KP = (NJ - 1) * QB + 128
    widths = [min(QB, T - QB * j) for j in range(NJ)]
    groups = [(0, 4), (4, NJ)]
    VH = w_l0.shape[1] // 5
    NV = NJ * (VH // HALF)

    x_v = x_in.rearrange("b (t p) c -> b p t c", p=128)

    with ExitStack() as ctx:
        def sb(name, shape, dt=F32):
            return ctx.enter_context(nc.sbuf_tensor("a_" + name, shape, dt))

        def ps(name, shape):
            return ctx.enter_context(nc.psum_tensor("a_" + name, shape, F32))

        def sem(name):
            return ctx.enter_context(nc.semaphore("a_" + name))

        w_sb = sb("w", [128, 5 * VH])
        wo_sb = sb("wo", [128, PAIRS, C])
        rope = sb("rope", [128, 4, T])
        mq = sb("mq", [QB, NJ * 128], BF16)
        mk = sb("mk", [128, T], BF16)
        ident = sb("ident", [128, 128])
        identb = sb("identb", [128, 128], BF16)
        ones = sb("ones", [128, HD])
        xpre = sb("xpre", [128, NT, C])
        xres = sb("xres", [128, NT, C])
        xn = sb("xn", [128, NT, C])
        xnT = sb("xnT", [128, KP])
        v_sb = sb("v", [128, NJ, VH])
        prod = [sb(f"prod{k}", [128, 4, T]) for k in range(2)]
        qT = [sb(f"qT{k}", [128, QP]) for k in range(2)]
        kT = [sb(f"kT{k}", [128, KP]) for k in range(2)]
        qR = [sb(f"qR{k}", [128, QP], F32R) for k in range(2)]
        kR = [sb(f"kR{k}", [128, KP], F32R) for k in range(2)]
        nmax = [sb(f"nmax{k}", [QB, 2, NJ], BF16) for k in range(2)]
        pT = [[sb(f"pT{k}{h}", [128, T]) for h in range(2)] for k in range(2)]
        rden = sb("rden", [128, T])
        oT = sb("oT", [128, PAIRS, T])
        yT = sb("yT", [128, T])
        ynorm = sb("ynorm", [128, NT, C])
        st1 = sb("st1", [128, NT, 6])
        mv1 = sb("mv1", [128, NT, 2])
        st2 = sb("st2", [128, NT, 6])
        mv2 = sb("mv2", [128, NT, 2])
        neg_half = sb("neg_half", [128, NT])
        ve = sb("ve", [128, NT])
        rstd = sb("rstd", [128, NT])
        ms = sb("ms", [128, NT])
        ms2 = sb("ms2", [128, NT])
        rr = sb("rr", [128, NT])
        comb = sb("comb", [128, NT])
        eps5 = sb("eps5", [128, NT])
        eps6 = sb("eps6", [128, NT])
        mark = sb("mark", [128, 1])
        ve2 = sb("ve2", [128, NT])
        rstd2 = sb("rstd2", [128, NT])

        proj = [ps(f"proj{k}", [128, HALF]) for k in range(2)]
        s_ps = [ps(f"s{k}", [128, HALF]) for k in range(2)]
        t_ps = [ps(f"t{k}", [128, HALF]) for k in range(2)]
        o_ps = ps("o", [128, HALF])
        d_ps = ps("d", [128, HALF])

        loaded = sem("loaded")
        const_set = sem("const_set")
        identb_ready = sem("identb_ready")
        xpre_in = sem("xpre_in")
        xres_in = sem("xres_in")
        stats1 = sem("stats1")
        pool_step = sem("pool_step")
        comb_ready = sem("comb_ready")
        xn_ready = sem("xn_ready")
        xn_transposed = sem("xn_transposed")
        xnT_ready = sem("xnT_ready")
        v_done = sem("v_done")
        v_evac = sem("v_evac")
        qk_done = sem("qk_done")
        rope_done = sem("rope_done")
        add_done = sem("add_done")
        round_done = sem("round_done")
        s_done = sem("s_done")
        max_done = sem("max_done")
        st_done = sem("st_done")
        exp_done = sem("exp_done")
        av_done = sem("av_done")
        rden_done = sem("rden_done")
        norm_done = sem("norm_done")
        y_done = sem("y_done")
        yT_ready = sem("yT_ready")
        y_back = sem("y_back")
        stats2 = sem("stats2")
        x_stat = sem("x_stat")
        y_stat = sem("y_stat")
        rstd2_ready = sem("rstd2_ready")
        ynorm_done = sem("ynorm_done")
        x1_ready = sem("x1_ready")
        NCONST = 10
        NLOADS = 6

        block = ctx.enter_context(nc.Block())

        @block.sync
        def _(sp):
            sp.dma_start(xpre[:], x_v[0]).then_inc(xpre_in, 16)
            sp.dma_start(ident[:], ident_in).then_inc(loaded, 16)
            sp.dma_start(w_sb[:], w_l0).then_inc(loaded, 16)
            sp.dma_start(rope[:], rope_l0).then_inc(loaded, 16)
            sp.dma_start(mq[:], masks_q).then_inc(loaded, 16)
            sp.dma_start(mk[:], masks_k).then_inc(loaded, 16)
            sp.dma_start(wo_sb[:], wo_l0.rearrange("(k p) c -> p k c", p=128)).then_inc(loaded, 16)

            def batch(i, last):
                if not last:
                    sp.wait_ge(xn_ready, i + 1)
                    sp.dma_start(xpre[:], x_v[i + 1]).then_inc(xpre_in, 16)
                sp.wait_ge(x1_ready, i + 1)
                sp.dma_start(xres[:], x_v[i]).then_inc(xres_in, 16)

            with sp.Fori(0, NB - 1) as i:
                batch(i, False)
            batch(NB - 1, True)

        @block.gpsimd
        def _(pool):
            nc.gpsimd.memset(neg_half[:], -0.5).then_inc(const_set, 1)
            nc.gpsimd.memset(eps5[:], 1e-5).then_inc(const_set, 1)
            nc.gpsimd.memset(eps6[:], 1e-6).then_inc(const_set, 1)
            nc.gpsimd.memset(ones[:], 1.0).then_inc(const_set, 1)
            nc.gpsimd.memset(xnT[:, 0:WIN], 0.0).then_inc(const_set, 1)
            nc.gpsimd.memset(xnT[:, WIN + T:KP], 0.0).then_inc(const_set, 1)
            for k in range(2):
                nc.gpsimd.memset(qT[k][:], 0.0).then_inc(const_set, 1)
                nc.gpsimd.memset(kT[k][:], 0.0).then_inc(const_set, 1)

            def pre_stats(i):
                n = 6 * i
                pool.wait_ge(stats1, i + 1)
                nc.gpsimd.tensor_tensor(ve[:], mv1[:, :, 1], eps5[:], ALU.add).then_inc(pool_step, 1)
                pool.wait_ge(pool_step, n + 1)
                nc.gpsimd.tensor_tensor(rstd[:], ve[:], neg_half[:], ALU.pow).then_inc(pool_step, 1)
                pool.wait_ge(pool_step, n + 2)
                nc.gpsimd.tensor_tensor(ms[:], rstd[:], rstd[:], ALU.mult).then_inc(pool_step, 1)
                pool.wait_ge(pool_step, n + 3)
                nc.gpsimd.tensor_tensor(ms2[:], ms[:], mv1[:, :, 1], ALU.mult).then_inc(pool_step, 1)
                pool.wait_ge(pool_step, n + 4)
                nc.gpsimd.tensor_tensor(ms[:], ms2[:], eps6[:], ALU.add).then_inc(pool_step, 1)
                pool.wait_ge(pool_step, n + 5)
                nc.gpsimd.tensor_tensor(rr[:], ms[:], neg_half[:], ALU.pow).then_inc(pool_step, 1)
                pool.wait_ge(pool_step, n + 6)
                nc.gpsimd.tensor_tensor(comb[:], rr[:], rstd[:], ALU.mult).then_inc(comb_ready, 1)

            pool.wait_ge(const_set, NCONST)
            pre_stats(0)

            def batch(i, last):
                for s in range(PAIRS):
                    b = s % 2
                    for side, dst in ((0, qT[b][:, 0:T]), (1, kT[b][:, WIN:WIN + T])):
                        pool.wait_ge(rope_done, 4 * PAIRS * i + 4 * s + 2 * side + 2)
                        if s >= 2 and side == 0:
                            pool.wait_ge(st_done, 2 * PAIRS * i + 2 * (s - 1))
                        nc.gpsimd.tensor_tensor(dst, prod[b][:, 2 * side, :], prod[b][:, 2 * side + 1, :],
                                                ALU.add).then_inc(add_done, 1)
                    if s == 6 and not last:
                        pre_stats(i + 1)
                pool.wait_ge(stats2, i + 1)
                nc.gpsimd.tensor_tensor(rstd2[:], ve2[:], neg_half[:], ALU.pow).then_inc(rstd2_ready, 1)

            with pool.Fori(0, NB - 1) as i:
                batch(i, False)
            batch(NB - 1, True)

        @block.scalar
        def _(act):
            act.wait_ge(const_set, NCONST)
            for k in range(2):
                nc.scalar.copy(qR[k][:], qT[k][:])
                nc.scalar.copy(kR[k][:], kT[k][:])
            act.wait_ge(loaded, 16 * NLOADS)
            nc.scalar.copy(identb[:], ident[:]).then_inc(identb_ready, 1)

            def pre(i):
                act.wait_ge(xn_transposed, i + 1)
                nc.scalar.copy(xnT[:, WIN:WIN + T], s_ps[0][:, 0:T]).then_inc(xnT_ready, 1)

            def v_copies(i):
                for n in range(NV):
                    j, half = divmod(n, VH // HALF)
                    act.wait_ge(v_done, NV * i + n + 1)
                    nc.scalar.copy(v_sb[:, j, half * HALF:(half + 1) * HALF], proj[n % 2][:]).then_inc(v_evac, 1)

            pre(0)
            v_copies(0)

            def batch(i, last):
                def rounds(s):
                    b = s % 2
                    if s >= 2:
                        act.wait_ge(s_done, 4 * PAIRS * i + 4 * (s - 1))
                    act.wait_ge(add_done, 2 * PAIRS * i + 2 * s + 1)
                    nc.scalar.copy(qR[b][:, 0:T], qT[b][:, 0:T]).then_inc(round_done, 1)
                    act.wait_ge(add_done, 2 * PAIRS * i + 2 * s + 2)
                    nc.scalar.copy(kR[b][:, WIN:WIN + T], kT[b][:, WIN:WIN + T]).then_inc(round_done, 1)

                def exps(s):
                    b = s % 2
                    for h in range(2):
                        if s >= 2 and h == 0:
                            act.wait_ge(av_done, PAIRS * i + s - 1)
                        act.wait_ge(st_done, 2 * PAIRS * i + 2 * s + h + 1)
                        nc.scalar.activation(pT[b][h][:], t_ps[h][:, 0:T], ACT.Exp).then_inc(exp_done, 1)

                for s in range(PAIRS + 1):
                    if s < PAIRS:
                        rounds(s)
                    if s == PAIRS and not last:
                        pre(i + 1)
                    if s >= 1:
                        exps(s - 1)
                if not last:
                    v_copies(i + 1)
                act.wait_ge(y_done, i + 1)
                nc.scalar.copy(yT[:], o_ps[:, 0:T]).then_inc(yT_ready, 1)

            with act.Fori(0, NB - 1) as i:
                batch(i, False)
            batch(NB - 1, True)

        @block.vector
        def _(dve):
            def pre(i):
                dve.wait_ge(xpre_in, 16 * (i + 1))
                for t in range(NT):
                    last = nc.vector.bn_stats(st1[:, t, :], xpre[:, t, :])
                last.then_inc(x_stat, 1)
                dve.wait_ge(x_stat, i + 1)
                nc.vector.memset(mark[:], 0.0)
                for t in range(NT):
                    last = nc.vector.bn_aggr(mv1[:, t, :], st1[:, t, :])
                last.then_inc(stats1, 1)
                dve.wait_ge(comb_ready, i + 1)
                for t in range(NT):
                    last = nc.vector.tensor_scalar(xn[:, t, :], xpre[:, t, :], mv1[:, t, 0:1], comb[:, t:t + 1],
                                                   ALU.subtract, ALU.mult)
                last.then_inc(xn_ready, 1)

            nc.vector.memset(mark[:], 0.0).then_inc(x1_ready, 1)
            pre(0)
            dve.wait_ge(loaded, 16 * NLOADS)

            def batch(i, last):
                def rotary(s):
                    b = s % 2
                    for c in range(4):
                        dve.wait_ge(qk_done, 4 * PAIRS * i + 4 * s + c + 1)
                        if s >= 2 and c % 2 == 0:
                            dve.wait_ge(add_done, 2 * PAIRS * i + 2 * (s - 2) + c // 2 + 1)
                        nc.vector.tensor_tensor(prod[b][:, c, :], proj[c % 2][:, 0:T], rope[:, c, :],
                                                ALU.mult).then_inc(rope_done, 1)

                def maxima(s):
                    b = s % 2
                    for h in range(2):
                        for g, (j0, j1) in enumerate(groups):
                            if s >= 2 and h == 0 and g == 0:
                                dve.wait_ge(st_done, 2 * PAIRS * i + 2 * (s - 1))
                            dve.wait_ge(s_done, 4 * PAIRS * i + 4 * s + 2 * h + g + 1)
                            scores = s_ps[g][0:QB, 0:(j1 - j0) * 128].rearrange("p (j k) -> p j k", k=128)
                            nc.vector.reduce_max(nmax[b][:, h, j0:j1], scores, AX_X,
                                                 negate=True).then_inc(max_done, 1)

                def normalise(s):
                    dve.wait_ge(av_done, PAIRS * i + s + 1)
                    nc.vector.reciprocal(rden[:], d_ps[:, 0:T]).then_inc(rden_done, 1)
                    dve.wait_ge(rden_done, PAIRS * i + s + 1)
                    nc.vector.tensor_tensor(oT[:, s, :], o_ps[:, 0:T], rden[:], ALU.mult).then_inc(norm_done, 1)

                for s in range(PAIRS + 2):
                    if s < PAIRS:
                        rotary(s)
                        maxima(s)
                    if s >= 2:
                        normalise(s - 2)
                    if s == 6 and not last:
                        dve.wait_ge(xn_transposed, i + 1)
                        pre(i + 1)
                dve.wait_ge(y_back, i + 1)
                for t in range(NT):
                    last_i = nc.vector.bn_stats(st2[:, t, :], d_ps[:, t * 128:(t + 1) * 128])
                last_i.then_inc(y_stat, 1)
                dve.wait_ge(y_stat, i + 1)
                nc.vector.memset(mark[:], 0.0)
                for t in range(NT):
                    last_i = nc.vector.bn_aggr(mv2[:, t, :], st2[:, t, :])
                last_i.then_inc(ynorm_done, 1)
                dve.wait_ge(ynorm_done, 3 * i + 1)
                nc.vector.tensor_scalar(ve2[:], mv2[:, :, 1], 1e-5, None, ALU.add).then_inc(stats2, 1)
                dve.wait_ge(rstd2_ready, i + 1)
                for t in range(NT):
                    last_i = nc.vector.tensor_scalar(ynorm[:, t, :], d_ps[:, t * 128:(t + 1) * 128], mv2[:, t, 0:1],
                                                     rstd2[:, t:t + 1], ALU.subtract, ALU.mult)
                last_i.then_inc(ynorm_done, 2)
                dve.wait_ge(ynorm_done, 3 * i + 3)
                dve.wait_ge(xres_in, 16 * (i + 1))
                nc.vector.tensor_tensor(x1[:, bass.ds(NT * i, NT), :], ynorm[:], xres[:], ALU.add).then_inc(x1_ready, 1)

            with dve.Fori(0, NB - 1) as i:
                batch(i, False)
            batch(NB - 1, True)

        @block.tensor
        def _(pe):
            def transposes(i):
                pe.wait_ge(xn_ready, i + 1)
                for t in range(NT):
                    last = nc.tensor.transpose(s_ps[0][:, t * 128:(t + 1) * 128], xn[:, t, :], ident[:])
                last.then_inc(xn_transposed, 1)

            def values(i, first):
                pe.wait_ge(xnT_ready, i + 1)
                for n in range(NV):
                    j, half = divmod(n, VH // HALF)
                    if n >= 2:
                        pe.wait_ge(v_evac, NV * i + n - 1)
                    elif not first:
                        pe.wait_ge(rope_done, 4 * PAIRS * i - 1 + n)
                    nc.tensor.matmul(proj[n % 2][:], xnT[:, QB * j:QB * j + 128],
                                     w_sb[:, 4 * VH + half * HALF:4 * VH + (half + 1) * HALF],
                                     start=True, stop=True).then_inc(v_done, 1)

            pe.wait_ge(loaded, 16 * NLOADS)
            pe.wait_ge(const_set, NCONST)
            transposes(0)
            values(0, True)
            pe.wait_ge(identb_ready, 1)

            def batch(i, last):
                def project(s):
                    for c in range(4):
                        if 4 * s + c < 2:
                            pe.wait_ge(v_evac, NV * i + NV - 1 + c)
                        else:
                            pe.wait_ge(rope_done, 4 * PAIRS * i + 4 * s + c - 1)
                        nc.tensor.matmul(proj[c % 2][:, 0:T], w_sb[:, c * VH + s * 128:c * VH + (s + 1) * 128],
                                         xnT[:, WIN:WIN + T], start=True, stop=True).then_inc(qk_done, 1)

                def max_scores(s):
                    b = s % 2
                    pe.wait_ge(round_done, 2 * PAIRS * i + 2 * s + 2)
                    for h in range(2):
                        rows = slice(HD * h, HD * h + HD)
                        for g, (j0, j1) in enumerate(groups):
                            use = 4 * s + 2 * h + g
                            if use >= 2:
                                pe.wait_ge(max_done, 4 * PAIRS * i + use - 1)
                            nc.tensor.matmul(s_ps[g][0:QB, 0:(j1 - j0) * 128], identb[0:QB, 0:QB],
                                             mq[:, j0 * 128:j1 * 128], start=True, stop=False)
                            for j in range(j0, j1):
                                last_i = nc.tensor.matmul(s_ps[g][0:QB, (j - j0) * 128:(j - j0 + 1) * 128],
                                                          qR[b][rows, QB * j:QB * (j + 1)],
                                                          kR[b][rows, QB * j:QB * j + 128],
                                                          start=False, stop=j == j1 - 1)
                            last_i.then_inc(s_done, 1)

                def shifted_scores(s):
                    b = s % 2
                    for h in range(2):
                        rows = slice(HD * h, HD * h + HD)
                        pe.wait_ge(max_done, 4 * PAIRS * i + 4 * s + 2 * h + 2)
                        if s >= 1:
                            pe.wait_ge(exp_done, 2 * PAIRS * i + 2 * (s - 1) + h + 1)
                        nc.tensor.matmul(t_ps[h][:, 0:T], identb[:], mk[:], start=True, stop=False)
                        for j in range(NJ):
                            cols = slice(QB * j, QB * j + widths[j])
                            nc.tensor.matmul(t_ps[h][:, cols], kT[b][rows, QB * j:QB * j + 128], qT[b][rows, cols],
                                             start=False, stop=False)
                        for j in range(NJ):
                            cols = slice(QB * j, QB * j + widths[j])
                            last_i = nc.tensor.matmul(t_ps[h][:, cols],
                                                      nmax[b][:, h, j:j + 1].to_broadcast([QB, 128]),
                                                      identb[0:QB, 0:widths[j]], start=False, stop=j == NJ - 1)
                        last_i.then_inc(st_done, 1)

                def weighted_values(s):
                    b = s % 2
                    pe.wait_ge(exp_done, 2 * PAIRS * i + 2 * s + 2)
                    if s >= 1:
                        pe.wait_ge(norm_done, PAIRS * i + s)
                    else:
                        pe.wait_ge(x1_ready, i + 1)
                    for j in range(NJ):
                        cols = slice(QB * j, QB * j + widths[j])
                        for h in range(2):
                            col = (2 * s + h) * HD
                            nc.tensor.matmul(o_ps[HD * h:HD * h + HD, cols], v_sb[:, j, col:col + HD],
                                             pT[b][h][:, cols], start=True, stop=True)
                    for h in range(2):
                        last_i = nc.tensor.matmul(d_ps[HD * h:HD * h + HD, 0:T], ones[:], pT[b][h][:],
                                                  start=True, stop=True)
                    last_i.then_inc(av_done, 1)

                for s in range(PAIRS + 2):
                    if s < PAIRS:
                        project(s)
                    if s == PAIRS and not last:
                        pe.wait_ge(max_done, 4 * PAIRS * (i + 1))
                        transposes(i + 1)
                    if 1 <= s <= PAIRS:
                        shifted_scores(s - 1)
                    if s < PAIRS:
                        max_scores(s)
                    if s >= 2:
                        weighted_values(s - 2)
                if not last:
                    values(i + 1, False)
                pe.wait_ge(norm_done, PAIRS * (i + 1))
                for s in range(PAIRS):
                    last_i = nc.tensor.matmul(o_ps[:, 0:T], wo_sb[:, s, :], oT[:, s, :],
                                              start=s == 0, stop=s == PAIRS - 1)
                last_i.then_inc(y_done, 1)
                pe.wait_ge(yT_ready, i + 1)
                for t in range(NT):
                    last_i = nc.tensor.transpose(d_ps[:, t * 128:(t + 1) * 128], yT[:, t * 128:(t + 1) * 128], ident[:])
                last_i.then_inc(y_back, 1)

            with pe.Fori(0, NB - 1) as i:
                batch(i, False)
            batch(NB - 1, True)


def routing(nc, x1, pos, mean, rstd, cent_t, ln_g, ln_b, ident_in, ones_in, before_in, sorted_x):
    _, TILES, C = x1.shape
    E = cent_t.shape[1]
    CAP = TILES * 128 // E
    G4 = 4
    DIGITS = 8
    TIES = 3

    with ExitStack() as ctx:
        def sb(name, shape, dt=F32):
            return ctx.enter_context(nc.sbuf_tensor("b_" + name, shape, dt))

        def ps(name, shape):
            return ctx.enter_context(nc.psum_tensor("b_" + name, shape, F32))

        def sem(name):
            return ctx.enter_context(nc.semaphore("b_" + name))

        cent = sb("cent", [128, E])
        gamma = sb("gamma", [128, 1])
        beta = sb("beta", [128, 1])
        ident = sb("ident", [128, 128])
        ones = sb("ones", [128, 128], BF16)
        before = sb("before", [128, 128], BF16)
        st = sb("st", [128, TILES, 6])
        msum = sb("msum", [128, TILES])
        mdif = sb("mdif", [128, TILES])
        mdd = sb("mdd", [128, TILES])
        m2 = sb("m2", [128, TILES])
        var = sb("var", [128, TILES])
        neg_half = sb("neg_half", [128, TILES])
        eps = sb("eps", [128, TILES])
        ve = sb("ve", [128, TILES])
        r2 = sb("r2", [128, TILES])
        rv = sb("rv", [128, TILES])
        comb = sb("comb", [128, TILES])
        zz = [sb(f"zz{k}", [128, G4, C]) for k in range(2)]
        nT = [sb(f"nT{k}", [128, G4 * 128]) for k in range(2)]
        score = sb("score", [128, E, TILES])
        sign = sb("sign", [128, E, TILES], I32)
        key = sb("key", [128, E, TILES], I32)
        half_i = sb("half_i", [128, E, TILES], I32)
        half_j = sb("half_j", [128, E, TILES], I32)
        hi1 = sb("hi1", [128, E, TILES])
        lo1 = sb("lo1", [128, E, TILES])
        free = sb("free", [128, TILES])
        place = sb("place", [128, TILES])
        a1 = sb("a1", [128, TILES])
        b1 = sb("b1", [128, TILES])
        eq = sb("eq", [128, TILES])
        above = sb("above", [128, TILES])
        above2 = sb("above2", [128, TILES])
        tied = sb("tied", [128, TILES], BF16)
        taken = sb("taken", [128, TILES], BF16)
        run = sb("run", [128, TILES])
        rank = sb("rank", [128, TILES])
        junk = sb("junk", [128, TIES, TILES])
        junk3 = sb("junk3", [128, TIES])
        steps = sb("steps", [128, DIGITS, TIES])
        first = sb("first", [128, TIES])
        base = sb("base", [128, 1])
        thr = [sb(f"thr{k}", [128, 1]) for k in range(2)]
        tries = sb("tries", [128, TIES])
        tries_base = sb("tries_base", [128, TIES])
        count = sb("count", [128, TIES], BF16)
        digit = sb("digit", [128, 1])
        need = [sb(f"need{k}", [128, 1]) for k in range(3)]
        one_col = sb("one_col", [128, TILES])

        tp = [ps(f"tp{k}", [128, 512]) for k in range(2)]
        sp_ps = [ps(f"sp{k}", [128, 512]) for k in range(2)]
        tot = ps("tot", [128, 512])
        pre_ps = ps("pre", [128, 512])
        all_ps = ps("all", [128, 512])

        loaded = sem("loaded")
        stats = sem("stats")
        pool_step = sem("pool_step")
        comb_ready = sem("comb_ready")
        zz_ready = sem("zz_ready")
        zz_turned = sem("zz_turned")
        nT_ready = sem("nT_ready")
        sc_done = sem("sc_done")
        sc_kept = sem("sc_kept")
        chain = sem("chain")
        setup_done = sem("setup_done")
        cnt_ready = sem("cnt_ready")
        tot_ready = sem("tot_ready")
        tied_ready = sem("tied_ready")
        rank_ready = sem("rank_ready")
        pos_ready = sem("pos_ready")
        scattered = sem("scattered")
        NLOADS = 6

        CNT = 2 * DIGITS + 2

        block = ctx.enter_context(nc.Block())

        @block.sync
        def _(sp):
            sp.dma_start(cent[:], cent_t).then_inc(loaded, 16)
            sp.dma_start(gamma[:], ln_g).then_inc(loaded, 16)
            sp.dma_start(beta[:], ln_b).then_inc(loaded, 16)
            sp.dma_start(ident[:], ident_in).then_inc(loaded, 16)
            sp.dma_start(ones[:], ones_in).then_inc(loaded, 16)
            sp.dma_start(before[:], before_in).then_inc(loaded, 16)

        @block.gpsimd
        def _(pool):
            nc.gpsimd.memset(neg_half[:], -0.5).then_inc(pool_step, 1)
            nc.gpsimd.memset(eps[:], 1e-5).then_inc(pool_step, 1)
            pool.wait_ge(pool_step, 2)
            pool.wait_ge(stats, 1)
            nc.gpsimd.tensor_tensor(ve[:], var[:], eps[:], ALU.add).then_inc(pool_step, 1)
            pool.wait_ge(pool_step, 3)
            nc.gpsimd.tensor_tensor(rstd[:], ve[:], neg_half[:], ALU.pow).then_inc(pool_step, 1)
            pool.wait_ge(pool_step, 4)
            nc.gpsimd.tensor_tensor(rv[:], rstd[:], rstd[:], ALU.mult).then_inc(pool_step, 1)
            pool.wait_ge(pool_step, 5)
            nc.gpsimd.tensor_tensor(r2[:], rv[:], var[:], ALU.mult).then_inc(pool_step, 1)
            pool.wait_ge(pool_step, 6)
            nc.gpsimd.tensor_tensor(rv[:], r2[:], eps[:], ALU.add).then_inc(pool_step, 1)
            pool.wait_ge(pool_step, 7)
            nc.gpsimd.tensor_tensor(r2[:], rv[:], neg_half[:], ALU.pow).then_inc(pool_step, 1)
            pool.wait_ge(pool_step, 8)
            nc.gpsimd.tensor_tensor(comb[:], r2[:], rstd[:], ALU.mult).then_inc(comb_ready, 1)

            pool.wait_ge(pos_ready, 1)
            for t in range(TILES):
                pool.indirect_dma_start(out=sorted_x, out_offset=bass.IndirectOffsetOnAxis(ap=pos[:, t:t + 1], axis=0),
                                        in_=x1[:, t, :], in_offset=None).then_inc(scattered, 16)
            pool.wait_ge(scattered, 16 * TILES)

        @block.scalar
        def _(act):
            act.wait_ge(loaded, 16 * NLOADS)
            with act.Fori(0, TILES // G4 // 2) as i:
                for k in range(2):
                    act.wait_ge(zz_turned, 2 * i + k + 1)
                    nc.scalar.activation(nT[k][:], tp[k][:], ACT.Identity, bias=beta[:], scale=gamma[:]).then_inc(nT_ready, 1)

        @block.tensor
        def _(pe):
            pe.wait_ge(loaded, 16 * NLOADS)
            with pe.Fori(0, TILES // G4 // 2) as i:
                for k in range(2):
                    pe.wait_ge(zz_ready, 2 * i + k + 1)
                    for t in range(G4):
                        last = nc.tensor.transpose(tp[k][:, t * 128:(t + 1) * 128], zz[k][:, t, :], ident[:])
                    last.then_inc(zz_turned, 1)
                for k in range(2):
                    pe.wait_ge(nT_ready, 2 * i + k + 1)
                    pe.wait_ge(sc_kept, 2 * i + k + 1)
                    for t in range(G4):
                        last = nc.tensor.matmul(sp_ps[k][:, t * E:(t + 1) * E], nT[k][:, t * 128:(t + 1) * 128], cent[:],
                                                start=True, stop=True)
                    last.then_inc(sc_done, 1)

            def ranks(flags, n):
                pe.wait_ge(tied_ready, n)
                nc.tensor.matmul(pre_ps[:, 0:TILES], before[:], flags[:], start=True, stop=True)
                nc.tensor.matmul(all_ps[:, 0:TILES], ones[:], flags[:], start=True, stop=True).then_inc(rank_ready, 1)

            with pe.Fori(0, E - 1) as e:
                for n in range(CNT):
                    pe.wait_ge(cnt_ready, CNT * e + n + 1)
                    nc.tensor.matmul(tot[:, 0:TIES], ones[:], count[:], start=True, stop=True).then_inc(tot_ready, 1)
                ranks(tied, 2 * e + 1)
                ranks(taken, 2 * e + 2)
            ranks(taken, 2 * (E - 1) + 1)

        @block.vector
        def _(dve):
            with dve.Fori(0, TILES // G4) as i:
                for u in range(G4):
                    nc.vector.bn_stats(st[:, i * G4 + u, :], x1[:, i * G4 + u, :])
            chained = [0]

            def link(ins):
                chained[0] += 1
                ins.then_inc(chain, 1)
                dve.wait_ge(chain, chained[0])

            link(nc.vector.memset(base[:], 0.0))
            nc.vector.tensor_tensor(msum[:], st[:, :, 1], st[:, :, 4], ALU.add)
            nc.vector.tensor_tensor(mdif[:], st[:, :, 1], st[:, :, 4], ALU.subtract)
            link(nc.vector.tensor_tensor(m2[:], st[:, :, 2], st[:, :, 5], ALU.add))
            nc.vector.tensor_scalar(mean[:], msum[:], 0.5, None, ALU.mult)
            link(nc.vector.scalar_tensor_tensor(mdd[:], mdif[:], 0.25, mdif[:], ALU.mult, ALU.mult))
            nc.vector.scalar_tensor_tensor(var[:], m2[:], 1.0 / C, mdd[:], ALU.mult, ALU.add).then_inc(stats, 1)

            nc.vector.memset(free[:], 1.0)
            nc.vector.memset(place[:], 0.0)
            nc.vector.memset(one_col[:], 1.0)
            nc.vector.memset(need[0][:], float(CAP))
            nc.vector.memset(count[:], 0.0)
            for d in range(DIGITS):
                for k in range(TIES):
                    nc.vector.memset(steps[:, d, k:k + 1], float((k + 1) * 4 ** d))
            for k in range(TIES):
                nc.vector.memset(first[:, k:k + 1], float((k + 1) * 4 ** (DIGITS - 1) + 1))
            nc.vector.memset(junk3[:], 0.0).then_inc(sc_kept, 2)

            dve.wait_ge(comb_ready, 1)
            with dve.Fori(0, TILES // G4 // 2) as i:
                for k in range(2):
                    for u in range(G4):
                        t = (2 * i + k) * G4 + u
                        last = nc.vector.tensor_scalar(zz[k][:, u, :], x1[:, t, :], mean[:, bass.ds(t, 1)],
                                                       comb[:, bass.ds(t, 1)], ALU.subtract, ALU.mult)
                    last.then_inc(zz_ready, 1)
                for k in range(2):
                    dve.wait_ge(sc_done, 2 * i + k + 1)
                    nc.vector.tensor_copy(score[:, :, bass.ds((2 * i + k) * G4, G4)],
                                          sp_ps[k][:, 0:G4 * E].rearrange("p (t e) -> p e t", e=E)).then_inc(sc_kept, 1)
            dve.wait_ge(sc_kept, TILES // G4 + 2)
            bits = score[:].bitcast(I32)
            link(nc.vector.tensor_scalar(sign[:], bits, 31, -2 ** 31, ALU.arith_shift_right, ALU.bitwise_or))
            link(nc.vector.tensor_tensor(key[:], bits, sign[:], ALU.bitwise_xor))
            nc.vector.tensor_scalar(half_i[:], key[:], 16, 0xffff, ALU.arith_shift_right, ALU.bitwise_and)
            link(nc.vector.tensor_scalar(half_j[:], key[:], 0xffff, None, ALU.bitwise_and))
            nc.vector.tensor_scalar(hi1[:], half_i[:], 1.0, None, ALU.add)
            link(nc.vector.tensor_scalar(lo1[:], half_j[:], 1.0, None, ALU.add))
            done = chained[0]

            def expert(e, last):
                step = [0]

                def link(ins):
                    step[0] += 1
                    ins.then_inc(chain, 1)
                    dve.wait_ge(chain, PER * e + done + step[0])

                totals = [0]

                def total(ins):
                    totals[0] += 1
                    ins.then_inc(cnt_ready, 1)
                    return lambda: dve.wait_ge(tot_ready, CNT * e + totals[0])

                def search(values, needed, thr):
                    nc.vector.memset(thr[:], 1.0)
                    link(nc.vector.tensor_copy(tries[:], first[:]))
                    for d in reversed(range(DIGITS)):
                        for k in range(TIES):
                            ins = nc.vector.tensor_scalar(junk[:, k, :], values, tries[:, k:k + 1], None, ALU.is_ge,
                                                          ALU.add, accum_out=count[:, k:k + 1])
                        wait_total = total(ins)
                        if d:
                            nc.vector.tensor_scalar(tries_base[:], steps[:, d - 1, :], thr[:], None, ALU.add)
                        wait_total()
                        link(nc.vector.tensor_scalar(junk3[:], tot[:, 0:TIES], needed[:], None, ALU.is_ge,
                                                     ALU.add, accum_out=digit[:]))
                        if d:
                            nc.vector.scalar_tensor_tensor(tries[:], digit[:].to_broadcast([128, TIES]), float(4 ** d),
                                                           tries_base[:], ALU.mult, ALU.add)
                        link(nc.vector.scalar_tensor_tensor(thr[:], digit[:], float(4 ** d), thr[:], ALU.mult, ALU.add))

                def ranked(flags_done, n):
                    flags_done.then_inc(tied_ready, 1)
                    dve.wait_ge(rank_ready, n)
                    link(nc.vector.tensor_tensor_scan(run[:], one_col[:], all_ps[:, 0:TILES], 0.0, ALU.mult, ALU.add))
                    link(nc.vector.tensor_tensor(run[:], run[:], all_ps[:, 0:TILES], ALU.subtract))
                    link(nc.vector.tensor_tensor(rank[:], run[:], pre_ps[:, 0:TILES], ALU.add))

                if last:
                    ins = nc.vector.tensor_copy(taken[:], free[:])
                    ranked(ins, 2 * e + 1)
                else:
                    link(nc.vector.tensor_tensor(a1[:], hi1[:, e, :], free[:], ALU.mult))
                    search(a1[:], need[0], thr[0])
                    total(nc.vector.tensor_scalar(above[:], a1[:], thr[0][:], None, ALU.is_gt, ALU.add,
                                                  accum_out=count[:, 0:1]))()
                    nc.vector.tensor_scalar(eq[:], a1[:], thr[0][:], None, ALU.is_equal)
                    link(nc.vector.tensor_tensor(need[1][:], need[0][:], tot[:, 0:1], ALU.subtract))
                    link(nc.vector.tensor_tensor(b1[:], eq[:], lo1[:, e, :], ALU.mult))
                    search(b1[:], need[1], thr[1])
                    total(nc.vector.tensor_scalar(above2[:], b1[:], thr[1][:], None, ALU.is_gt, ALU.add,
                                                  accum_out=count[:, 0:1]))()
                    nc.vector.tensor_tensor(need[2][:], need[1][:], tot[:, 0:1], ALU.subtract)
                    ins = nc.vector.tensor_scalar(tied[:], b1[:], thr[1][:], None, ALU.is_equal)
                    ranked(ins, 2 * e + 1)
                    link(nc.vector.scalar_tensor_tensor(eq[:], rank[:], need[2][:], tied[:], ALU.is_lt, ALU.mult))
                    link(nc.vector.tensor_tensor(above[:], above[:], above2[:], ALU.add))
                    link(nc.vector.tensor_tensor(eq[:], eq[:], above[:], ALU.add))
                    ins = nc.vector.tensor_copy(taken[:], eq[:])
                    ranked(ins, 2 * e + 2)
                link(nc.vector.scalar_tensor_tensor(run[:], rank[:], base[:], taken[:], ALU.add, ALU.mult))
                nc.vector.tensor_tensor(place[:], place[:], run[:], ALU.add)
                nc.vector.tensor_tensor(free[:], free[:], taken[:], ALU.subtract)
                link(nc.vector.tensor_scalar(base[:], base[:], float(CAP), None, ALU.add))
                assert last or (step[0] == PER and totals[0] == CNT)

            PER = 4 * DIGITS + 16
            with dve.Fori(0, E - 1) as e:
                expert(e, False)
            expert(E - 1, True)
            nc.vector.tensor_copy(pos[:], place[:]).then_inc(pos_ready, 1)


def expert_ffn(nc, sorted_x, w1_d, b1_d, w2_d, b2_d, ln_g, ln_b, ident_in, sorted_out):
    N, C = sorted_x.shape
    E, _, F = w1_d.shape
    CH = 512
    NT = CH // 128
    NF = F // 128
    U = 4
    TURNS = N // CH // U
    assert N // E == 2 * CH
    x_v = sorted_x.rearrange("(n p t) c -> n p t c", p=128, t=NT)
    o_v = sorted_out.rearrange("(n p t) c -> n p t c", p=128, t=NT)

    with ExitStack() as ctx:
        def sb(name, shape, dt=F32):
            return ctx.enter_context(nc.sbuf_tensor("c_" + name + "_", shape, dt))

        def ps(name, shape):
            return ctx.enter_context(nc.psum_tensor("c_" + name + "_", shape, F32))

        def sem(name):
            return ctx.enter_context(nc.semaphore("c_" + name))

        gamma = sb("gamma", [128, 1])
        beta = sb("beta", [128, 1])
        ident = sb("ident", [128, 128])
        w1 = [sb(f"w1_{k}", [128, F]) for k in range(2)]
        w2 = [sb(f"w2_{k}", [128, NF, C]) for k in range(2)]
        b1 = [sb(f"b1_{k}", [128, NF]) for k in range(2)]
        b2 = [sb(f"b2_{k}", [128, 1]) for k in range(2)]
        xs = [sb(f"xs_{k}", [128, NT, C]) for k in range(U)]
        mv = [sb(f"mv_{k}", [128, NT, 2]) for k in range(U)]
        st = [sb(f"st_{k}", [128, NT, 6]) for k in range(2)]
        rstd = [sb(f"rstd_{k}", [128, NT]) for k in range(U)]
        comb = [sb(f"comb_{k}", [128, NT]) for k in range(U)]
        ve = sb("ve", [128, NT])
        va = sb("va", [128, NT])
        vb = sb("vb", [128, NT])
        neg_half = sb("neg_half", [128, NT])
        eps = sb("eps", [128, NT])
        zz = [sb(f"zz_{k}", [128, NT, C]) for k in range(2)]
        z = [sb(f"z_{k}", [128, NT, C]) for k in range(2)]
        hT = [sb(f"hT_{k}", [128, CH]) for k in range(2)]
        gT = sb("gT", [128, NF, CH])
        yT = sb("yT", [128, CH])
        res = sb("res", [128, NT, C])
        resn = sb("resn", [128, NT, C])
        st2 = sb("st2", [128, NT, 6])
        mv2 = sb("mv2", [128, NT, 2])
        ve2 = sb("ve2", [128, NT])
        rstd2 = sb("rstd2", [128, NT])
        mark = sb("mark", [128, 1])

        in_ps = [ps(f"in_{k}", [128, CH]) for k in range(2)]
        h_ps = [ps(f"h_{k}", [128, CH]) for k in range(2)]
        y_ps = [ps(f"y_{k}", [128, CH]) for k in range(2)]
        back_ps = [ps(f"back_{k}", [128, CH]) for k in range(2)]

        loaded = sem("loaded")
        w_in = [sem(f"w_in{k}") for k in range(2)]
        xs_in = [sem(f"xs_in{k}") for k in range(U)]
        const_set = sem("const_set")
        stat_step = sem("stat_step")
        stats = sem("stats")
        pool_step = sem("pool_step")
        comb_ready = sem("comb_ready")
        zz_ready = sem("zz_ready")
        turned = sem("turned")
        hT_ready = sem("hT_ready")
        h_done = sem("h_done")
        gelu_done = sem("gelu_done")
        y_done = sem("y_done")
        yT_ready = sem("yT_ready")
        back_done = sem("back_done")
        post_step = sem("post_step")
        var2_ready = sem("var2_ready")
        rstd2_ready = sem("rstd2_ready")
        x2_ready = sem("x2_ready")
        stored = sem("stored")

        block = ctx.enter_context(nc.Block())

        @block.sync
        def _(sp):
            def weights(e, k):
                sp.dma_start(w1[k][:], w1_d[e]).then_inc(w_in[k], 16)
                sp.dma_start(w2[k][:], w2_d[e].rearrange("(f p) c -> p f c", p=128)).then_inc(w_in[k], 16)
                sp.dma_start(b1[k][:], b1_d[e]).then_inc(w_in[k], 16)
                sp.dma_start(b2[k][:], b2_d[e]).then_inc(w_in[k], 16)

            sp.dma_start(xs[0][:], x_v[0]).then_inc(xs_in[0], 16)
            sp.dma_start(xs[1][:], x_v[1]).then_inc(xs_in[1], 16)
            sp.dma_start(gamma[:], ln_g).then_inc(loaded, 16)
            sp.dma_start(beta[:], ln_b).then_inc(loaded, 16)
            sp.dma_start(ident[:], ident_in).then_inc(loaded, 16)
            weights(0, 0)
            for u in range(2, U):
                sp.dma_start(xs[u][:], x_v[u]).then_inc(xs_in[u], 16)
            weights(1, 1)

            def turn(i, last):
                for u in range(U):
                    c = U * i + u
                    sp.wait_ge(x2_ready, c + 1)
                    sp.dma_start(o_v[c], xs[u][:]).then_inc(stored, 16)
                    if not last:
                        sp.wait_ge(stored, 16 * (c + 1))
                        sp.dma_start(xs[u][:], x_v[c + U]).then_inc(xs_in[u], 16)
                        if u % 2:
                            sp.wait_ge(yT_ready, c + 1)
                            weights(2 * (i + 1) + u // 2, u // 2)

            with sp.Fori(0, TURNS - 1) as i:
                turn(i, False)
            turn(TURNS - 1, True)
            sp.wait_ge(stored, 16 * U * TURNS)

        @block.gpsimd
        def _(pool):
            nc.gpsimd.memset(neg_half[:], -0.5).then_inc(const_set, 1)
            nc.gpsimd.memset(eps[:], 1e-5).then_inc(const_set, 1)
            pool.wait_ge(const_set, 2)

            def factors(c, k):
                def link(ins, n):
                    ins.then_inc(pool_step, 1)
                    pool.wait_ge(pool_step, 6 * c + n)
                pool.wait_ge(stats, c + 1)
                link(nc.gpsimd.tensor_tensor(ve[:], mv[k][:, :, 1], eps[:], ALU.add), 1)
                link(nc.gpsimd.tensor_tensor(rstd[k][:], ve[:], neg_half[:], ALU.pow), 2)
                link(nc.gpsimd.tensor_tensor(va[:], rstd[k][:], rstd[k][:], ALU.mult), 3)
                link(nc.gpsimd.tensor_tensor(vb[:], va[:], mv[k][:, :, 1], ALU.mult), 4)
                link(nc.gpsimd.tensor_tensor(va[:], vb[:], eps[:], ALU.add), 5)
                link(nc.gpsimd.tensor_tensor(vb[:], va[:], neg_half[:], ALU.pow), 6)
                nc.gpsimd.tensor_tensor(comb[k][:], vb[:], rstd[k][:], ALU.mult).then_inc(comb_ready, 1)

            factors(0, 0)
            factors(1, 1)

            def turn(i, last):
                for u in range(U):
                    c = U * i + u
                    if not (last and u >= U - 2):
                        factors(c + 2, (u + 2) % U)
                    pool.wait_ge(var2_ready, c + 1)
                    nc.gpsimd.tensor_tensor(rstd2[:], ve2[:], neg_half[:], ALU.pow).then_inc(rstd2_ready, 1)

            with pool.Fori(0, TURNS - 1) as i:
                turn(i, False)
            turn(TURNS - 1, True)

        @block.scalar
        def _(act):
            def turn_in(c, k):
                act.wait_ge(turned, c + 1)
                nc.scalar.activation(hT[k % 2][:], in_ps[k % 2][:], ACT.Identity, bias=beta[:],
                                     scale=gamma[:]).then_inc(hT_ready, 1)

            act.wait_ge(loaded, 16 * 3)
            turn_in(0, 0)

            def turn(i, last):
                for u in range(U):
                    c = U * i + u
                    w = u // 2
                    if u % 2 == 0:
                        act.wait_ge(w_in[w], 64 * (i + 1))
                    for f in range(NF):
                        act.wait_ge(h_done, NF * c + f + 1)
                        nc.scalar.activation(gT[:, f, :], h_ps[f % 2][:], ACT.Gelu_apprx_tanh,
                                             bias=b1[w][:, f:f + 1]).then_inc(gelu_done, 1)
                    if not (last and u == U - 1):
                        turn_in(c + 1, u + 1)
                    act.wait_ge(y_done, c + 1)
                    nc.scalar.activation(yT[:], y_ps[u % 2][:], ACT.Identity, bias=b2[w][:]).then_inc(yT_ready, 1)

            with act.Fori(0, TURNS - 1) as i:
                turn(i, False)
            turn(TURNS - 1, True)

        @block.vector
        def _(dve):
            def statistics(c, i, k):
                dve.wait_ge(xs_in[k], 16 * (i + 1))
                for t in range(NT):
                    last = nc.vector.bn_stats(st[k % 2][:, t, :], xs[k][:, t, :])
                last.then_inc(stat_step, 1)
                dve.wait_ge(stat_step, c + 1)
                nc.vector.memset(mark[:], 0.0)
                for t in range(NT):
                    last = nc.vector.bn_aggr(mv[k][:, t, :], st[k % 2][:, t, :])
                last.then_inc(stats, 1)

            def normalised(c, k):
                dve.wait_ge(comb_ready, c + 1)
                for t in range(NT):
                    last = nc.vector.tensor_scalar(zz[k % 2][:, t, :], xs[k][:, t, :], mv[k][:, t, 0:1],
                                                   comb[k][:, t:t + 1], ALU.subtract, ALU.mult)
                last.then_inc(zz_ready, 1)
                for t in range(NT):
                    nc.vector.tensor_scalar(z[k % 2][:, t, :], xs[k][:, t, :], mv[k][:, t, 0:1],
                                            rstd[k][:, t:t + 1], ALU.subtract, ALU.mult)

            statistics(0, 0, 0)
            statistics(1, 0, 1)
            normalised(0, 0)

            def turn(i, last):
                for u in range(U):
                    c = U * i + u
                    if not (last and u >= U - 2):
                        statistics(c + 2, i + (u + 2) // U, (u + 2) % U)
                    if not (last and u == U - 1):
                        normalised(c + 1, (u + 1) % U)
                    n = 5 * c

                    def link(ins, k):
                        ins.then_inc(post_step, 1)
                        dve.wait_ge(post_step, n + k)
                    dve.wait_ge(back_done, c + 1)
                    link(nc.vector.tensor_tensor(res[:], z[u % 2][:], back_ps[u % 2][:].rearrange("p (t c) -> p t c", c=C),
                                                 ALU.add), 1)
                    for t in range(NT - 1):
                        nc.vector.bn_stats(st2[:, t, :], res[:, t, :])
                    link(nc.vector.bn_stats(st2[:, NT - 1, :], res[:, NT - 1, :]), 2)
                    nc.vector.memset(mark[:], 0.0)
                    for t in range(NT - 1):
                        nc.vector.bn_aggr(mv2[:, t, :], st2[:, t, :])
                    link(nc.vector.bn_aggr(mv2[:, NT - 1, :], st2[:, NT - 1, :]), 3)
                    nc.vector.tensor_scalar(ve2[:], mv2[:, :, 1], 1e-5, None, ALU.add).then_inc(var2_ready, 1)
                    dve.wait_ge(rstd2_ready, c + 1)
                    for t in range(NT - 1):
                        nc.vector.tensor_scalar(resn[:, t, :], res[:, t, :], mv2[:, t, 0:1], rstd2[:, t:t + 1],
                                                ALU.subtract, ALU.mult)
                    t = NT - 1
                    link(nc.vector.tensor_scalar(resn[:, t, :], res[:, t, :], mv2[:, t, 0:1], rstd2[:, t:t + 1],
                                                 ALU.subtract, ALU.mult), 4)
                    link(nc.vector.tensor_tensor(xs[u][:], resn[:], xs[u][:], ALU.add), 5)
                    nc.vector.memset(mark[:], 0.0).then_inc(x2_ready, 1)

            with dve.Fori(0, TURNS - 1) as i:
                turn(i, False)
            turn(TURNS - 1, True)

        @block.tensor
        def _(pe):
            def turn_in(c, k):
                pe.wait_ge(zz_ready, c + 1)
                for t in range(NT):
                    last = nc.tensor.transpose(in_ps[k % 2][:, t * 128:(t + 1) * 128], zz[k % 2][:, t, :], ident[:])
                last.then_inc(turned, 1)

            pe.wait_ge(loaded, 16 * 3)
            turn_in(0, 0)

            def turn(i, last):
                for u in range(U):
                    c = U * i + u
                    w = u // 2
                    if u % 2 == 0:
                        pe.wait_ge(w_in[w], 64 * (i + 1))
                    pe.wait_ge(hT_ready, c + 1)
                    for f in range(NF):
                        if f >= 2:
                            pe.wait_ge(gelu_done, NF * c + f - 1)
                        nc.tensor.matmul(h_ps[f % 2][:], w1[w][:, f * 128:(f + 1) * 128], hT[u % 2][:],
                                         start=True, stop=True).then_inc(h_done, 1)
                    if not (last and u == U - 1):
                        turn_in(c + 1, u + 1)
                    for f in range(NF):
                        pe.wait_ge(gelu_done, NF * c + f + 1)
                        last_i = nc.tensor.matmul(y_ps[u % 2][:], w2[w][:, f, :], gT[:, f, :],
                                                  start=f == 0, stop=f == NF - 1)
                    last_i.then_inc(y_done, 1)
                    pe.wait_ge(yT_ready, c + 1)
                    for t in range(NT):
                        last_i = nc.tensor.transpose(back_ps[u % 2][:, t * 128:(t + 1) * 128],
                                                     yT[:, t * 128:(t + 1) * 128], ident[:])
                    last_i.then_inc(back_done, 1)

            with pe.Fori(0, TURNS - 1) as i:
                turn(i, False)
            turn(TURNS - 1, True)


def row_statistics(nc, tag, x, mean, rstd):
    _, TILES, C = x.shape
    with ExitStack() as ctx:
        def sb(name, shape, dt=F32):
            return ctx.enter_context(nc.sbuf_tensor(f"{tag}_{name}", shape, dt))

        st = sb("st", [128, TILES, 6])
        msum = sb("msum", [128, TILES])
        mdif = sb("mdif", [128, TILES])
        mdd = sb("mdd", [128, TILES])
        m2 = sb("m2", [128, TILES])
        var = sb("var", [128, TILES])
        neg_half = sb("neg_half", [128, TILES])
        chain = ctx.enter_context(nc.semaphore(tag + "_chain"))
        var_ready = ctx.enter_context(nc.semaphore(tag + "_var_ready"))
        const_set = ctx.enter_context(nc.semaphore(tag + "_const_set"))
        rstd_ready = ctx.enter_context(nc.semaphore(tag + "_rstd_ready"))
        block = ctx.enter_context(nc.Block())

        @block.gpsimd
        def _(pool):
            nc.gpsimd.memset(neg_half[:], -0.5).then_inc(const_set, 1)
            pool.wait_ge(const_set, 1)
            pool.wait_ge(var_ready, 1)
            nc.gpsimd.tensor_tensor(rstd[:], var[:], neg_half[:], ALU.pow).then_inc(rstd_ready, 1)
            pool.wait_ge(rstd_ready, 1)

        @block.vector
        def _(dve):
            with dve.Fori(0, TILES // 4) as i:
                for u in range(4):
                    nc.vector.bn_stats(st[:, i * 4 + u, :], x[:, i * 4 + u, :])
            chained = [0]

            def link(ins):
                chained[0] += 1
                ins.then_inc(chain, 1)
                dve.wait_ge(chain, chained[0])

            link(nc.vector.memset(mdd[:], 0.0))
            nc.vector.tensor_tensor(msum[:], st[:, :, 1], st[:, :, 4], ALU.add)
            nc.vector.tensor_tensor(mdif[:], st[:, :, 1], st[:, :, 4], ALU.subtract)
            link(nc.vector.tensor_tensor(m2[:], st[:, :, 2], st[:, :, 5], ALU.add))
            nc.vector.tensor_scalar(mean[:], msum[:], 0.5, None, ALU.mult)
            link(nc.vector.scalar_tensor_tensor(mdd[:], mdif[:], 0.25, mdif[:], ALU.mult, ALU.mult))
            link(nc.vector.scalar_tensor_tensor(var[:], m2[:], 1.0 / C, mdd[:], ALU.mult, ALU.add))
            nc.vector.tensor_scalar(var[:], var[:], 1e-5, None, ALU.add).then_inc(var_ready, 1)


def l1_attention(nc, x, mean, rstd, wqk_d, wv_d, bqk_d, bv_d, wo_d, bo_d, rope_d, ident_in, parts):
    _, TILES, C = x.shape
    NT = 4
    T = NT * 128
    NB = TILES // NT
    HD = 8
    H = C // HD
    GH = 4
    NG = H // GH
    NP = 3
    ROWS = NP * NP * HD
    HC = 32
    MICRO = GH * NT
    PER_S = NG * MICRO
    M_PRE = 6
    M_BATCH = M_PRE + NG + 2
    qp_d, kp_d = parts

    with ExitStack() as ctx:
        def sb(name, shape, dt=F32):
            return ctx.enter_context(nc.sbuf_tensor("d_" + name + "_", shape, dt))

        def ps(name, shape):
            return ctx.enter_context(nc.psum_tensor("d_" + name + "_", shape, F32))

        def sem(name):
            return ctx.enter_context(nc.semaphore("d_" + name))

        wqk = sb("wqk", [128, 4, C])
        wv = sb("wv", [128, C])
        wo = sb("wo", [128, C])
        bqk = sb("bqk", [128, 4])
        bv = sb("bv", [128, C])
        bo = sb("bo", [128, C])
        rope = sb("rope", [128, 4, T])
        ident = sb("ident", [128, 128])
        identb = sb("identb", [128, 128], BF16)
        zz = sb("zz", [128, NT, C])
        zT = sb("zT", [128, T])
        prod = sb("prod", [128, 4, T])
        whole = [sb(f"whole{k}", [128, T]) for k in range(2)]
        rest = [sb(f"rest{k}", [128, T]) for k in range(2)]
        part = [sb(f"part{k}", [128, NP, T], BF16) for k in range(2)]
        qs = [sb(f"qs{k}", [ROWS, H, T], BF16) for k in range(2)]
        ks = [sb(f"ks{k}", [ROWS, H, T], BF16) for k in range(2)]
        v = [sb(f"v{k}", [128, NT, H, HC]) for k in range(2)]
        nmax = [sb(f"nmax{k}", [128, GH, NT], BF16) for k in range(2)]
        pT = [[sb(f"pT{k}_{h}", [128, T]) for h in range(GH)] for k in range(2)]
        oE = sb("oE", [128, T])
        rden = sb("rden", [128, NT, GH])
        quot = sb("quot", [128, NT, C])
        plus = sb("plus", [128, NT, C])
        att = sb("att", [128, NT, C])
        attT = sb("attT", [128, T])
        yb = sb("yb", [128, NT, C])
        yn = sb("yn", [128, NT, C])
        st2 = sb("st2", [128, NT, 6])
        mv2 = sb("mv2", [128, NT, 2])
        ve2 = sb("ve2", [128, NT])
        rstd2 = sb("rstd2", [128, NT])
        neg_half = sb("neg_half", [128, NT])
        mark = sb("mark", [128, 1])

        s_ps = [ps(f"s{k}", [128, T]) for k in range(2)]
        t_ps = [ps(f"t{k}", [128, T]) for k in range(GH)]
        o_ps = ps("o", [128, T])
        m_ps = ps("m", [128, T])
        m3 = m_ps[:].rearrange("p (t c) -> p t c", c=C)

        loaded = sem("loaded")
        const_set = sem("const_set")
        identb_ready = sem("identb_ready")
        zz_ready = sem("zz_ready")
        m_done = sem("m_done")
        m_free = sem("m_free")
        whole_ready = sem("whole_ready")
        part1 = sem("part1")
        rest_ready = sem("rest_ready")
        part2 = sem("part2")
        part3 = sem("part3")
        parts_out = sem("parts_out")
        stacked = sem("stacked")
        s_done = sem("s_done")
        max_done = sem("max_done")
        st_done = sem("st_done")
        exp_done = sem("exp_done")
        av_done = sem("av_done")
        oe_done = sem("oe_done")
        post_step = sem("post_step")
        var2_step = sem("var2_step")
        var2_ready = sem("var2_ready")
        rstd2_ready = sem("rstd2_ready")
        NLOADS = 8
        NSTACK = NP * NP + NP

        def m_use(b, n):
            return M_PRE + M_BATCH * b + n

        block = ctx.enter_context(nc.Block())

        @block.sync
        def _(sp):
            for dst, src in ((ident, ident_in), (wqk, wqk_d), (bqk, bqk_d), (rope, rope_d), (wv, wv_d),
                             (wo, wo_d), (bv, bv_d.to_broadcast([128, C])), (bo, bo_d.to_broadcast([128, C]))):
                sp.dma_start(dst[:], src).then_inc(loaded, 16)

            def stack(b, k):
                for side, dst in ((0, qp_d), (1, kp_d)):
                    sp.wait_ge(part3, 2 * b + side + 1)
                    sp.dma_start(dst[k].rearrange("n p t -> p n t"), part[side][:]).then_inc(parts_out, 16)
                sp.wait_ge(parts_out, 32 * (b + 1))
                for a in range(NP):
                    for c in range(NP):
                        r = (NP * a + c) * HD
                        sp.dma_start(qs[k][r:r + HD, :, :],
                                     qp_d[k, a].rearrange("(d h) t -> d h t", h=H)).then_inc(stacked, 16)
                    sp.dma_start(ks[k][NP * HD * a:NP * HD * (a + 1), :, :],
                                 kp_d[k].rearrange("n (d h) t -> (n d) h t", h=H)).then_inc(stacked, 16)

            stack(0, 0)

            def batch(b, k, last):
                if not last:
                    stack(b + 1, 1 - k)

            with sp.Fori(0, NB // 2 - 1) as i:
                for k in range(2):
                    batch(2 * i + k, k, False)
            batch(NB - 2, 0, False)

        @block.gpsimd
        def _(pool):
            nc.gpsimd.memset(neg_half[:], -0.5).then_inc(const_set, 1)
            for k in range(2):
                nc.gpsimd.memset(v[k][:], 0.0).then_inc(const_set, 1)
            pool.wait_ge(const_set, 3)
            for k in range(2):
                nc.gpsimd.memset(v[k][:, :, :, HD:HD + 1], 1.0).then_inc(const_set, 1)

            def wholes(b, use):
                for side in range(2):
                    pool.wait_ge(m_free, use + 2 * side + 2)
                    nc.gpsimd.tensor_tensor(whole[side][:], prod[:, 2 * side, :], prod[:, 2 * side + 1, :],
                                            ALU.add).then_inc(whole_ready, 1)

            wholes(0, 1)

            def batch(b, k, last):
                if not last:
                    wholes(b + 1, m_use(b, 1))
                pool.wait_ge(var2_ready, b + 1)
                nc.gpsimd.tensor_tensor(rstd2[:], ve2[:], neg_half[:], ALU.pow).then_inc(rstd2_ready, 1)

            with pool.Fori(0, NB // 2 - 1) as i:
                for k in range(2):
                    batch(2 * i + k, k, False)
            batch(NB - 2, 0, False)
            batch(NB - 1, 1, True)

        @block.scalar
        def _(act):
            act.wait_ge(loaded, 16 * NLOADS)
            nc.scalar.copy(identb[:], ident[:]).then_inc(identb_ready, 1)

            def turned(use):
                act.wait_ge(m_done, use + 1)
                nc.scalar.copy(zT[:], m_ps[:]).then_inc(m_free, 1)

            def first_part(b, side):
                act.wait_ge(whole_ready, 2 * b + side + 1)
                nc.scalar.copy(part[side][:, 0, :], whole[side][:]).then_inc(part1, 1)

            def second_part(b, side):
                act.wait_ge(rest_ready, 2 * b + side + 1)
                nc.scalar.copy(part[side][:, 1, :], rest[side][:]).then_inc(part2, 1)

            turned(0)
            for side in range(2):
                first_part(0, side)
                second_part(0, side)

            def batch(b, k, last):
                def out_copy(g):
                    act.wait_ge(av_done, NG * NT * b + NT * (g + 1))
                    if g:
                        act.wait_ge(m_done, m_use(b, (0 if last else M_PRE) + g - 1) + 1)
                    nc.scalar.copy(oE[:], o_ps[:]).then_inc(oe_done, 1)

                for g in range(NG):
                    for n in range(MICRO):
                        kt, h = divmod(n, GH)
                        if (g, kt) >= (0, 2) and h == 0:
                            act.wait_ge(av_done, NG * NT * b + NT * g + kt - 1)
                        act.wait_ge(st_done, PER_S * b + MICRO * g + n + 1)
                        nc.scalar.activation(pT[kt % 2][h][:], t_ps[h][:], ACT.Exp).then_inc(exp_done, 1)
                        if g >= 1 and n == 4:
                            out_copy(g - 1)
                        if not last:
                            if (g, n) == (0, 1):
                                turned(m_use(b, 0))
                            if (g, n) == (0, 8):
                                first_part(b + 1, 0)
                            if (g, n) == (0, 10):
                                second_part(b + 1, 0)
                            if (g, n) == (0, 13):
                                first_part(b + 1, 1)
                            if (g, n) == (1, 0):
                                second_part(b + 1, 1)
                out_copy(NG - 1)
                use = m_use(b, (0 if last else M_PRE) + NG)
                act.wait_ge(m_done, use + 1)
                nc.scalar.copy(attT[:], m_ps[:]).then_inc(m_free, 1)

            with act.Fori(0, NB // 2 - 1) as i:
                for k in range(2):
                    batch(2 * i + k, k, False)
            batch(NB - 2, 0, False)
            batch(NB - 1, 1, True)

        @block.vector
        def _(dve):
            def normalised(b):
                for t in range(NT):
                    n = NT * b + t
                    last = nc.vector.tensor_scalar(zz[:, t, :], x[:, n, :], mean[:, bass.ds(n, 1)],
                                                   rstd[:, bass.ds(n, 1)], ALU.subtract, ALU.mult)
                last.then_inc(zz_ready, 1)

            def rotary(b, c, use):
                dve.wait_ge(m_done, use + 1)
                nc.vector.scalar_tensor_tensor(prod[:, c, :], m_ps[:], bqk[:, c:c + 1], rope[:, c, :],
                                               ALU.add, ALU.mult).then_inc(m_free, 1)

            def values(b, k, use):
                dve.wait_ge(m_done, use + 1)
                nc.vector.tensor_tensor(v[k][:, :, :, 0:HD], m_ps[:].rearrange("p (t h d) -> p t h d", t=NT, h=H),
                                        bv[:].rearrange("p (o h d) -> p o h d", o=1, h=H).to_broadcast([128, NT, H, HD]),
                                        ALU.add).then_inc(m_free, 1)

            def remainder(b, side):
                dve.wait_ge(part1, 2 * b + side + 1)
                nc.vector.tensor_tensor(rest[side][:], whole[side][:], part[side][:, 0, :],
                                        ALU.subtract).then_inc(rest_ready, 1)

            def third_part(b, side):
                dve.wait_ge(part2, 2 * b + side + 1)
                nc.vector.tensor_tensor(part[side][:, 2, :], rest[side][:], part[side][:, 1, :],
                                        ALU.subtract).then_inc(part3, 1)

            def maximum(step, g, n):
                h, qt = divmod(n, NT)
                dve.wait_ge(s_done, step + 1)
                nc.vector.reduce_max(nmax[g % 2][:, h, qt:qt + 1], s_ps[n % 2][:], AX_X, negate=True).then_inc(max_done, 1)

            dve.wait_ge(loaded, 16 * NLOADS)
            normalised(0)
            for c in range(4):
                rotary(0, c, 1 + c)
            dve.wait_ge(const_set, 5)
            values(0, 0, 5)
            for side in range(2):
                remainder(0, side)
                third_part(0, side)
            for n in range(MICRO):
                maximum(n, 0, n)

            def batch(b, k, last):
                pre = 0 if last else M_PRE

                def quotients(g):
                    use = m_use(b, pre + g)
                    dve.wait_ge(m_done, use + 1)
                    got = m_ps[:].rearrange("p (t h c) -> p t h c", t=NT, c=HC)
                    cols = slice(g * GH * HD, (g + 1) * GH * HD)
                    nc.vector.reciprocal(rden[:], got[:, :, :, HD]).then_inc(post_step, 1)
                    dve.wait_ge(post_step, 13 * b + 3 * g + 1)
                    nc.vector.tensor_tensor(quot[:, :, cols].rearrange("p t (h d) -> p t h d", d=HD), got[:, :, :, 0:HD],
                                            rden[:].rearrange("p t (h o) -> p t h o", o=1).to_broadcast([128, NT, GH, HD]),
                                            ALU.mult).then_inc(m_free, 1)
                    dve.wait_ge(m_free, use + 1)
                    nc.vector.tensor_scalar(plus[:, :, cols], quot[:, :, cols], 0.0, None, ALU.max).then_inc(post_step, 1)
                    dve.wait_ge(post_step, 13 * b + 3 * g + 2)
                    nc.vector.scalar_tensor_tensor(att[:, :, cols], quot[:, :, cols], 0.0, plus[:, :, cols],
                                                   ALU.min, ALU.add).then_inc(post_step, 1)

                if not last:
                    normalised(b + 1)
                for g in range(NG):
                    for n in range(MICRO):
                        if not (last and g == NG - 1):
                            maximum(PER_S * b + MICRO * (g + 1) + n, g + 1, n)
                        if g >= 1 and n == 9:
                            quotients(g - 1)
                        if not last:
                            if (g, n) in ((0, 4), (0, 6), (0, 8), (0, 10)):
                                c = n // 2 - 2
                                rotary(b + 1, c, m_use(b, 1 + c))
                            if (g, n) == (0, 13):
                                values(b + 1, 1 - k, m_use(b, 5))
                            if (g, n) == (0, 9):
                                remainder(b + 1, 0)
                            if (g, n) == (0, 11):
                                third_part(b + 1, 0)
                            if (g, n) == (0, 14):
                                remainder(b + 1, 1)
                            if (g, n) == (1, 2):
                                third_part(b + 1, 1)
                quotients(NG - 1)
                use = m_use(b, pre + NG + 1)
                dve.wait_ge(m_done, use + 1)
                nc.vector.tensor_tensor(yb[:], m3, bo[:].rearrange("p (o c) -> p o c", o=1).to_broadcast([128, NT, C]),
                                        ALU.add).then_inc(m_free, 1)
                dve.wait_ge(m_free, use + 1)
                for t in range(NT):
                    ins = nc.vector.bn_stats(st2[:, t, :], yb[:, t, :])
                ins.then_inc(var2_step, 1)
                dve.wait_ge(var2_step, 2 * b + 1)
                nc.vector.memset(mark[:], 0.0)
                for t in range(NT):
                    ins = nc.vector.bn_aggr(mv2[:, t, :], st2[:, t, :])
                ins.then_inc(var2_step, 1)
                dve.wait_ge(var2_step, 2 * b + 2)
                nc.vector.tensor_scalar(ve2[:], mv2[:, :, 1], 1e-5, None, ALU.add).then_inc(var2_ready, 1)
                dve.wait_ge(rstd2_ready, b + 1)
                for t in range(NT):
                    ins = nc.vector.tensor_scalar(yn[:, t, :], yb[:, t, :], mv2[:, t, 0:1], rstd2[:, t:t + 1],
                                                  ALU.subtract, ALU.mult)
                ins.then_inc(post_step, 1)
                dve.wait_ge(post_step, 13 * b + 13)
                rows = x[:, bass.ds(NT * b, NT), :]
                nc.vector.tensor_tensor(rows, yn[:], rows, ALU.add)

            with dve.Fori(0, NB // 2 - 1) as i:
                for k in range(2):
                    batch(2 * i + k, k, False)
            batch(NB - 2, 0, False)
            batch(NB - 1, 1, True)

        @block.tensor
        def _(pe):
            def m_ready(use):
                if not (isinstance(use, int) and use == 0):
                    pe.wait_ge(m_free, use)

            def turn_in(b, use):
                pe.wait_ge(zz_ready, b + 1)
                m_ready(use)
                for t in range(NT):
                    ins = nc.tensor.transpose(m_ps[:, t * 128:(t + 1) * 128], zz[:, t, :], ident[:])
                ins.then_inc(m_done, 1)

            def project(c, use):
                m_ready(use)
                nc.tensor.matmul(m_ps[:], wqk[:, c, :], zT[:], start=True, stop=True).then_inc(m_done, 1)

            def project_v(use):
                m_ready(use)
                for t in range(NT):
                    ins = nc.tensor.matmul(m_ps[:, t * C:(t + 1) * C], zT[:, t * 128:(t + 1) * 128], wv[:],
                                           start=True, stop=True)
                ins.then_inc(m_done, 1)

            def scores(step, k, g, n):
                h, qt = divmod(n, NT)
                h += g * GH
                if not (isinstance(step, int) and step < 2):
                    pe.wait_ge(max_done, step - 1)
                nc.tensor.matmul(s_ps[n % 2][:], qs[k][:, h, qt * 128:(qt + 1) * 128], ks[k][:, h, :],
                                 start=True, stop=True).then_inc(s_done, 1)

            pe.wait_ge(loaded, 16 * NLOADS)
            turn_in(0, 0)
            for c in range(4):
                project(c, 1 + c)
            project_v(5)
            pe.wait_ge(identb_ready, 1)
            pe.wait_ge(stacked, 16 * NSTACK)
            for n in range(MICRO):
                scores(n, 0, 0, n)

            def batch(b, k, last):
                pre = 0 if last else M_PRE

                def shifted(g, n):
                    kt, h = divmod(n, GH)
                    if (g, kt) >= (0, 1):
                        pe.wait_ge(exp_done, PER_S * b + MICRO * g + n - GH + 1)
                    if n == 0:
                        pe.wait_ge(max_done, PER_S * b + MICRO * (g + 1))
                    hh = g * GH + h
                    nc.tensor.matmul(t_ps[h][:], ks[k][:, hh, kt * 128:(kt + 1) * 128], qs[k][:, hh, :],
                                     start=True, stop=False)
                    for qt in range(NT):
                        ins = nc.tensor.matmul(t_ps[h][:, qt * 128:(qt + 1) * 128],
                                               nmax[g % 2][:, h, qt:qt + 1].to_broadcast([128, 128]), identb[:],
                                               start=False, stop=qt == NT - 1)
                    ins.then_inc(st_done, 1)

                def weighted(g, kt):
                    pe.wait_ge(exp_done, PER_S * b + MICRO * g + GH * (kt + 1))
                    if kt == 0 and g:
                        pe.wait_ge(oe_done, NG * b + g)
                    for h in range(GH):
                        ins = nc.tensor.matmul(o_ps[HC * h:HC * (h + 1), :], v[k][:, kt, g * GH + h, :], pT[kt % 2][h][:],
                                               start=kt == 0, stop=kt == NT - 1)
                    ins.then_inc(av_done, 1)

                def turn_out(g):
                    use = m_use(b, pre + g)
                    m_ready(use)
                    pe.wait_ge(oe_done, NG * b + g + 1)
                    for t in range(NT):
                        ins = nc.tensor.transpose(m_ps[:, t * 128:(t + 1) * 128], oE[:, t * 128:(t + 1) * 128], ident[:])
                    ins.then_inc(m_done, 1)

                for g in range(NG):
                    for n in range(MICRO):
                        if g < NG - 1:
                            scores(PER_S * b + MICRO * (g + 1) + n, k, g + 1, n)
                        elif not last:
                            if n == 0:
                                pe.wait_ge(stacked, 16 * NSTACK * (b + 2))
                            scores(PER_S * b + MICRO * (g + 1) + n, 1 - k, 0, n)
                        shifted(g, n)
                        if n % GH == GH - 1 and n > GH:
                            weighted(g, n // GH - 1)
                        if g and n == GH - 1:
                            weighted(g - 1, NT - 1)
                        if g and n == 9:
                            turn_out(g - 1)
                        if g == 0 and not last:
                            if n == 1:
                                turn_in(b + 1, m_use(b, 0))
                            if n in (4, 6, 8, 10):
                                project(n // 2 - 2, m_use(b, n // 2 - 1))
                            if n == 13:
                                project_v(m_use(b, 5))
                weighted(NG - 1, NT - 1)
                turn_out(NG - 1)
                use = m_use(b, pre + NG)
                m_ready(use)
                pe.wait_ge(post_step, 13 * b + 12)
                for t in range(NT):
                    ins = nc.tensor.transpose(m_ps[:, t * 128:(t + 1) * 128], att[:, t, :], ident[:])
                ins.then_inc(m_done, 1)
                m_ready(use + 1)
                for t in range(NT):
                    ins = nc.tensor.matmul(m_ps[:, t * C:(t + 1) * C], attT[:, t * 128:(t + 1) * 128], wo[:],
                                           start=True, stop=True)
                ins.then_inc(m_done, 1)

            with pe.Fori(0, NB // 2 - 1) as i:
                for k in range(2):
                    batch(2 * i + k, k, False)
            batch(NB - 2, 0, False)
            batch(NB - 1, 1, True)


def l1_ffn(nc, x, mean, rstd, w1_d, b1_d, phase_d, real_d, imag_d, w2_d, b2_d, ident_in, out):
    _, TILES, C = x.shape
    NT = 4
    CH = NT * 128
    NCH = TILES // NT
    F = w1_d.shape[1]
    NF = F // 128
    U = 2
    TURNS = NCH // U
    INV = 1.0 / (2 * np.pi)
    MAGIC = 1.5 * 2.0 ** 23
    P1 = 6.28125
    P2 = float(np.float32(int((2 * np.pi - P1) * 2 ** 21) / 2 ** 21))
    P3 = float(np.float32(2 * np.pi - P1 - P2))
    TURN = 6.283185
    out_v = out.rearrange("(n t p) c -> n p t c", p=128, t=NT)

    with ExitStack() as ctx:
        def sb(name, shape, dt=F32):
            return ctx.enter_context(nc.sbuf_tensor("e_" + name + "_", shape, dt))

        def ps(name, shape):
            return ctx.enter_context(nc.psum_tensor("e_" + name + "_", shape, F32))

        def sem(name):
            return ctx.enter_context(nc.semaphore("e_" + name))

        w1 = sb("w1", [128, F])
        w2 = sb("w2", [128, NF, C])
        b1 = sb("b1", [128, NF])
        b2 = sb("b2", [128, 1])
        phase = sb("phase", [128, NF])
        real = sb("real", [128, NF])
        imag = sb("imag", [128, NF])
        ident = sb("ident", [128, 128])
        kk = sb("kk", [128, NF])
        red = [sb(f"red{k}", [128, NF]) for k in range(2)]
        theta = sb("theta", [128, NF])
        quarter = sb("quarter", [128, NF])
        whole = sb("whole", [128, NF])
        cosine = sb("cosine", [128, NF])
        sine = sb("sine", [128, NF])
        qa = sb("qa", [128, NF])
        qb = sb("qb", [128, NF])
        gain = sb("gain", [128, NF])
        offset = sb("offset", [128, NF])
        zz = [sb(f"zz{k}", [128, NT, C]) for k in range(U)]
        zT = [sb(f"zT{k}", [128, CH]) for k in range(U)]
        turns = [sb(f"turns{k}", [128, CH]) for k in range(2)]
        near = [sb(f"near{k}", [128, CH]) for k in range(2)]
        frac = [sb(f"frac{k}", [128, CH]) for k in range(2)]
        sn = [sb(f"sn{k}", [128, CH]) for k in range(2)]
        pre = [sb(f"pre{k}", [128, CH]) for k in range(2)]
        gT = sb("gT", [128, NF, CH])
        yT = sb("yT", [128, CH])
        yn = sb("yn", [128, NT, C])
        xo = [sb(f"xo{k}", [128, NT, C]) for k in range(U)]
        st2 = sb("st2", [128, NT, 6])
        mv2 = sb("mv2", [128, NT, 2])
        ve2 = sb("ve2", [128, NT])
        rstd2 = sb("rstd2", [128, NT])
        neg_half = sb("neg_half", [128, NT])
        mark = sb("mark", [128, 1])

        in_ps = ps("in", [128, CH])
        h_ps = [ps(f"h{k}", [128, CH]) for k in range(NF)]
        y_ps = ps("y", [128, CH])
        back_ps = ps("back", [128, CH])

        loaded = sem("loaded")
        const_set = sem("const_set")
        chain = sem("chain")
        angles = sem("angles")
        sines = sem("sines")
        factors = sem("factors")
        zz_ready = sem("zz_ready")
        turned = sem("turned")
        zT_ready = sem("zT_ready")
        h_done = sem("h_done")
        turns_ready = sem("turns_ready")
        near_ready = sem("near_ready")
        frac_ready = sem("frac_ready")
        sin_ready = sem("sin_ready")
        pre_ready = sem("pre_ready")
        relu_done = sem("relu_done")
        y_done = sem("y_done")
        yT_ready = sem("yT_ready")
        back_done = sem("back_done")
        post_step = sem("post_step")
        var2_ready = sem("var2_ready")
        rstd2_ready = sem("rstd2_ready")
        x_ready = sem("x_ready")
        stored = sem("stored")
        NLOADS = 8

        block = ctx.enter_context(nc.Block())

        @block.sync
        def _(sp):
            for dst, src in ((ident, ident_in), (w1, w1_d), (phase, phase_d), (b1, b1_d), (real, real_d), (imag, imag_d),
                             (b2, b2_d), (w2, w2_d.rearrange("(f p) c -> p f c", p=128))):
                sp.dma_start(dst[:], src).then_inc(loaded, 16)
            with sp.Fori(0, TURNS) as i:
                for u in range(U):
                    c = U * i + u
                    sp.wait_ge(x_ready, c + 1)
                    sp.dma_start(out_v[c], xo[u][:]).then_inc(stored, 16)
            sp.wait_ge(stored, 16 * NCH + 1)

        @block.gpsimd
        def _(pool):
            nc.gpsimd.memset(neg_half[:], -0.5).then_inc(const_set, 1)
            nc.gpsimd.memset(mark[:], 0.0).then_inc(stored, 1)
            pool.wait_ge(const_set, 1)
            with pool.Fori(0, NCH) as c:
                pool.wait_ge(var2_ready, c + 1)
                nc.gpsimd.tensor_tensor(rstd2[:], ve2[:], neg_half[:], ALU.pow).then_inc(rstd2_ready, 1)

        @block.scalar
        def _(act):
            act.wait_ge(angles, 1)
            nc.scalar.activation(sine[:], theta[:], ACT.Sin, scale=TURN)
            nc.scalar.activation(cosine[:], quarter[:], ACT.Sin, scale=TURN).then_inc(sines, 1)

            def turn_in(c, k):
                act.wait_ge(turned, c + 1)
                nc.scalar.activation(zT[k][:], in_ps[:], ACT.Copy).then_inc(zT_ready, 1)

            turn_in(0, 0)
            act.wait_ge(factors, 1)

            def turn(i, last):
                for u in range(U):
                    c = U * i + u

                    def angle(f):
                        act.wait_ge(h_done, NF * c + f + 1)
                        nc.scalar.activation(turns[f % 2][:], h_ps[f][:], ACT.Identity, bias=offset[:, f:f + 1],
                                             scale=0.1 * INV).then_inc(turns_ready, 1)

                    def sin(f):
                        act.wait_ge(frac_ready, NF * c + f + 1)
                        nc.scalar.activation(sn[f % 2][:], frac[f % 2][:], ACT.Sin, scale=TURN).then_inc(sin_ready, 1)

                    def relu(f):
                        act.wait_ge(pre_ready, NF * c + f + 1)
                        nc.scalar.activation(gT[:, f, :], pre[f % 2][:], ACT.Relu, bias=b1[:, f:f + 1]).then_inc(relu_done, 1)

                    for f in range(NF + 2):
                        if f < NF:
                            angle(f)
                        if 1 <= f <= NF:
                            sin(f - 1)
                        if f >= 2:
                            relu(f - 2)
                        if f == NF and not (last and u == U - 1):
                            turn_in(c + 1, 1 - u)
                    act.wait_ge(y_done, c + 1)
                    nc.scalar.activation(yT[:], y_ps[:], ACT.Identity, bias=b2[:]).then_inc(yT_ready, 1)

            with act.Fori(0, TURNS - 1) as i:
                turn(i, False)
            turn(TURNS - 1, True)

        @block.vector
        def _(dve):
            chained = [0]

            def link(ins):
                chained[0] += 1
                ins.then_inc(chain, 1)
                dve.wait_ge(chain, chained[0])

            def normalised(c, k):
                for t in range(NT):
                    n = NT * c + t
                    ins = nc.vector.tensor_scalar(zz[k][:, t, :], x[:, n, :], mean[:, bass.ds(n, 1)],
                                                  rstd[:, bass.ds(n, 1)], ALU.subtract, ALU.mult)
                ins.then_inc(zz_ready, 1)

            nc.vector.memset(whole[:], 0.0).then_inc(post_step, 1)
            normalised(0, 0)
            dve.wait_ge(loaded, 16 * NLOADS)
            link(nc.vector.tensor_scalar(kk[:], phase[:], INV, MAGIC, ALU.mult, ALU.add))
            link(nc.vector.tensor_scalar(kk[:], kk[:], MAGIC, None, ALU.subtract))
            link(nc.vector.scalar_tensor_tensor(red[0][:], kk[:], -P1, phase[:], ALU.mult, ALU.add))
            link(nc.vector.scalar_tensor_tensor(red[1][:], kk[:], -P2, red[0][:], ALU.mult, ALU.add))
            link(nc.vector.scalar_tensor_tensor(red[0][:], kk[:], -P3, red[1][:], ALU.mult, ALU.add))
            link(nc.vector.tensor_scalar(red[1][:], red[0][:], INV, None, ALU.mult))
            link(nc.vector.tensor_scalar(kk[:], red[1][:], MAGIC, MAGIC, ALU.add, ALU.subtract))
            link(nc.vector.tensor_tensor(theta[:], red[1][:], kk[:], ALU.subtract))
            link(nc.vector.tensor_scalar(quarter[:], theta[:], 0.25, None, ALU.add))
            link(nc.vector.tensor_scalar(whole[:], quarter[:], MAGIC, MAGIC, ALU.add, ALU.subtract))
            nc.vector.tensor_tensor(quarter[:], quarter[:], whole[:], ALU.subtract).then_inc(angles, 1)
            dve.wait_ge(sines, 1)
            nc.vector.tensor_tensor(qa[:], cosine[:], real[:], ALU.mult)
            link(nc.vector.tensor_tensor(qb[:], sine[:], imag[:], ALU.mult))
            link(nc.vector.tensor_tensor(qa[:], qa[:], qb[:], ALU.add))
            link(nc.vector.scalar_tensor_tensor(gain[:], qa[:], 0.1, imag[:], ALU.mult, ALU.mult))
            nc.vector.scalar_tensor_tensor(offset[:], b1[:], 0.1 * INV, theta[:], ALU.mult, ALU.add).then_inc(factors, 1)
            dve.wait_ge(factors, 1)

            def turn(i, last):
                for u in range(U):
                    c = U * i + u
                    if not (last and u == U - 1):
                        normalised(c + 1, 1 - u)

                    def fraction(f):
                        k = f % 2
                        dve.wait_ge(turns_ready, NF * c + f + 1)
                        nc.vector.tensor_scalar(near[k][:], turns[k][:], MAGIC, MAGIC, ALU.add,
                                                ALU.subtract).then_inc(near_ready, 1)
                        dve.wait_ge(near_ready, NF * c + f + 1)
                        nc.vector.tensor_tensor(frac[k][:], turns[k][:], near[k][:], ALU.subtract).then_inc(frac_ready, 1)

                    def combine(f):
                        dve.wait_ge(sin_ready, NF * c + f + 1)
                        nc.vector.scalar_tensor_tensor(pre[f % 2][:], sn[f % 2][:], gain[:, f:f + 1], h_ps[f][:],
                                                       ALU.mult, ALU.add).then_inc(pre_ready, 1)

                    for f in range(NF + 1):
                        if f < NF:
                            fraction(f)
                        if f:
                            combine(f - 1)

                    n = 3 * c
                    dve.wait_ge(back_done, c + 1)
                    for t in range(NT):
                        ins = nc.vector.bn_stats(st2[:, t, :], back_ps[:, t * 128:(t + 1) * 128])
                    ins.then_inc(post_step, 1)
                    dve.wait_ge(post_step, n + 2)
                    nc.vector.memset(kk[:], 0.0)
                    for t in range(NT):
                        ins = nc.vector.bn_aggr(mv2[:, t, :], st2[:, t, :])
                    ins.then_inc(post_step, 1)
                    dve.wait_ge(post_step, n + 3)
                    nc.vector.tensor_scalar(ve2[:], mv2[:, :, 1], 1e-5, None, ALU.add).then_inc(var2_ready, 1)
                    dve.wait_ge(rstd2_ready, c + 1)
                    for t in range(NT):
                        ins = nc.vector.tensor_scalar(yn[:, t, :], back_ps[:, t * 128:(t + 1) * 128], mv2[:, t, 0:1],
                                                      rstd2[:, t:t + 1], ALU.subtract, ALU.mult)
                    ins.then_inc(post_step, 1)
                    dve.wait_ge(post_step, n + 4)
                    dve.wait_ge(stored, 16 * c + 1)
                    nc.vector.tensor_tensor(xo[u][:], yn[:], x[:, bass.ds(NT * c, NT), :], ALU.add).then_inc(x_ready, 1)

            with dve.Fori(0, TURNS - 1) as i:
                turn(i, False)
            turn(TURNS - 1, True)

        @block.tensor
        def _(pe):
            def turn_in(c, k):
                pe.wait_ge(zz_ready, c + 1)
                for t in range(NT):
                    ins = nc.tensor.transpose(in_ps[:, t * 128:(t + 1) * 128], zz[k][:, t, :], ident[:])
                ins.then_inc(turned, 1)

            pe.wait_ge(loaded, 16 * NLOADS)
            turn_in(0, 0)

            def turn(i, last):
                for u in range(U):
                    c = U * i + u
                    pe.wait_ge(zT_ready, c + 1)
                    for f in range(NF):
                        nc.tensor.matmul(h_ps[f][:], w1[:, f * 128:(f + 1) * 128], zT[u][:],
                                         start=True, stop=True).then_inc(h_done, 1)
                    if not (last and u == U - 1):
                        turn_in(c + 1, 1 - u)
                    for f in range(NF):
                        pe.wait_ge(relu_done, NF * c + f + 1)
                        ins = nc.tensor.matmul(y_ps[:], w2[:, f, :], gT[:, f, :], start=f == 0, stop=f == NF - 1)
                    ins.then_inc(y_done, 1)
                    pe.wait_ge(yT_ready, c + 1)
                    pe.wait_ge(post_step, 3 * c + 1)
                    for t in range(NT):
                        ins = nc.tensor.transpose(back_ps[:, t * 128:(t + 1) * 128], yT[:, t * 128:(t + 1) * 128], ident[:])
                    ins.then_inc(back_done, 1)

            with pe.Fori(0, TURNS - 1) as i:
                turn(i, False)
            turn(TURNS - 1, True)


def gather_rows(nc, x, pos, rows):
    _, TILES, _ = x.shape
    with nc.semaphore("g_gathered") as gathered, nc.Block() as block:
        @block.gpsimd
        def _(pool):
            for t in range(TILES):
                pool.indirect_dma_start(out=x[:, t, :], out_offset=None, in_=rows,
                                        in_offset=bass.IndirectOffsetOnAxis(ap=pos[:, t:t + 1], axis=0)).then_inc(gathered, 16)
            pool.wait_ge(gathered, 16 * TILES)


def program(nc, a, out, B, T, C):
    TILES = B * T // 128
    sorted_x = nc.dram_tensor("sorted_x", (B * T, C), F32).ap()
    sorted_x2 = nc.dram_tensor("sorted_x2", (B * T, C), F32).ap()
    q_parts = nc.dram_tensor("q_parts", (2, 3, C, T), BF16).ap()
    k_parts = nc.dram_tensor("k_parts", (2, 3, C, T), BF16).ap()
    with ExitStack() as ctx:
        x = ctx.enter_context(nc.sbuf_tensor("x_tokens", [128, TILES, C], F32))
        pos = ctx.enter_context(nc.sbuf_tensor("pos", [128, TILES], I32))
        mean = ctx.enter_context(nc.sbuf_tensor("mean", [128, TILES], F32))
        rstd = ctx.enter_context(nc.sbuf_tensor("rstd", [128, TILES], F32))
        l0_attention(nc, a["x"], a["l0_w"], a["l0_wo"], a["l0_rope"], a["l0_masks_q"], a["l0_masks_k"], a["ident"], x)
        routing(nc, x, pos, mean, rstd, a["centroids"], a["ln_g"], a["ln_b"], a["ident"], a["ones"], a["before"], sorted_x)
        expert_ffn(nc, sorted_x, a["e_w1"], a["e_b1"], a["e_w2"], a["e_b2"], a["ln_g"], a["ln_b"], a["ident"], sorted_x2)
        gather_rows(nc, x, pos, sorted_x2)
        row_statistics(nc, "r1", x, mean, rstd)
        l1_attention(nc, x, mean, rstd, a["l1_wqk"], a["l1_wv"], a["l1_bqk"], a["l1_bv"], a["l1_wo"], a["l1_bo"],
                     a["l1_rope"], a["ident"], (q_parts, k_parts))
        row_statistics(nc, "r2", x, mean, rstd)
        l1_ffn(nc, x, mean, rstd, a["f_w1"], a["f_b1"], a["f_phase"], a["f_real"], a["f_imag"], a["f_w2"], a["f_b2"],
               a["ident"], out)


def l0_constants(T, head_dim, window, block):
    half = head_dim // 2
    inv_freq = np.float32(1.0) / np.power(np.float32(10000.0), np.arange(0, head_dim, 2, dtype=np.float32) / np.float32(head_dim))
    freqs = np.outer(np.arange(T, dtype=np.float32), inv_freq.astype(np.float32))
    cos, sin = np.cos(freqs).T, np.sin(freqs).T
    cos2 = np.concatenate([cos, cos] * 2)
    sin2 = np.concatenate([-sin, sin] * 2)
    scale = head_dim ** -0.5
    rope = np.stack([cos2 * scale, sin2 * scale, cos2, sin2], axis=1).astype(np.float32)
    nj = -(-T // block)
    key = np.arange(128)[:, None, None]
    blk = np.arange(nj)[None, :, None]
    qry = np.arange(block)[None, None, :]
    seen = (qry <= key) & (key <= qry + window) & (key + block * blk >= window)
    off = np.where(seen, 0.0, MASKED).astype(np.float32)
    masks_k = off.reshape(128, nj * block)[:, :T]
    masks_q = off.transpose(2, 1, 0).reshape(block, nj * 128)
    return np.ascontiguousarray(rope), masks_q, np.ascontiguousarray(masks_k)


def partner(w, head_dim):
    half = head_dim // 2
    n, c = w.shape
    return w.reshape(n // head_dim, 2, half, c)[:, ::-1].reshape(n, c)


def l1_constants(T, heads, head_dim):
    inv_freq = np.float32(1.0) / np.power(np.float32(10000.0), np.arange(0, head_dim, 2, dtype=np.float32) / np.float32(head_dim))
    freqs = np.outer(np.arange(T, dtype=np.float32), inv_freq.astype(np.float32))
    cos, sin = np.cos(freqs).T, np.sin(freqs).T
    cos2 = np.repeat(np.concatenate([cos, cos]), heads, axis=0)
    sin2 = np.repeat(np.concatenate([-sin, sin]), heads, axis=0)
    scale = head_dim ** -0.5
    return np.stack([cos2 * scale, sin2 * scale, cos2, sin2], axis=1).astype(np.float32)


def by_dimension(w, heads, head_dim, swapped):
    w = w.reshape(*w.shape[:-1], heads, head_dim)
    if swapped:
        w = np.roll(w, head_dim // 2, axis=-1)
    return np.swapaxes(w, -1, -2).reshape(*w.shape[:-2], heads * head_dim)


def l1_weights(wqkv, bqkv, heads):
    c = wqkv.shape[0]
    d = c // heads
    q, k, v = (wqkv[:, n * c:(n + 1) * c] for n in range(3))
    bq, bk, bv = (bqkv[n * c:(n + 1) * c] for n in range(3))
    w = np.stack([by_dimension(a, heads, d, s) for a in (q, k) for s in (False, True)], axis=1)
    b = np.stack([by_dimension(a, heads, d, s) for a in (bq, bk) for s in (False, True)], axis=1)
    return w, b, v, bv.reshape(1, c)


def kernel(L0_attn_x, L0_attn_w_qkv, L0_attn_w_out, L0_ffn_centroids, L0_ffn_ln_g, L0_ffn_ln_b, L0_ffn_w1, L0_ffn_b1,
           L0_ffn_w2, L0_ffn_b2, L1_attn_Wqkv, L1_attn_bqkv, L1_attn_Wout, L1_attn_bout, L1_ffn_W1, L1_ffn_b1,
           L1_ffn_quantum_phases, L1_ffn_quantum_weights_real, L1_ffn_quantum_weights_imag, L1_ffn_W2, L1_ffn_b2):
    import ml_dtypes
    import concourse.bacc as _bacc
    from concourse.bass_utils import run_bass_kernel_spmd as _run

    nc = _bacc.Bacc("TRN2", target_bir_lowering=False, num_devices=1)
    arrays, a = {}, {}

    def give(name, array):
        array = np.ascontiguousarray(array)
        arrays[name] = array
        a[name] = nc.dram_tensor(name, array.shape, mybir.dt.from_np(array.dtype), kind="ExternalInput").ap()

    def columns(v):
        return np.asarray(v).reshape(-1, 128).T

    x = np.asarray(L0_attn_x)
    B, T, C = x.shape
    bf = ml_dtypes.bfloat16
    give("x", x)
    give("ident", np.eye(128, dtype=np.float32))
    give("ones", np.ones((128, 128), bf))
    give("before", np.triu(np.ones((128, 128)), 1).astype(bf))
    q, k, v = np.split(np.asarray(L0_attn_w_qkv), 3)
    give("l0_w", np.concatenate([q, partner(q, L0_HEAD), k, partner(k, L0_HEAD), v]).T)
    give("l0_wo", np.asarray(L0_attn_w_out).T)
    rope, masks_q, masks_k = l0_constants(T, L0_HEAD, L0_WINDOW, L0_BLOCK)
    give("l0_rope", rope)
    give("l0_masks_q", masks_q.astype(bf))
    give("l0_masks_k", masks_k.astype(bf))
    E, _, F = np.asarray(L0_ffn_w1).shape
    give("centroids", np.asarray(L0_ffn_centroids).T)
    give("ln_g", columns(L0_ffn_ln_g))
    give("ln_b", columns(L0_ffn_ln_b))
    give("e_w1", np.asarray(L0_ffn_w1))
    give("e_b1", np.asarray(L0_ffn_b1).reshape(E, F // 128, 128).transpose(0, 2, 1))
    give("e_w2", np.asarray(L0_ffn_w2))
    give("e_b2", np.asarray(L0_ffn_b2).reshape(E, C, 1))
    wqk, bqk, wv, bv = l1_weights(np.asarray(L1_attn_Wqkv), np.asarray(L1_attn_bqkv), L1_HEADS)
    give("l1_wqk", wqk)
    give("l1_bqk", bqk)
    give("l1_wv", wv)
    give("l1_bv", bv)
    give("l1_wo", np.asarray(L1_attn_Wout))
    give("l1_bo", np.asarray(L1_attn_bout).reshape(1, C))
    give("l1_rope", l1_constants(T, L1_HEADS, C // L1_HEADS))
    give("f_w1", np.asarray(L1_ffn_W1))
    give("f_b1", columns(L1_ffn_b1))
    give("f_phase", columns(L1_ffn_quantum_phases))
    give("f_real", columns(L1_ffn_quantum_weights_real))
    give("f_imag", columns(L1_ffn_quantum_weights_imag))
    give("f_w2", np.asarray(L1_ffn_W2))
    give("f_b2", columns(L1_ffn_b2))

    out = nc.dram_tensor("out_0_dram", x.shape, F32, kind="ExternalOutput").ap()
    program(nc, a, out.rearrange("b t c -> (b t) c"), B, T, C)
    return _run(nc, [arrays], core_ids=[0]).results[0]["out_0_dram"]
```

```python
from contextlib import ExitStack

import numpy as np

import concourse.bass as bass
from concourse import mybir

F32 = mybir.dt.float32
F32R = mybir.dt.float32r
BF16 = mybir.dt.bfloat16
I32 = mybir.dt.int32
ALU = mybir.AluOpType
ACT = mybir.ActivationFunctionType
AX_X = mybir.AxisListType.X
MASKED = -1e30
L0_HEAD = 64
L0_WINDOW = 32
L1_HEADS = 16


def l0_attention(nc, x_in, w_l0, wo_l0, rope_l0, masks_q, masks_k, ident_in, x1):
    NB, T, C = x_in.shape
    NT = T // 128
    HD = 64
    PAIRS = wo_l0.shape[0] // 128
    HALF = 4 * 128
    WIN = 32
    BAND = 128 + WIN
    widths = [min(BAND, T - 128 * t) for t in range(NT)]
    GT = NT // 2
    PW = BAND * (NT - 1) + widths[-1]
    VH = w_l0.shape[1] // 5
    NV = NT * (VH // HALF)

    x_v = x_in.rearrange("b (t p) c -> b p t c", p=128)

    with ExitStack() as ctx:
        def sb(name, shape, dt=F32):
            return ctx.enter_context(nc.sbuf_tensor("a_" + name, shape, dt))

        def ps(name, shape):
            return ctx.enter_context(nc.psum_tensor("a_" + name, shape, F32))

        def sem(name):
            return ctx.enter_context(nc.semaphore("a_" + name))

        w_sb = sb("w", [128, 5 * VH])
        wo_sb = sb("wo", [128, PAIRS, C])
        rope = sb("rope", [128, 4, T])
        mq = sb("mq", [128, NT * BAND], BF16)
        mk = sb("mk", [128, GT * BAND], BF16)
        ident = sb("ident", [128, 128])
        identx = sb("identx", [128, WIN + 128], BF16)
        ones = sb("ones", [128, HD])
        xpre = sb("xpre", [128, NT, C])
        xres = sb("xres", [128, NT, C])
        xn = sb("xn", [128, NT, C])
        xnT = [sb(f"xnT{k}", [128, T]) for k in range(2)]
        v_sb = [sb(f"v{k}", [128, NT, VH]) for k in range(2)]
        prod = [sb(f"prod{k}", [128, 4, T]) for k in range(2)]
        qT = [sb(f"qT{k}", [128, T]) for k in range(4)]
        kT = [sb(f"kT{k}", [128, T]) for k in range(4)]
        qB = [sb(f"qB{k}", [128, T], BF16) for k in range(2)]
        kB = [sb(f"kB{k}", [128, WIN + T], BF16) for k in range(2)]
        nmax = [sb(f"nmax{k}", [128, 2, NT], BF16) for k in range(2)]
        pT = [[sb(f"pT{k}{h}", [128, PW]) for h in range(2)] for k in range(2)]
        lnden = sb("lnden", [128, T])
        rden = sb("rden", [128, T])
        oT = sb("oT", [128, PAIRS, T])
        yT = sb("yT", [128, T])
        ynorm = sb("ynorm", [128, NT, C])
        st1 = sb("st1", [128, NT, 6])
        mv1 = sb("mv1", [128, NT, 2])
        st2 = sb("st2", [128, NT, 6])
        mv2 = sb("mv2", [128, NT, 2])
        neg_half = sb("neg_half", [128, NT])
        ve = sb("ve", [128, NT])
        rstd = sb("rstd", [128, NT])
        ms = sb("ms", [128, NT])
        ms2 = sb("ms2", [128, NT])
        rr = sb("rr", [128, NT])
        comb = sb("comb", [128, NT])
        eps5 = sb("eps5", [128, NT])
        eps6 = sb("eps6", [128, NT])
        mark = sb("mark", [128, 1])
        ve2 = sb("ve2", [128, NT])
        rstd2 = sb("rstd2", [128, NT])

        proj = [ps(f"proj{k}", [128, HALF]) for k in range(2)]
        s_ps = [ps(f"s{k}", [128, HALF]) for k in range(2)]
        t_ps = [ps(f"t{k}", [128, HALF]) for k in range(2)]
        o_ps = ps("o", [128, HALF])
        d_ps = ps("d", [128, HALF])

        loaded = sem("loaded")
        const_set = sem("const_set")
        identx_ready = sem("identx_ready")
        xpre_in = sem("xpre_in")
        xres_in = sem("xres_in")
        stats1 = sem("stats1")
        pool_step = sem("pool_step")
        comb_ready = sem("comb_ready")
        xn_ready = sem("xn_ready")
        xn_transposed = sem("xn_transposed")
        xnT_ready = sem("xnT_ready")
        v_done = sem("v_done")
        v_evac = sem("v_evac")
        qk_done = sem("qk_done")
        rope_done = sem("rope_done")
        add_done = sem("add_done")
        round_done = sem("round_done")
        s_done = sem("s_done")
        max_done = sem("max_done")
        st_done = sem("st_done")
        exp_done = sem("exp_done")
        av_done = sem("av_done")
        lnden_done = sem("lnden_done")
        rden_done = sem("rden_done")
        norm_done = sem("norm_done")
        y_done = sem("y_done")
        yT_ready = sem("yT_ready")
        y_back = sem("y_back")
        stats2 = sem("stats2")
        x_stat = sem("x_stat")
        y_stat = sem("y_stat")
        rstd2_ready = sem("rstd2_ready")
        ynorm_done = sem("ynorm_done")
        x1_ready = sem("x1_ready")
        NCONST = 6
        NLOADS = 6

        LAG_MAX, LAG_EXP, LAG_VAL = 1, 2, 3
        OUT_STEP, BACK_STEP, V_STEP = 3, 4, 5
        V_EACH = -(-NV // (PAIRS - V_STEP))

        uses = []
        for s in range(PAIRS):
            uses += [("qk", s, c) for c in range(4)]
            if s >= V_STEP:
                uses += [("v", s, n) for n in range(V_EACH * (s - V_STEP), min(NV, V_EACH * (s - V_STEP + 1)))]

        def program(engine, step):
            many = 10 * PAIRS
            for r in range(2 * PAIRS):
                step(r // PAIRS, r // PAIRS, r % PAIRS, r, many)
            with engine.Fori(1, NB // 2 - 1) as i:
                for r in range(2 * PAIRS):
                    step(2 * i + r // PAIRS, r // PAIRS, r % PAIRS, many, many)
            for r in range(2 * PAIRS + BACK_STEP + 1):
                step(NB - 2 + r // PAIRS, r // PAIRS % 2, r % PAIRS, many, 2 * PAIRS - r)

        def alive(lag, before, left):
            return before >= lag and left + lag > 0

        block = ctx.enter_context(nc.Block())

        @block.sync
        def _(sp):
            sp.dma_start(xpre[:], x_v[0]).then_inc(xpre_in, 16)
            sp.dma_start(ident[:], ident_in).then_inc(loaded, 16)
            sp.dma_start(w_sb[:], w_l0).then_inc(loaded, 16)
            sp.dma_start(rope[:], rope_l0).then_inc(loaded, 16)
            sp.dma_start(mq[:], masks_q).then_inc(loaded, 16)
            sp.dma_start(mk[:], masks_k).then_inc(loaded, 16)
            sp.dma_start(wo_sb[:], wo_l0.rearrange("(k p) c -> p k c", p=128)).then_inc(loaded, 16)
            sp.wait_ge(xn_ready, 1)
            sp.dma_start(xpre[:], x_v[1]).then_inc(xpre_in, 16)
            sp.dma_start(xres[:], x_v[0]).then_inc(xres_in, 16)

            with sp.Fori(1, NB - 1) as i:
                sp.wait_ge(xn_ready, i + 1)
                sp.dma_start(xpre[:], x_v[i + 1]).then_inc(xpre_in, 16)
                sp.wait_ge(x1_ready, i)
                sp.dma_start(xres[:], x_v[i]).then_inc(xres_in, 16)
            sp.wait_ge(x1_ready, NB - 1)
            sp.dma_start(xres[:], x_v[NB - 1]).then_inc(xres_in, 16)

        @block.gpsimd
        def _(pool):
            nc.gpsimd.memset(neg_half[:], -0.5).then_inc(const_set, 1)
            nc.gpsimd.memset(eps5[:], 1e-5).then_inc(const_set, 1)
            nc.gpsimd.memset(eps6[:], 1e-6).then_inc(const_set, 1)
            nc.gpsimd.memset(ones[:], 1.0).then_inc(const_set, 1)
            for k in range(2):
                nc.gpsimd.memset(kB[k][:, 0:WIN], 0.0).then_inc(const_set, 1)

            def factors(b):
                n = 6 * b
                pool.wait_ge(stats1, b + 1)
                nc.gpsimd.tensor_tensor(ve[:], mv1[:, :, 1], eps5[:], ALU.add).then_inc(pool_step, 1)
                pool.wait_ge(pool_step, n + 1)
                nc.gpsimd.tensor_tensor(rstd[:], ve[:], neg_half[:], ALU.pow).then_inc(pool_step, 1)
                pool.wait_ge(pool_step, n + 2)
                nc.gpsimd.tensor_tensor(ms[:], rstd[:], rstd[:], ALU.mult).then_inc(pool_step, 1)
                pool.wait_ge(pool_step, n + 3)
                nc.gpsimd.tensor_tensor(ms2[:], ms[:], mv1[:, :, 1], ALU.mult).then_inc(pool_step, 1)
                pool.wait_ge(pool_step, n + 4)
                nc.gpsimd.tensor_tensor(ms[:], ms2[:], eps6[:], ALU.add).then_inc(pool_step, 1)
                pool.wait_ge(pool_step, n + 5)
                nc.gpsimd.tensor_tensor(rr[:], ms[:], neg_half[:], ALU.pow).then_inc(pool_step, 1)
                pool.wait_ge(pool_step, n + 6)
                nc.gpsimd.tensor_tensor(comb[:], rr[:], rstd[:], ALU.mult).then_inc(comb_ready, 1)

            pool.wait_ge(const_set, NCONST)
            factors(0)

            def step(b, k, s, before, left):
                n = PAIRS * b + s
                if alive(0, before, left):
                    for side, dst in ((0, qT[s % 4][:]), (1, kT[s % 4][:])):
                        pool.wait_ge(rope_done, 4 * n + 2 * side + 2)
                        if before >= 4 and side == 0:
                            pool.wait_ge(st_done, 4 * (n - 3))
                        nc.gpsimd.tensor_tensor(dst, prod[s % 2][:, 2 * side, :], prod[s % 2][:, 2 * side + 1, :],
                                                ALU.add).then_inc(add_done, 1)
                if s == 1 and left > PAIRS:
                    factors(b + 1)
                if s == BACK_STEP and before >= PAIRS:
                    pool.wait_ge(stats2, b)
                    nc.gpsimd.tensor_tensor(rstd2[:], ve2[:], neg_half[:], ALU.pow).then_inc(rstd2_ready, 1)

            program(pool, step)

        @block.scalar
        def _(act):
            act.wait_ge(loaded, 16 * NLOADS)
            nc.scalar.copy(identx[:, 0:WIN], ident[:, 0:WIN])
            nc.scalar.copy(identx[:, WIN:BAND], ident[:]).then_inc(identx_ready, 1)

            def turned(b, k):
                act.wait_ge(xn_transposed, b + 1)
                nc.scalar.copy(xnT[k][:], o_ps[:, 0:T]).then_inc(xnT_ready, 1)

            def v_copy(b, k, n, bank):
                t, half = divmod(n, VH // HALF)
                act.wait_ge(v_done, NV * b + n + 1)
                nc.scalar.copy(v_sb[k][:, t, half * HALF:(half + 1) * HALF], proj[bank][:]).then_inc(v_evac, 1)

            turned(0, 0)
            for n in range(NV):
                v_copy(0, 0, n, n % 2)

            def exponentials(m, s, h, av_before):
                for g in range(2):
                    if av_before and h == 0 and g == 0:
                        act.wait_ge(av_done, m - 1)
                    cols = slice(BAND * GT * g, min(BAND * GT * (g + 1), PW))
                    act.wait_ge(st_done, 4 * m + 2 * h + g + 1)
                    nc.scalar.activation(pT[s % 2][h][:, cols], t_ps[g][:, 0:cols.stop - cols.start],
                                         ACT.Exp).then_inc(exp_done, 1)

            def step(b, k, s, before, left):
                n = PAIRS * b + s
                m = n - LAG_EXP
                if s == BACK_STEP and left > PAIRS:
                    turned(b + 1, 1 - k)
                if s == OUT_STEP and before >= PAIRS:
                    act.wait_ge(y_done, b)
                    nc.scalar.copy(yT[:], o_ps[:, 0:T]).then_inc(yT_ready, 1)
                if alive(0, before, left):
                    if before >= 2:
                        act.wait_ge(s_done, 4 * (n - 1))
                    act.wait_ge(add_done, 2 * n + 1)
                    nc.scalar.copy(qB[s % 2][:], qT[s % 4][:]).then_inc(round_done, 1)
                if alive(LAG_EXP, before, left):
                    exponentials(m, s, 0, before >= LAG_EXP + 2)
                if alive(LAG_VAL, before, left):
                    v = n - LAG_VAL
                    act.wait_ge(av_done, v + 1)
                    nc.scalar.activation(lnden[:], d_ps[:, 0:T], ACT.Ln).then_inc(lnden_done, 1)
                    act.wait_ge(lnden_done, v + 1)
                    nc.scalar.activation(rden[:], lnden[:], ACT.Exp, scale=-1.0).then_inc(rden_done, 1)
                if alive(0, before, left):
                    act.wait_ge(add_done, 2 * n + 2)
                    nc.scalar.copy(kB[s % 2][:, WIN:WIN + T], kT[s % 4][:]).then_inc(round_done, 1)
                    if left > PAIRS:
                        for u, (what, at, i) in enumerate(uses):
                            if (what, at) == ("v", s):
                                v_copy(b + 1, 1 - k, i, u % 2)
                if alive(LAG_EXP, before, left):
                    exponentials(m, s, 1, False)

            program(act, step)

        @block.vector
        def _(dve):
            def statistics(b):
                dve.wait_ge(xpre_in, 16 * (b + 1))
                for t in range(NT):
                    ins = nc.vector.bn_stats(st1[:, t, :], xpre[:, t, :])
                ins.then_inc(x_stat, 1)
                dve.wait_ge(x_stat, b + 1)
                nc.vector.memset(mark[:], 0.0)
                for t in range(NT):
                    ins = nc.vector.bn_aggr(mv1[:, t, :], st1[:, t, :])
                ins.then_inc(stats1, 1)

            def normalised(b):
                dve.wait_ge(comb_ready, b + 1)
                for t in range(NT):
                    ins = nc.vector.tensor_scalar(xn[:, t, :], xpre[:, t, :], mv1[:, t, 0:1], comb[:, t:t + 1],
                                                  ALU.subtract, ALU.mult)
                ins.then_inc(xn_ready, 1)

            statistics(0)
            normalised(0)
            dve.wait_ge(loaded, 16 * NLOADS)

            def output_statistics(b):
                dve.wait_ge(y_back, b + 1)
                for t in range(NT):
                    ins = nc.vector.bn_stats(st2[:, t, :], d_ps[:, t * 128:(t + 1) * 128])
                ins.then_inc(y_stat, 1)
                dve.wait_ge(y_stat, b + 1)
                nc.vector.memset(mark[:], 0.0)
                for t in range(NT):
                    ins = nc.vector.bn_aggr(mv2[:, t, :], st2[:, t, :])
                ins.then_inc(ynorm_done, 1)
                dve.wait_ge(ynorm_done, 3 * b + 1)
                nc.vector.tensor_scalar(ve2[:], mv2[:, :, 1], 1e-5, None, ALU.add).then_inc(stats2, 1)

            def output(b):
                dve.wait_ge(rstd2_ready, b + 1)
                for t in range(NT):
                    ins = nc.vector.tensor_scalar(ynorm[:, t, :], d_ps[:, t * 128:(t + 1) * 128], mv2[:, t, 0:1],
                                                  rstd2[:, t:t + 1], ALU.subtract, ALU.mult)
                ins.then_inc(ynorm_done, 2)
                dve.wait_ge(ynorm_done, 3 * b + 3)
                dve.wait_ge(xres_in, 16 * (b + 1))
                nc.vector.tensor_tensor(x1[:, bass.ds(NT * b, NT), :], ynorm[:], xres[:], ALU.add).then_inc(x1_ready, 1)

            def step(b, k, s, before, left):
                n = PAIRS * b + s

                def rope_product(c):
                    if not alive(0, before, left):
                        return
                    dve.wait_ge(qk_done, 4 * n + c + 1)
                    if before >= 2 and c % 2 == 0:
                        dve.wait_ge(add_done, 2 * (n - 2) + c // 2 + 1)
                    bank = uses.index(("qk", s, c)) % 2
                    nc.vector.tensor_tensor(prod[s % 2][:, c, :], proj[bank][:, 0:T], rope[:, c, :],
                                            ALU.mult).then_inc(rope_done, 1)

                def maxima(h):
                    if not alive(LAG_MAX, before, left):
                        return
                    m = n - LAG_MAX
                    for g in range(2):
                        if before >= LAG_MAX + 2 and h == 0 and g == 0:
                            dve.wait_ge(st_done, 4 * (m - 1))
                        dve.wait_ge(s_done, 4 * m + 2 * h + g + 1)
                        scores = s_ps[g][:, 0:GT * BAND].rearrange("p (j k) -> p j k", k=BAND)
                        nc.vector.reduce_max(nmax[(s - LAG_MAX) % 2][:, h, GT * g:GT * (g + 1)], scores, AX_X,
                                             negate=True).then_inc(max_done, 1)

                rope_product(0)
                if s == BACK_STEP and before >= PAIRS:
                    output_statistics(b - 1)
                maxima(0)
                rope_product(1)
                maxima(1)
                rope_product(2)
                rope_product(3)
                if s == 1 and left > PAIRS:
                    statistics(b + 1)
                if s == OUT_STEP and left > PAIRS:
                    dve.wait_ge(xn_transposed, b + 1)
                    normalised(b + 1)
                if s == BACK_STEP and before >= PAIRS:
                    output(b - 1)
                if alive(LAG_VAL, before, left):
                    m = n - LAG_VAL
                    dve.wait_ge(rden_done, m + 1)
                    nc.vector.tensor_tensor(oT[:, (s - LAG_VAL) % PAIRS, :], o_ps[:, 0:T], rden[:],
                                            ALU.mult).then_inc(norm_done, 1)

            program(dve, step)

        @block.tensor
        def _(pe):
            def transposes(b):
                pe.wait_ge(xn_ready, b + 1)
                for t in range(NT):
                    ins = nc.tensor.transpose(o_ps[:, t * 128:(t + 1) * 128], xn[:, t, :], ident[:])
                ins.then_inc(xn_transposed, 1)

            def value(k, n, bank):
                t, half = divmod(n, VH // HALF)
                nc.tensor.matmul(proj[bank][:], xnT[k][:, 128 * t:128 * (t + 1)],
                                 w_sb[:, 4 * VH + half * HALF:4 * VH + (half + 1) * HALF],
                                 start=True, stop=True).then_inc(v_done, 1)

            def bank_free(b, u, last):
                if u < 2:
                    b, u = b - 1, u + len(uses)
                    last = False
                while last and uses[u - 2][0] == "v":
                    u -= 2
                what, s, m = uses[u - 2]
                if what == "qk":
                    pe.wait_ge(rope_done, 4 * (PAIRS * b + s) + m + 1)
                else:
                    pe.wait_ge(v_evac, NV * (b + 1) + m + 1)

            pe.wait_ge(loaded, 16 * NLOADS)
            pe.wait_ge(const_set, NCONST)
            transposes(0)
            pe.wait_ge(xnT_ready, 1)
            for n in range(NV):
                if n >= 2:
                    pe.wait_ge(v_evac, n - 1)
                value(0, n, n % 2)
            pe.wait_ge(identx_ready, 1)

            def max_scores(m, s, h):
                pe.wait_ge(round_done, 2 * m + 2)
                rows = slice(HD * h, HD * h + HD)
                for g in range(2):
                    use = 4 * m + 2 * h + g
                    if not (isinstance(m, int) and use < 2):
                        pe.wait_ge(max_done, use - 1)
                    nc.tensor.matmul(s_ps[g][:, 0:GT * BAND], identx[:, WIN:BAND],
                                     mq[:, GT * BAND * g:GT * BAND * (g + 1)], start=True, stop=False)
                    for i in range(GT):
                        t = GT * g + i
                        ins = nc.tensor.matmul(s_ps[g][:, BAND * i:BAND * (i + 1)],
                                               qB[s % 2][rows, 128 * t:128 * (t + 1)],
                                               kB[s % 2][rows, 128 * t:128 * t + BAND],
                                               start=False, stop=i == GT - 1)
                    ins.then_inc(s_done, 1)

            def shifted_scores(m, s, h):
                rows = slice(HD * h, HD * h + HD)
                pe.wait_ge(max_done, 4 * m + 2 * h + 2)
                for g in range(2):
                    use = 4 * m + 2 * h + g
                    if not (isinstance(m, int) and use < 2):
                        pe.wait_ge(exp_done, use - 1)
                    width = sum(widths[GT * g:GT * (g + 1)])
                    nc.tensor.matmul(t_ps[g][:, 0:width], identx[:, WIN:BAND], mk[:, 0:width], start=True, stop=False)
                    for i in range(GT):
                        t = GT * g + i
                        nc.tensor.matmul(t_ps[g][:, BAND * i:BAND * i + widths[t]],
                                         kT[s % 4][rows, 128 * t:128 * (t + 1)],
                                         qT[s % 4][rows, 128 * t:128 * t + widths[t]], start=False, stop=False)
                    for t in range(GT * g, min(GT * (g + 1) + 1, NT)):
                        first = BAND * (t - GT * g) - (WIN if t > GT * g else 0)
                        last = min(BAND * (t - GT * g) + 128, width)
                        skip = WIN if t == GT * g else 0
                        ins = nc.tensor.matmul(t_ps[g][:, first:last], nmax[s % 2][:, h, t:t + 1].to_broadcast([128, 128]),
                                               identx[:, skip:skip + last - first], start=False,
                                               stop=last == width)
                    ins.then_inc(st_done, 1)

            def weighted_values(m, k, s):
                for t in range(NT):
                    for h in range(2):
                        col = (2 * s + h) * HD
                        nc.tensor.matmul(o_ps[HD * h:HD * h + HD, 128 * t:128 * t + widths[t]],
                                         v_sb[k][:, t, col:col + HD],
                                         pT[s % 2][h][:, BAND * t:BAND * t + widths[t]], start=t == 0,
                                         stop=t == NT - 1, skip_group_check=True)
                for t in range(NT):
                    for h in range(2):
                        ins = nc.tensor.matmul(d_ps[HD * h:HD * h + HD, 128 * t:128 * t + widths[t]], ones[:],
                                               pT[s % 2][h][:, BAND * t:BAND * t + widths[t]], start=t == 0,
                                               stop=t == NT - 1, skip_group_check=True)
                ins.then_inc(av_done, 1)

            def step(b, k, s, before, left):
                n = PAIRS * b + s

                def projections(kind, which=None):
                    for u, (what, at, i) in enumerate(uses):
                        if (what, at) != (kind, s) or which not in (None, i):
                            continue
                        if kind == "qk" and alive(0, before, left):
                            bank_free(b, u, left <= PAIRS)
                            nc.tensor.matmul(proj[u % 2][:, 0:T], w_sb[:, i * VH + s * 128:i * VH + (s + 1) * 128],
                                             xnT[k][:], start=True, stop=True).then_inc(qk_done, 1)
                        if kind == "v" and left > PAIRS:
                            bank_free(b, u, False)
                            value(1 - k, i, u % 2)

                def maxima(h):
                    if alive(LAG_MAX, before, left):
                        max_scores(n - LAG_MAX, (s - LAG_MAX) % PAIRS, h)

                def shifted(h):
                    if alive(LAG_EXP, before, left):
                        shifted_scores(n - LAG_EXP, (s - LAG_EXP) % PAIRS, h)

                if s == BACK_STEP and (before >= PAIRS or left > PAIRS):
                    if alive(LAG_VAL, before - 1, left + 1):
                        pe.wait_ge(norm_done, n - LAG_VAL)
                    if before >= PAIRS:
                        pe.wait_ge(yT_ready, b)
                        for t in range(NT):
                            ins = nc.tensor.transpose(d_ps[:, t * 128:(t + 1) * 128], yT[:, t * 128:(t + 1) * 128],
                                                      ident[:])
                        ins.then_inc(y_back, 1)
                    if left > PAIRS:
                        transposes(b + 1)
                projections("qk", 0)
                maxima(0)
                if s == OUT_STEP and before >= PAIRS:
                    pe.wait_ge(norm_done, PAIRS * b)
                    for p in range(PAIRS):
                        ins = nc.tensor.matmul(o_ps[:, 0:T], wo_sb[:, p, :], oT[:, p, :],
                                               start=p == 0, stop=p == PAIRS - 1)
                    ins.then_inc(y_done, 1)
                projections("qk", 1)
                maxima(1)
                projections("qk", 2)
                shifted(0)
                projections("qk", 3)
                if alive(LAG_VAL, before, left):
                    m = n - LAG_VAL
                    pe.wait_ge(exp_done, 4 * m + 4)
                    if before > LAG_VAL:
                        pe.wait_ge(norm_done, m)
                    if s == OUT_STEP and before >= PAIRS:
                        pe.wait_ge(yT_ready, b)
                    if s == BACK_STEP and before >= PAIRS:
                        pe.wait_ge(ynorm_done, 3 * b)
                    if s == BACK_STEP and left > PAIRS:
                        pe.wait_ge(xnT_ready, b + 2)
                    weighted_values(m, k if s >= LAG_VAL else 1 - k, (s - LAG_VAL) % PAIRS)
                projections("v")
                shifted(1)

            program(pe, step)


def routing(nc, x1, pos, mean, rstd, cent_t, ln_g, ln_b, ident_in, ones_in, before_in, sorted_x):
    _, TILES, C = x1.shape
    E = cent_t.shape[1]
    CAP = TILES * 128 // E
    G4 = 4
    DIGITS = 8
    TIES = 3

    with ExitStack() as ctx:
        def sb(name, shape, dt=F32):
            return ctx.enter_context(nc.sbuf_tensor("b_" + name, shape, dt))

        def ps(name, shape):
            return ctx.enter_context(nc.psum_tensor("b_" + name, shape, F32))

        def sem(name):
            return ctx.enter_context(nc.semaphore("b_" + name))

        cent = sb("cent", [128, E])
        gamma = sb("gamma", [128, 1])
        beta = sb("beta", [128, 1])
        ident = sb("ident", [128, 128])
        ones = sb("ones", [128, 128], BF16)
        before = sb("before", [128, 128], BF16)
        st = sb("st", [128, TILES, 6])
        msum = sb("msum", [128, TILES])
        mdif = sb("mdif", [128, TILES])
        mdd = sb("mdd", [128, TILES])
        m2 = sb("m2", [128, TILES])
        var = sb("var", [128, TILES])
        neg_half = sb("neg_half", [128, TILES])
        eps = sb("eps", [128, TILES])
        ve = sb("ve", [128, TILES])
        r2 = sb("r2", [128, TILES])
        rv = sb("rv", [128, TILES])
        comb = sb("comb", [128, TILES])
        zz = [sb(f"zz{k}", [128, G4, C]) for k in range(2)]
        nT = [sb(f"nT{k}", [128, G4 * 128]) for k in range(2)]
        score = sb("score", [128, E, TILES])
        sign = sb("sign", [128, E, TILES], I32)
        key = sb("key", [128, E, TILES], I32)
        half_i = sb("half_i", [128, E, TILES], I32)
        half_j = sb("half_j", [128, E, TILES], I32)
        hi1 = sb("hi1", [128, E, TILES])
        lo1 = sb("lo1", [128, E, TILES])
        free = sb("free", [128, TILES])
        place = sb("place", [128, TILES])
        a1 = sb("a1", [128, TILES])
        b1 = sb("b1", [128, TILES])
        eq = sb("eq", [128, TILES])
        above = sb("above", [128, TILES])
        above2 = sb("above2", [128, TILES])
        tied = sb("tied", [128, TILES], BF16)
        taken = sb("taken", [128, TILES], BF16)
        run = sb("run", [128, TILES])
        rank = sb("rank", [128, TILES])
        junk = sb("junk", [128, TIES, TILES])
        junk3 = sb("junk3", [128, TIES])
        steps = sb("steps", [128, DIGITS, TIES])
        first = sb("first", [128, TIES])
        base = sb("base", [128, 1])
        thr = [sb(f"thr{k}", [128, 1]) for k in range(2)]
        tries = sb("tries", [128, TIES])
        tries_base = sb("tries_base", [128, TIES])
        count = sb("count", [128, TIES], BF16)
        digit = sb("digit", [128, 1])
        need = [sb(f"need{k}", [128, 1]) for k in range(3)]
        one_col = sb("one_col", [128, TILES])

        tp = [ps(f"tp{k}", [128, 512]) for k in range(2)]
        sp_ps = [ps(f"sp{k}", [128, 512]) for k in range(2)]
        tot = ps("tot", [128, 512])
        pre_ps = ps("pre", [128, 512])
        all_ps = ps("all", [128, 512])

        loaded = sem("loaded")
        stats = sem("stats")
        pool_step = sem("pool_step")
        comb_ready = sem("comb_ready")
        zz_ready = sem("zz_ready")
        zz_turned = sem("zz_turned")
        nT_ready = sem("nT_ready")
        sc_done = sem("sc_done")
        sc_kept = sem("sc_kept")
        chain = sem("chain")
        setup_done = sem("setup_done")
        cnt_ready = sem("cnt_ready")
        tot_ready = sem("tot_ready")
        tied_ready = sem("tied_ready")
        rank_ready = sem("rank_ready")
        pos_ready = sem("pos_ready")
        scattered = sem("scattered")
        NLOADS = 6

        CNT = 2 * DIGITS + 2

        block = ctx.enter_context(nc.Block())

        @block.sync
        def _(sp):
            sp.dma_start(cent[:], cent_t).then_inc(loaded, 16)
            sp.dma_start(gamma[:], ln_g).then_inc(loaded, 16)
            sp.dma_start(beta[:], ln_b).then_inc(loaded, 16)
            sp.dma_start(ident[:], ident_in).then_inc(loaded, 16)
            sp.dma_start(ones[:], ones_in).then_inc(loaded, 16)
            sp.dma_start(before[:], before_in).then_inc(loaded, 16)

        @block.gpsimd
        def _(pool):
            nc.gpsimd.memset(neg_half[:], -0.5).then_inc(pool_step, 1)
            nc.gpsimd.memset(eps[:], 1e-5).then_inc(pool_step, 1)
            pool.wait_ge(pool_step, 2)
            pool.wait_ge(stats, 1)
            nc.gpsimd.tensor_tensor(ve[:], var[:], eps[:], ALU.add).then_inc(pool_step, 1)
            pool.wait_ge(pool_step, 3)
            nc.gpsimd.tensor_tensor(rstd[:], ve[:], neg_half[:], ALU.pow).then_inc(pool_step, 1)
            pool.wait_ge(pool_step, 4)
            nc.gpsimd.tensor_tensor(rv[:], rstd[:], rstd[:], ALU.mult).then_inc(pool_step, 1)
            pool.wait_ge(pool_step, 5)
            nc.gpsimd.tensor_tensor(r2[:], rv[:], var[:], ALU.mult).then_inc(pool_step, 1)
            pool.wait_ge(pool_step, 6)
            nc.gpsimd.tensor_tensor(rv[:], r2[:], eps[:], ALU.add).then_inc(pool_step, 1)
            pool.wait_ge(pool_step, 7)
            nc.gpsimd.tensor_tensor(r2[:], rv[:], neg_half[:], ALU.pow).then_inc(pool_step, 1)
            pool.wait_ge(pool_step, 8)
            nc.gpsimd.tensor_tensor(comb[:], r2[:], rstd[:], ALU.mult).then_inc(comb_ready, 1)

            pool.wait_ge(pos_ready, 1)
            for t in range(TILES):
                pool.indirect_dma_start(out=sorted_x, out_offset=bass.IndirectOffsetOnAxis(ap=pos[:, t:t + 1], axis=0),
                                        in_=x1[:, t, :], in_offset=None).then_inc(scattered, 16)
            pool.wait_ge(scattered, 16 * TILES)

        @block.scalar
        def _(act):
            act.wait_ge(loaded, 16 * NLOADS)
            with act.Fori(0, TILES // G4 // 2) as i:
                for k in range(2):
                    act.wait_ge(zz_turned, 2 * i + k + 1)
                    nc.scalar.activation(nT[k][:], tp[k][:], ACT.Identity, bias=beta[:], scale=gamma[:]).then_inc(nT_ready, 1)

        @block.tensor
        def _(pe):
            pe.wait_ge(loaded, 16 * NLOADS)
            with pe.Fori(0, TILES // G4 // 2) as i:
                for k in range(2):
                    pe.wait_ge(zz_ready, 2 * i + k + 1)
                    for t in range(G4):
                        last = nc.tensor.transpose(tp[k][:, t * 128:(t + 1) * 128], zz[k][:, t, :], ident[:])
                    last.then_inc(zz_turned, 1)
                for k in range(2):
                    pe.wait_ge(nT_ready, 2 * i + k + 1)
                    pe.wait_ge(sc_kept, 2 * i + k + 1)
                    for t in range(G4):
                        last = nc.tensor.matmul(sp_ps[k][:, t * E:(t + 1) * E], nT[k][:, t * 128:(t + 1) * 128], cent[:],
                                                start=True, stop=True)
                    last.then_inc(sc_done, 1)

            def ranks(flags, n):
                pe.wait_ge(tied_ready, n)
                nc.tensor.matmul(pre_ps[:, 0:TILES], before[:], flags[:], start=True, stop=True)
                nc.tensor.matmul(all_ps[:, 0:TILES], ones[:], flags[:], start=True, stop=True).then_inc(rank_ready, 1)

            with pe.Fori(0, E - 1) as e:
                for n in range(CNT):
                    pe.wait_ge(cnt_ready, CNT * e + n + 1)
                    nc.tensor.matmul(tot[:, 0:TIES], ones[:], count[:], start=True, stop=True).then_inc(tot_ready, 1)
                ranks(tied, 2 * e + 1)
                ranks(taken, 2 * e + 2)
            ranks(taken, 2 * (E - 1) + 1)

        @block.vector
        def _(dve):
            with dve.Fori(0, TILES // G4) as i:
                for u in range(G4):
                    nc.vector.bn_stats(st[:, i * G4 + u, :], x1[:, i * G4 + u, :])
            chained = [0]

            def link(ins):
                chained[0] += 1
                ins.then_inc(chain, 1)
                dve.wait_ge(chain, chained[0])

            link(nc.vector.memset(base[:], 0.0))
            nc.vector.tensor_tensor(msum[:], st[:, :, 1], st[:, :, 4], ALU.add)
            nc.vector.tensor_tensor(mdif[:], st[:, :, 1], st[:, :, 4], ALU.subtract)
            link(nc.vector.tensor_tensor(m2[:], st[:, :, 2], st[:, :, 5], ALU.add))
            nc.vector.tensor_scalar(mean[:], msum[:], 0.5, None, ALU.mult)
            link(nc.vector.scalar_tensor_tensor(mdd[:], mdif[:], 0.25, mdif[:], ALU.mult, ALU.mult))
            nc.vector.scalar_tensor_tensor(var[:], m2[:], 1.0 / C, mdd[:], ALU.mult, ALU.add).then_inc(stats, 1)

            nc.vector.memset(free[:], 1.0)
            nc.vector.memset(place[:], 0.0)
            nc.vector.memset(one_col[:], 1.0)
            nc.vector.memset(need[0][:], float(CAP))
            nc.vector.memset(count[:], 0.0)
            for d in range(DIGITS):
                for k in range(TIES):
                    nc.vector.memset(steps[:, d, k:k + 1], float((k + 1) * 4 ** d))
            for k in range(TIES):
                nc.vector.memset(first[:, k:k + 1], float((k + 1) * 4 ** (DIGITS - 1) + 1))
            nc.vector.memset(junk3[:], 0.0).then_inc(sc_kept, 2)

            dve.wait_ge(comb_ready, 1)
            with dve.Fori(0, TILES // G4 // 2) as i:
                for k in range(2):
                    for u in range(G4):
                        t = (2 * i + k) * G4 + u
                        last = nc.vector.tensor_scalar(zz[k][:, u, :], x1[:, t, :], mean[:, bass.ds(t, 1)],
                                                       comb[:, bass.ds(t, 1)], ALU.subtract, ALU.mult)
                    last.then_inc(zz_ready, 1)
                for k in range(2):
                    dve.wait_ge(sc_done, 2 * i + k + 1)
                    nc.vector.tensor_copy(score[:, :, bass.ds((2 * i + k) * G4, G4)],
                                          sp_ps[k][:, 0:G4 * E].rearrange("p (t e) -> p e t", e=E)).then_inc(sc_kept, 1)
            dve.wait_ge(sc_kept, TILES // G4 + 2)
            bits = score[:].bitcast(I32)
            link(nc.vector.tensor_scalar(sign[:], bits, 31, -2 ** 31, ALU.arith_shift_right, ALU.bitwise_or))
            link(nc.vector.tensor_tensor(key[:], bits, sign[:], ALU.bitwise_xor))
            nc.vector.tensor_scalar(half_i[:], key[:], 16, 0xffff, ALU.arith_shift_right, ALU.bitwise_and)
            link(nc.vector.tensor_scalar(half_j[:], key[:], 0xffff, None, ALU.bitwise_and))
            nc.vector.tensor_scalar(hi1[:], half_i[:], 1.0, None, ALU.add)
            link(nc.vector.tensor_scalar(lo1[:], half_j[:], 1.0, None, ALU.add))
            done = chained[0]

            def expert(e, last):
                step = [0]

                def link(ins):
                    step[0] += 1
                    ins.then_inc(chain, 1)
                    dve.wait_ge(chain, PER * e + done + step[0])

                totals = [0]

                def total(ins):
                    totals[0] += 1
                    ins.then_inc(cnt_ready, 1)
                    return lambda: dve.wait_ge(tot_ready, CNT * e + totals[0])

                def search(values, needed, thr):
                    nc.vector.memset(thr[:], 1.0)
                    link(nc.vector.tensor_copy(tries[:], first[:]))
                    for d in reversed(range(DIGITS)):
                        for k in range(TIES):
                            ins = nc.vector.tensor_scalar(junk[:, k, :], values, tries[:, k:k + 1], None, ALU.is_ge,
                                                          ALU.add, accum_out=count[:, k:k + 1])
                        wait_total = total(ins)
                        if d:
                            nc.vector.tensor_scalar(tries_base[:], steps[:, d - 1, :], thr[:], None, ALU.add)
                        wait_total()
                        link(nc.vector.tensor_scalar(junk3[:], tot[:, 0:TIES], needed[:], None, ALU.is_ge,
                                                     ALU.add, accum_out=digit[:]))
                        if d:
                            nc.vector.scalar_tensor_tensor(tries[:], digit[:].to_broadcast([128, TIES]), float(4 ** d),
                                                           tries_base[:], ALU.mult, ALU.add)
                        link(nc.vector.scalar_tensor_tensor(thr[:], digit[:], float(4 ** d), thr[:], ALU.mult, ALU.add))

                def ranked(flags_done, n):
                    flags_done.then_inc(tied_ready, 1)
                    dve.wait_ge(rank_ready, n)
                    link(nc.vector.tensor_tensor_scan(run[:], one_col[:], all_ps[:, 0:TILES], 0.0, ALU.mult, ALU.add))
                    link(nc.vector.tensor_tensor(run[:], run[:], all_ps[:, 0:TILES], ALU.subtract))
                    link(nc.vector.tensor_tensor(rank[:], run[:], pre_ps[:, 0:TILES], ALU.add))

                if last:
                    ins = nc.vector.tensor_copy(taken[:], free[:])
                    ranked(ins, 2 * e + 1)
                else:
                    link(nc.vector.tensor_tensor(a1[:], hi1[:, e, :], free[:], ALU.mult))
                    search(a1[:], need[0], thr[0])
                    total(nc.vector.tensor_scalar(above[:], a1[:], thr[0][:], None, ALU.is_gt, ALU.add,
                                                  accum_out=count[:, 0:1]))()
                    nc.vector.tensor_scalar(eq[:], a1[:], thr[0][:], None, ALU.is_equal)
                    link(nc.vector.tensor_tensor(need[1][:], need[0][:], tot[:, 0:1], ALU.subtract))
                    link(nc.vector.tensor_tensor(b1[:], eq[:], lo1[:, e, :], ALU.mult))
                    search(b1[:], need[1], thr[1])
                    total(nc.vector.tensor_scalar(above2[:], b1[:], thr[1][:], None, ALU.is_gt, ALU.add,
                                                  accum_out=count[:, 0:1]))()
                    nc.vector.tensor_tensor(need[2][:], need[1][:], tot[:, 0:1], ALU.subtract)
                    ins = nc.vector.tensor_scalar(tied[:], b1[:], thr[1][:], None, ALU.is_equal)
                    ranked(ins, 2 * e + 1)
                    link(nc.vector.scalar_tensor_tensor(eq[:], rank[:], need[2][:], tied[:], ALU.is_lt, ALU.mult))
                    link(nc.vector.tensor_tensor(above[:], above[:], above2[:], ALU.add))
                    link(nc.vector.tensor_tensor(eq[:], eq[:], above[:], ALU.add))
                    ins = nc.vector.tensor_copy(taken[:], eq[:])
                    ranked(ins, 2 * e + 2)
                link(nc.vector.scalar_tensor_tensor(run[:], rank[:], base[:], taken[:], ALU.add, ALU.mult))
                nc.vector.tensor_tensor(place[:], place[:], run[:], ALU.add)
                nc.vector.tensor_tensor(free[:], free[:], taken[:], ALU.subtract)
                link(nc.vector.tensor_scalar(base[:], base[:], float(CAP), None, ALU.add))
                assert last or (step[0] == PER and totals[0] == CNT)

            PER = 4 * DIGITS + 16
            with dve.Fori(0, E - 1) as e:
                expert(e, False)
            expert(E - 1, True)
            nc.vector.tensor_copy(pos[:], place[:]).then_inc(pos_ready, 1)


def expert_ffn(nc, sorted_x, w1_d, b1_d, w2_d, b2_d, ln_g, ln_b, ident_in, sorted_out):
    N, C = sorted_x.shape
    E, _, F = w1_d.shape
    CH = 512
    NT = CH // 128
    NF = F // 128
    U = 4
    TURNS = N // CH // U
    assert N // E == 2 * CH
    x_v = sorted_x.rearrange("(n p t) c -> n p t c", p=128, t=NT)
    o_v = sorted_out.rearrange("(n p t) c -> n p t c", p=128, t=NT)

    with ExitStack() as ctx:
        def sb(name, shape, dt=F32):
            return ctx.enter_context(nc.sbuf_tensor("c_" + name + "_", shape, dt))

        def ps(name, shape):
            return ctx.enter_context(nc.psum_tensor("c_" + name + "_", shape, F32))

        def sem(name):
            return ctx.enter_context(nc.semaphore("c_" + name))

        gamma = sb("gamma", [128, 1])
        beta = sb("beta", [128, 1])
        ident = sb("ident", [128, 128])
        w1 = [sb(f"w1_{k}", [128, F]) for k in range(2)]
        w2 = [sb(f"w2_{k}", [128, NF, C]) for k in range(2)]
        b1 = [sb(f"b1_{k}", [128, NF]) for k in range(2)]
        b2 = [sb(f"b2_{k}", [128, 1]) for k in range(2)]
        xs = [sb(f"xs_{k}", [128, NT, C]) for k in range(U)]
        mv = [sb(f"mv_{k}", [128, NT, 2]) for k in range(U)]
        st = [sb(f"st_{k}", [128, NT, 6]) for k in range(2)]
        rstd = [sb(f"rstd_{k}", [128, NT]) for k in range(U)]
        comb = [sb(f"comb_{k}", [128, NT]) for k in range(U)]
        ve = sb("ve", [128, NT])
        va = sb("va", [128, NT])
        vb = sb("vb", [128, NT])
        neg_half = sb("neg_half", [128, NT])
        eps = sb("eps", [128, NT])
        zz = [sb(f"zz_{k}", [128, NT, C]) for k in range(2)]
        z = [sb(f"z_{k}", [128, NT, C]) for k in range(2)]
        hT = [sb(f"hT_{k}", [128, CH]) for k in range(2)]
        gT = sb("gT", [128, NF, CH])
        yT = sb("yT", [128, CH])
        res = sb("res", [128, NT, C])
        resn = sb("resn", [128, NT, C])
        st2 = sb("st2", [128, NT, 6])
        mv2 = sb("mv2", [128, NT, 2])
        ve2 = sb("ve2", [128, NT])
        rstd2 = sb("rstd2", [128, NT])
        mark = sb("mark", [128, 1])

        in_ps = [ps(f"in_{k}", [128, CH]) for k in range(2)]
        h_ps = [ps(f"h_{k}", [128, CH]) for k in range(2)]
        y_ps = [ps(f"y_{k}", [128, CH]) for k in range(2)]
        back_ps = [ps(f"back_{k}", [128, CH]) for k in range(2)]

        loaded = sem("loaded")
        w_in = [sem(f"w_in{k}") for k in range(2)]
        xs_in = [sem(f"xs_in{k}") for k in range(U)]
        const_set = sem("const_set")
        stat_step = sem("stat_step")
        stats = sem("stats")
        pool_step = sem("pool_step")
        comb_ready = sem("comb_ready")
        zz_ready = sem("zz_ready")
        turned = sem("turned")
        hT_ready = sem("hT_ready")
        h_done = sem("h_done")
        gelu_done = sem("gelu_done")
        y_done = sem("y_done")
        yT_ready = sem("yT_ready")
        back_done = sem("back_done")
        post_step = sem("post_step")
        var2_ready = sem("var2_ready")
        rstd2_ready = sem("rstd2_ready")
        x2_ready = sem("x2_ready")
        stored = sem("stored")

        block = ctx.enter_context(nc.Block())

        @block.sync
        def _(sp):
            def weights(e, k):
                sp.dma_start(w1[k][:], w1_d[e]).then_inc(w_in[k], 16)
                sp.dma_start(w2[k][:], w2_d[e].rearrange("(f p) c -> p f c", p=128)).then_inc(w_in[k], 16)
                sp.dma_start(b1[k][:], b1_d[e]).then_inc(w_in[k], 16)
                sp.dma_start(b2[k][:], b2_d[e]).then_inc(w_in[k], 16)

            sp.dma_start(xs[0][:], x_v[0]).then_inc(xs_in[0], 16)
            sp.dma_start(xs[1][:], x_v[1]).then_inc(xs_in[1], 16)
            sp.dma_start(gamma[:], ln_g).then_inc(loaded, 16)
            sp.dma_start(beta[:], ln_b).then_inc(loaded, 16)
            sp.dma_start(ident[:], ident_in).then_inc(loaded, 16)
            weights(0, 0)
            for u in range(2, U):
                sp.dma_start(xs[u][:], x_v[u]).then_inc(xs_in[u], 16)
            weights(1, 1)

            def turn(i, last):
                for u in range(U):
                    c = U * i + u
                    sp.wait_ge(x2_ready, c + 1)
                    sp.dma_start(o_v[c], xs[u][:]).then_inc(stored, 16)
                    if not last:
                        sp.wait_ge(stored, 16 * (c + 1))
                        sp.dma_start(xs[u][:], x_v[c + U]).then_inc(xs_in[u], 16)
                        if u % 2:
                            sp.wait_ge(yT_ready, c + 1)
                            weights(2 * (i + 1) + u // 2, u // 2)

            with sp.Fori(0, TURNS - 1) as i:
                turn(i, False)
            turn(TURNS - 1, True)
            sp.wait_ge(stored, 16 * U * TURNS)

        @block.gpsimd
        def _(pool):
            nc.gpsimd.memset(neg_half[:], -0.5).then_inc(const_set, 1)
            nc.gpsimd.memset(eps[:], 1e-5).then_inc(const_set, 1)
            pool.wait_ge(const_set, 2)

            def factors(c, k):
                def link(ins, n):
                    ins.then_inc(pool_step, 1)
                    pool.wait_ge(pool_step, 6 * c + n)
                pool.wait_ge(stats, c + 1)
                link(nc.gpsimd.tensor_tensor(ve[:], mv[k][:, :, 1], eps[:], ALU.add), 1)
                link(nc.gpsimd.tensor_tensor(rstd[k][:], ve[:], neg_half[:], ALU.pow), 2)
                link(nc.gpsimd.tensor_tensor(va[:], rstd[k][:], rstd[k][:], ALU.mult), 3)
                link(nc.gpsimd.tensor_tensor(vb[:], va[:], mv[k][:, :, 1], ALU.mult), 4)
                link(nc.gpsimd.tensor_tensor(va[:], vb[:], eps[:], ALU.add), 5)
                link(nc.gpsimd.tensor_tensor(vb[:], va[:], neg_half[:], ALU.pow), 6)
                nc.gpsimd.tensor_tensor(comb[k][:], vb[:], rstd[k][:], ALU.mult).then_inc(comb_ready, 1)

            factors(0, 0)
            factors(1, 1)

            def turn(i, last):
                for u in range(U):
                    c = U * i + u
                    if not (last and u >= U - 2):
                        factors(c + 2, (u + 2) % U)
                    pool.wait_ge(var2_ready, c + 1)
                    nc.gpsimd.tensor_tensor(rstd2[:], ve2[:], neg_half[:], ALU.pow).then_inc(rstd2_ready, 1)

            with pool.Fori(0, TURNS - 1) as i:
                turn(i, False)
            turn(TURNS - 1, True)

        @block.scalar
        def _(act):
            def turn_in(c, k):
                act.wait_ge(turned, c + 1)
                nc.scalar.activation(hT[k % 2][:], in_ps[k % 2][:], ACT.Identity, bias=beta[:],
                                     scale=gamma[:]).then_inc(hT_ready, 1)

            act.wait_ge(loaded, 16 * 3)
            turn_in(0, 0)

            def turn(i, last):
                for u in range(U):
                    c = U * i + u
                    w = u // 2
                    if u % 2 == 0:
                        act.wait_ge(w_in[w], 64 * (i + 1))
                    for f in range(NF):
                        act.wait_ge(h_done, NF * c + f + 1)
                        nc.scalar.activation(gT[:, f, :], h_ps[f % 2][:], ACT.Gelu_apprx_tanh,
                                             bias=b1[w][:, f:f + 1]).then_inc(gelu_done, 1)
                    if not (last and u == U - 1):
                        turn_in(c + 1, u + 1)
                    act.wait_ge(y_done, c + 1)
                    nc.scalar.activation(yT[:], y_ps[u % 2][:], ACT.Identity, bias=b2[w][:]).then_inc(yT_ready, 1)

            with act.Fori(0, TURNS - 1) as i:
                turn(i, False)
            turn(TURNS - 1, True)

        @block.vector
        def _(dve):
            def statistics(c, i, k):
                dve.wait_ge(xs_in[k], 16 * (i + 1))
                for t in range(NT):
                    last = nc.vector.bn_stats(st[k % 2][:, t, :], xs[k][:, t, :])
                last.then_inc(stat_step, 1)
                dve.wait_ge(stat_step, c + 1)
                nc.vector.memset(mark[:], 0.0)
                for t in range(NT):
                    last = nc.vector.bn_aggr(mv[k][:, t, :], st[k % 2][:, t, :])
                last.then_inc(stats, 1)

            def normalised(c, k):
                dve.wait_ge(comb_ready, c + 1)
                for t in range(NT):
                    last = nc.vector.tensor_scalar(zz[k % 2][:, t, :], xs[k][:, t, :], mv[k][:, t, 0:1],
                                                   comb[k][:, t:t + 1], ALU.subtract, ALU.mult)
                last.then_inc(zz_ready, 1)
                for t in range(NT):
                    nc.vector.tensor_scalar(z[k % 2][:, t, :], xs[k][:, t, :], mv[k][:, t, 0:1],
                                            rstd[k][:, t:t + 1], ALU.subtract, ALU.mult)

            statistics(0, 0, 0)
            statistics(1, 0, 1)
            normalised(0, 0)

            def turn(i, last):
                for u in range(U):
                    c = U * i + u
                    if not (last and u >= U - 2):
                        statistics(c + 2, i + (u + 2) // U, (u + 2) % U)
                    if not (last and u == U - 1):
                        normalised(c + 1, (u + 1) % U)
                    n = 5 * c

                    def link(ins, k):
                        ins.then_inc(post_step, 1)
                        dve.wait_ge(post_step, n + k)
                    dve.wait_ge(back_done, c + 1)
                    link(nc.vector.tensor_tensor(res[:], z[u % 2][:], back_ps[u % 2][:].rearrange("p (t c) -> p t c", c=C),
                                                 ALU.add), 1)
                    for t in range(NT - 1):
                        nc.vector.bn_stats(st2[:, t, :], res[:, t, :])
                    link(nc.vector.bn_stats(st2[:, NT - 1, :], res[:, NT - 1, :]), 2)
                    nc.vector.memset(mark[:], 0.0)
                    for t in range(NT - 1):
                        nc.vector.bn_aggr(mv2[:, t, :], st2[:, t, :])
                    link(nc.vector.bn_aggr(mv2[:, NT - 1, :], st2[:, NT - 1, :]), 3)
                    nc.vector.tensor_scalar(ve2[:], mv2[:, :, 1], 1e-5, None, ALU.add).then_inc(var2_ready, 1)
                    dve.wait_ge(rstd2_ready, c + 1)
                    for t in range(NT - 1):
                        nc.vector.tensor_scalar(resn[:, t, :], res[:, t, :], mv2[:, t, 0:1], rstd2[:, t:t + 1],
                                                ALU.subtract, ALU.mult)
                    t = NT - 1
                    link(nc.vector.tensor_scalar(resn[:, t, :], res[:, t, :], mv2[:, t, 0:1], rstd2[:, t:t + 1],
                                                 ALU.subtract, ALU.mult), 4)
                    link(nc.vector.tensor_tensor(xs[u][:], resn[:], xs[u][:], ALU.add), 5)
                    nc.vector.memset(mark[:], 0.0).then_inc(x2_ready, 1)

            with dve.Fori(0, TURNS - 1) as i:
                turn(i, False)
            turn(TURNS - 1, True)

        @block.tensor
        def _(pe):
            def turn_in(c, k):
                pe.wait_ge(zz_ready, c + 1)
                for t in range(NT):
                    last = nc.tensor.transpose(in_ps[k % 2][:, t * 128:(t + 1) * 128], zz[k % 2][:, t, :], ident[:])
                last.then_inc(turned, 1)

            pe.wait_ge(loaded, 16 * 3)
            turn_in(0, 0)

            def turn(i, last):
                for u in range(U):
                    c = U * i + u
                    w = u // 2
                    if u % 2 == 0:
                        pe.wait_ge(w_in[w], 64 * (i + 1))
                    pe.wait_ge(hT_ready, c + 1)
                    for f in range(NF):
                        if f >= 2:
                            pe.wait_ge(gelu_done, NF * c + f - 1)
                        nc.tensor.matmul(h_ps[f % 2][:], w1[w][:, f * 128:(f + 1) * 128], hT[u % 2][:],
                                         start=True, stop=True).then_inc(h_done, 1)
                    if not (last and u == U - 1):
                        turn_in(c + 1, u + 1)
                    for f in range(NF):
                        pe.wait_ge(gelu_done, NF * c + f + 1)
                        last_i = nc.tensor.matmul(y_ps[u % 2][:], w2[w][:, f, :], gT[:, f, :],
                                                  start=f == 0, stop=f == NF - 1)
                    last_i.then_inc(y_done, 1)
                    pe.wait_ge(yT_ready, c + 1)
                    for t in range(NT):
                        last_i = nc.tensor.transpose(back_ps[u % 2][:, t * 128:(t + 1) * 128],
                                                     yT[:, t * 128:(t + 1) * 128], ident[:])
                    last_i.then_inc(back_done, 1)

            with pe.Fori(0, TURNS - 1) as i:
                turn(i, False)
            turn(TURNS - 1, True)


def row_statistics(nc, tag, x, mean, rstd):
    _, TILES, C = x.shape
    with ExitStack() as ctx:
        def sb(name, shape, dt=F32):
            return ctx.enter_context(nc.sbuf_tensor(f"{tag}_{name}", shape, dt))

        st = sb("st", [128, TILES, 6])
        msum = sb("msum", [128, TILES])
        mdif = sb("mdif", [128, TILES])
        mdd = sb("mdd", [128, TILES])
        m2 = sb("m2", [128, TILES])
        var = sb("var", [128, TILES])
        neg_half = sb("neg_half", [128, TILES])
        chain = ctx.enter_context(nc.semaphore(tag + "_chain"))
        var_ready = ctx.enter_context(nc.semaphore(tag + "_var_ready"))
        const_set = ctx.enter_context(nc.semaphore(tag + "_const_set"))
        rstd_ready = ctx.enter_context(nc.semaphore(tag + "_rstd_ready"))
        block = ctx.enter_context(nc.Block())

        @block.gpsimd
        def _(pool):
            nc.gpsimd.memset(neg_half[:], -0.5).then_inc(const_set, 1)
            pool.wait_ge(const_set, 1)
            pool.wait_ge(var_ready, 1)
            nc.gpsimd.tensor_tensor(rstd[:], var[:], neg_half[:], ALU.pow).then_inc(rstd_ready, 1)
            pool.wait_ge(rstd_ready, 1)

        @block.vector
        def _(dve):
            with dve.Fori(0, TILES // 4) as i:
                for u in range(4):
                    nc.vector.bn_stats(st[:, i * 4 + u, :], x[:, i * 4 + u, :])
            chained = [0]

            def link(ins):
                chained[0] += 1
                ins.then_inc(chain, 1)
                dve.wait_ge(chain, chained[0])

            link(nc.vector.memset(mdd[:], 0.0))
            nc.vector.tensor_tensor(msum[:], st[:, :, 1], st[:, :, 4], ALU.add)
            nc.vector.tensor_tensor(mdif[:], st[:, :, 1], st[:, :, 4], ALU.subtract)
            link(nc.vector.tensor_tensor(m2[:], st[:, :, 2], st[:, :, 5], ALU.add))
            nc.vector.tensor_scalar(mean[:], msum[:], 0.5, None, ALU.mult)
            link(nc.vector.scalar_tensor_tensor(mdd[:], mdif[:], 0.25, mdif[:], ALU.mult, ALU.mult))
            link(nc.vector.scalar_tensor_tensor(var[:], m2[:], 1.0 / C, mdd[:], ALU.mult, ALU.add))
            nc.vector.tensor_scalar(var[:], var[:], 1e-5, None, ALU.add).then_inc(var_ready, 1)


def l1_attention(nc, x, mean, rstd, wqk_d, wv_d, bqk_d, bv_d, wo_d, bo_d, rope_d, ident_in, parts):
    _, TILES, C = x.shape
    NT = 4
    T = NT * 128
    NB = TILES // NT
    HD = 8
    H = C // HD
    GH = 4
    NG = H // GH
    NP = 3
    ROWS = NP * NP * HD
    HC = 32
    MICRO = GH * NT
    PER_S = NG * MICRO
    M_PRE = 6
    M_BATCH = M_PRE + NG + 2
    qp_d, kp_d = parts

    with ExitStack() as ctx:
        def sb(name, shape, dt=F32):
            return ctx.enter_context(nc.sbuf_tensor("d_" + name + "_", shape, dt))

        def ps(name, shape):
            return ctx.enter_context(nc.psum_tensor("d_" + name + "_", shape, F32))

        def sem(name):
            return ctx.enter_context(nc.semaphore("d_" + name))

        wqk = sb("wqk", [128, 4, C])
        wv = sb("wv", [128, C])
        wo = sb("wo", [128, C])
        bqk = sb("bqk", [128, 4])
        bv = sb("bv", [128, C])
        bo = sb("bo", [128, C])
        rope = sb("rope", [128, 4, T])
        ident = sb("ident", [128, 128])
        identb = sb("identb", [128, 128], BF16)
        zz = sb("zz", [128, NT, C])
        zT = sb("zT", [128, T])
        prod = sb("prod", [128, 4, T])
        whole = [sb(f"whole{k}", [128, T]) for k in range(2)]
        rest = [sb(f"rest{k}", [128, T]) for k in range(2)]
        part = [sb(f"part{k}", [128, NP, T], BF16) for k in range(2)]
        qs = [sb(f"qs{k}", [ROWS, H, T], BF16) for k in range(2)]
        ks = [sb(f"ks{k}", [ROWS, H, T], BF16) for k in range(2)]
        v = [sb(f"v{k}", [128, NT, H, HC]) for k in range(2)]
        nmax = [sb(f"nmax{k}", [128, GH, NT], BF16) for k in range(2)]
        pT = [[sb(f"pT{k}_{h}", [128, T]) for h in range(GH)] for k in range(2)]
        oE = sb("oE", [128, T])
        rden = sb("rden", [128, NT, GH])
        quot = sb("quot", [128, NT, C])
        plus = sb("plus", [128, NT, C])
        att = sb("att", [128, NT, C])
        attT = sb("attT", [128, T])
        yb = sb("yb", [128, NT, C])
        yn = sb("yn", [128, NT, C])
        st2 = sb("st2", [128, NT, 6])
        mv2 = sb("mv2", [128, NT, 2])
        ve2 = sb("ve2", [128, NT])
        rstd2 = sb("rstd2", [128, NT])
        neg_half = sb("neg_half", [128, NT])
        mark = sb("mark", [128, 1])

        s_ps = [ps(f"s{k}", [128, T]) for k in range(2)]
        t_ps = [ps(f"t{k}", [128, T]) for k in range(GH)]
        o_ps = ps("o", [128, T])
        m_ps = ps("m", [128, T])
        m3 = m_ps[:].rearrange("p (t c) -> p t c", c=C)

        loaded = sem("loaded")
        const_set = sem("const_set")
        identb_ready = sem("identb_ready")
        zz_ready = sem("zz_ready")
        m_done = sem("m_done")
        m_free = sem("m_free")
        whole_ready = sem("whole_ready")
        part1 = sem("part1")
        rest_ready = sem("rest_ready")
        part2 = sem("part2")
        part3 = sem("part3")
        parts_out = sem("parts_out")
        stacked = sem("stacked")
        s_done = sem("s_done")
        max_done = sem("max_done")
        st_done = sem("st_done")
        exp_done = sem("exp_done")
        av_done = sem("av_done")
        oe_done = sem("oe_done")
        post_step = sem("post_step")
        var2_step = sem("var2_step")
        var2_ready = sem("var2_ready")
        rstd2_ready = sem("rstd2_ready")
        NLOADS = 8
        NSTACK = NP * NP + NP

        def m_use(b, n):
            return M_PRE + M_BATCH * b + n

        block = ctx.enter_context(nc.Block())

        @block.sync
        def _(sp):
            for dst, src in ((ident, ident_in), (wqk, wqk_d), (bqk, bqk_d), (rope, rope_d), (wv, wv_d),
                             (wo, wo_d), (bv, bv_d.to_broadcast([128, C])), (bo, bo_d.to_broadcast([128, C]))):
                sp.dma_start(dst[:], src).then_inc(loaded, 16)

            def stack(b, k):
                for side, dst in ((0, qp_d), (1, kp_d)):
                    sp.wait_ge(part3, 2 * b + side + 1)
                    sp.dma_start(dst[k].rearrange("n p t -> p n t"), part[side][:]).then_inc(parts_out, 16)
                sp.wait_ge(parts_out, 32 * (b + 1))
                for a in range(NP):
                    for c in range(NP):
                        r = (NP * a + c) * HD
                        sp.dma_start(qs[k][r:r + HD, :, :],
                                     qp_d[k, a].rearrange("(d h) t -> d h t", h=H)).then_inc(stacked, 16)
                    sp.dma_start(ks[k][NP * HD * a:NP * HD * (a + 1), :, :],
                                 kp_d[k].rearrange("n (d h) t -> (n d) h t", h=H)).then_inc(stacked, 16)

            stack(0, 0)

            def batch(b, k, last):
                if not last:
                    stack(b + 1, 1 - k)

            with sp.Fori(0, NB // 2 - 1) as i:
                for k in range(2):
                    batch(2 * i + k, k, False)
            batch(NB - 2, 0, False)

        @block.gpsimd
        def _(pool):
            nc.gpsimd.memset(neg_half[:], -0.5).then_inc(const_set, 1)
            for k in range(2):
                nc.gpsimd.memset(v[k][:], 0.0).then_inc(const_set, 1)
            pool.wait_ge(const_set, 3)
            for k in range(2):
                nc.gpsimd.memset(v[k][:, :, :, HD:HD + 1], 1.0).then_inc(const_set, 1)

            def wholes(b, use):
                for side in range(2):
                    pool.wait_ge(m_free, use + 2 * side + 2)
                    nc.gpsimd.tensor_tensor(whole[side][:], prod[:, 2 * side, :], prod[:, 2 * side + 1, :],
                                            ALU.add).then_inc(whole_ready, 1)

            wholes(0, 1)

            def batch(b, k, last):
                if not last:
                    wholes(b + 1, m_use(b, 1))
                pool.wait_ge(var2_ready, b + 1)
                nc.gpsimd.tensor_tensor(rstd2[:], ve2[:], neg_half[:], ALU.pow).then_inc(rstd2_ready, 1)

            with pool.Fori(0, NB // 2 - 1) as i:
                for k in range(2):
                    batch(2 * i + k, k, False)
            batch(NB - 2, 0, False)
            batch(NB - 1, 1, True)

        @block.scalar
        def _(act):
            act.wait_ge(loaded, 16 * NLOADS)
            nc.scalar.copy(identb[:], ident[:]).then_inc(identb_ready, 1)

            def turned(use):
                act.wait_ge(m_done, use + 1)
                nc.scalar.copy(zT[:], m_ps[:]).then_inc(m_free, 1)

            def first_part(b, side):
                act.wait_ge(whole_ready, 2 * b + side + 1)
                nc.scalar.copy(part[side][:, 0, :], whole[side][:]).then_inc(part1, 1)

            def second_part(b, side):
                act.wait_ge(rest_ready, 2 * b + side + 1)
                nc.scalar.copy(part[side][:, 1, :], rest[side][:]).then_inc(part2, 1)

            turned(0)
            for side in range(2):
                first_part(0, side)
                second_part(0, side)

            def batch(b, k, last):
                def out_copy(g):
                    act.wait_ge(av_done, NG * NT * b + NT * (g + 1))
                    if g:
                        act.wait_ge(m_done, m_use(b, (0 if last else M_PRE) + g - 1) + 1)
                    nc.scalar.copy(oE[:], o_ps[:]).then_inc(oe_done, 1)

                for g in range(NG):
                    for n in range(MICRO):
                        kt, h = divmod(n, GH)
                        if (g, kt) >= (0, 2) and h == 0:
                            act.wait_ge(av_done, NG * NT * b + NT * g + kt - 1)
                        act.wait_ge(st_done, PER_S * b + MICRO * g + n + 1)
                        nc.scalar.activation(pT[kt % 2][h][:], t_ps[h][:], ACT.Exp).then_inc(exp_done, 1)
                        if g >= 1 and n == 4:
                            out_copy(g - 1)
                        if not last:
                            if (g, n) == (0, 1):
                                turned(m_use(b, 0))
                            if (g, n) == (0, 8):
                                first_part(b + 1, 0)
                            if (g, n) == (0, 10):
                                second_part(b + 1, 0)
                            if (g, n) == (0, 13):
                                first_part(b + 1, 1)
                            if (g, n) == (1, 0):
                                second_part(b + 1, 1)
                out_copy(NG - 1)
                use = m_use(b, (0 if last else M_PRE) + NG)
                act.wait_ge(m_done, use + 1)
                nc.scalar.copy(attT[:], m_ps[:]).then_inc(m_free, 1)

            with act.Fori(0, NB // 2 - 1) as i:
                for k in range(2):
                    batch(2 * i + k, k, False)
            batch(NB - 2, 0, False)
            batch(NB - 1, 1, True)

        @block.vector
        def _(dve):
            def normalised(b):
                for t in range(NT):
                    n = NT * b + t
                    last = nc.vector.tensor_scalar(zz[:, t, :], x[:, n, :], mean[:, bass.ds(n, 1)],
                                                   rstd[:, bass.ds(n, 1)], ALU.subtract, ALU.mult)
                last.then_inc(zz_ready, 1)

            def rotary(b, c, use):
                dve.wait_ge(m_done, use + 1)
                nc.vector.scalar_tensor_tensor(prod[:, c, :], m_ps[:], bqk[:, c:c + 1], rope[:, c, :],
                                               ALU.add, ALU.mult).then_inc(m_free, 1)

            def values(b, k, use):
                dve.wait_ge(m_done, use + 1)
                nc.vector.tensor_tensor(v[k][:, :, :, 0:HD], m_ps[:].rearrange("p (t h d) -> p t h d", t=NT, h=H),
                                        bv[:].rearrange("p (o h d) -> p o h d", o=1, h=H).to_broadcast([128, NT, H, HD]),
                                        ALU.add).then_inc(m_free, 1)

            def remainder(b, side):
                dve.wait_ge(part1, 2 * b + side + 1)
                nc.vector.tensor_tensor(rest[side][:], whole[side][:], part[side][:, 0, :],
                                        ALU.subtract).then_inc(rest_ready, 1)

            def third_part(b, side):
                dve.wait_ge(part2, 2 * b + side + 1)
                nc.vector.tensor_tensor(part[side][:, 2, :], rest[side][:], part[side][:, 1, :],
                                        ALU.subtract).then_inc(part3, 1)

            def maximum(step, g, n):
                h, qt = divmod(n, NT)
                dve.wait_ge(s_done, step + 1)
                nc.vector.reduce_max(nmax[g % 2][:, h, qt:qt + 1], s_ps[n % 2][:], AX_X, negate=True).then_inc(max_done, 1)

            dve.wait_ge(loaded, 16 * NLOADS)
            normalised(0)
            for c in range(4):
                rotary(0, c, 1 + c)
            dve.wait_ge(const_set, 5)
            values(0, 0, 5)
            for side in range(2):
                remainder(0, side)
                third_part(0, side)
            for n in range(MICRO):
                maximum(n, 0, n)

            def batch(b, k, last):
                pre = 0 if last else M_PRE

                def quotients(g):
                    use = m_use(b, pre + g)
                    dve.wait_ge(m_done, use + 1)
                    got = m_ps[:].rearrange("p (t h c) -> p t h c", t=NT, c=HC)
                    cols = slice(g * GH * HD, (g + 1) * GH * HD)
                    nc.vector.reciprocal(rden[:], got[:, :, :, HD]).then_inc(post_step, 1)
                    dve.wait_ge(post_step, 13 * b + 3 * g + 1)
                    nc.vector.tensor_tensor(quot[:, :, cols].rearrange("p t (h d) -> p t h d", d=HD), got[:, :, :, 0:HD],
                                            rden[:].rearrange("p t (h o) -> p t h o", o=1).to_broadcast([128, NT, GH, HD]),
                                            ALU.mult).then_inc(m_free, 1)
                    dve.wait_ge(m_free, use + 1)
                    nc.vector.tensor_scalar(plus[:, :, cols], quot[:, :, cols], 0.0, None, ALU.max).then_inc(post_step, 1)
                    dve.wait_ge(post_step, 13 * b + 3 * g + 2)
                    nc.vector.scalar_tensor_tensor(att[:, :, cols], quot[:, :, cols], 0.0, plus[:, :, cols],
                                                   ALU.min, ALU.add).then_inc(post_step, 1)

                if not last:
                    normalised(b + 1)
                for g in range(NG):
                    for n in range(MICRO):
                        if not (last and g == NG - 1):
                            maximum(PER_S * b + MICRO * (g + 1) + n, g + 1, n)
                        if g >= 1 and n == 9:
                            quotients(g - 1)
                        if not last:
                            if (g, n) in ((0, 4), (0, 6), (0, 8), (0, 10)):
                                c = n // 2 - 2
                                rotary(b + 1, c, m_use(b, 1 + c))
                            if (g, n) == (0, 13):
                                values(b + 1, 1 - k, m_use(b, 5))
                            if (g, n) == (0, 9):
                                remainder(b + 1, 0)
                            if (g, n) == (0, 11):
                                third_part(b + 1, 0)
                            if (g, n) == (0, 14):
                                remainder(b + 1, 1)
                            if (g, n) == (1, 2):
                                third_part(b + 1, 1)
                quotients(NG - 1)
                use = m_use(b, pre + NG + 1)
                dve.wait_ge(m_done, use + 1)
                nc.vector.tensor_tensor(yb[:], m3, bo[:].rearrange("p (o c) -> p o c", o=1).to_broadcast([128, NT, C]),
                                        ALU.add).then_inc(m_free, 1)
                dve.wait_ge(m_free, use + 1)
                for t in range(NT):
                    ins = nc.vector.bn_stats(st2[:, t, :], yb[:, t, :])
                ins.then_inc(var2_step, 1)
                dve.wait_ge(var2_step, 2 * b + 1)
                nc.vector.memset(mark[:], 0.0)
                for t in range(NT):
                    ins = nc.vector.bn_aggr(mv2[:, t, :], st2[:, t, :])
                ins.then_inc(var2_step, 1)
                dve.wait_ge(var2_step, 2 * b + 2)
                nc.vector.tensor_scalar(ve2[:], mv2[:, :, 1], 1e-5, None, ALU.add).then_inc(var2_ready, 1)
                dve.wait_ge(rstd2_ready, b + 1)
                for t in range(NT):
                    ins = nc.vector.tensor_scalar(yn[:, t, :], yb[:, t, :], mv2[:, t, 0:1], rstd2[:, t:t + 1],
                                                  ALU.subtract, ALU.mult)
                ins.then_inc(post_step, 1)
                dve.wait_ge(post_step, 13 * b + 13)
                rows = x[:, bass.ds(NT * b, NT), :]
                nc.vector.tensor_tensor(rows, yn[:], rows, ALU.add)

            with dve.Fori(0, NB // 2 - 1) as i:
                for k in range(2):
                    batch(2 * i + k, k, False)
            batch(NB - 2, 0, False)
            batch(NB - 1, 1, True)

        @block.tensor
        def _(pe):
            def m_ready(use):
                if not (isinstance(use, int) and use == 0):
                    pe.wait_ge(m_free, use)

            def turn_in(b, use):
                pe.wait_ge(zz_ready, b + 1)
                m_ready(use)
                for t in range(NT):
                    ins = nc.tensor.transpose(m_ps[:, t * 128:(t + 1) * 128], zz[:, t, :], ident[:])
                ins.then_inc(m_done, 1)

            def project(c, use):
                m_ready(use)
                nc.tensor.matmul(m_ps[:], wqk[:, c, :], zT[:], start=True, stop=True).then_inc(m_done, 1)

            def project_v(use):
                m_ready(use)
                for t in range(NT):
                    ins = nc.tensor.matmul(m_ps[:, t * C:(t + 1) * C], zT[:, t * 128:(t + 1) * 128], wv[:],
                                           start=True, stop=True)
                ins.then_inc(m_done, 1)

            def scores(step, k, g, n):
                h, qt = divmod(n, NT)
                h += g * GH
                if not (isinstance(step, int) and step < 2):
                    pe.wait_ge(max_done, step - 1)
                nc.tensor.matmul(s_ps[n % 2][:], qs[k][:, h, qt * 128:(qt + 1) * 128], ks[k][:, h, :],
                                 start=True, stop=True).then_inc(s_done, 1)

            pe.wait_ge(loaded, 16 * NLOADS)
            turn_in(0, 0)
            for c in range(4):
                project(c, 1 + c)
            project_v(5)
            pe.wait_ge(identb_ready, 1)
            pe.wait_ge(stacked, 16 * NSTACK)
            for n in range(MICRO):
                scores(n, 0, 0, n)

            def batch(b, k, last):
                pre = 0 if last else M_PRE

                def shifted(g, n):
                    kt, h = divmod(n, GH)
                    if (g, kt) >= (0, 1):
                        pe.wait_ge(exp_done, PER_S * b + MICRO * g + n - GH + 1)
                    if n == 0:
                        pe.wait_ge(max_done, PER_S * b + MICRO * (g + 1))
                    hh = g * GH + h
                    nc.tensor.matmul(t_ps[h][:], ks[k][:, hh, kt * 128:(kt + 1) * 128], qs[k][:, hh, :],
                                     start=True, stop=False)
                    for qt in range(NT):
                        ins = nc.tensor.matmul(t_ps[h][:, qt * 128:(qt + 1) * 128],
                                               nmax[g % 2][:, h, qt:qt + 1].to_broadcast([128, 128]), identb[:],
                                               start=False, stop=qt == NT - 1)
                    ins.then_inc(st_done, 1)

                def weighted(g, kt):
                    pe.wait_ge(exp_done, PER_S * b + MICRO * g + GH * (kt + 1))
                    if kt == 0 and g:
                        pe.wait_ge(oe_done, NG * b + g)
                    for h in range(GH):
                        ins = nc.tensor.matmul(o_ps[HC * h:HC * (h + 1), :], v[k][:, kt, g * GH + h, :], pT[kt % 2][h][:],
                                               start=kt == 0, stop=kt == NT - 1)
                    ins.then_inc(av_done, 1)

                def turn_out(g):
                    use = m_use(b, pre + g)
                    m_ready(use)
                    pe.wait_ge(oe_done, NG * b + g + 1)
                    for t in range(NT):
                        ins = nc.tensor.transpose(m_ps[:, t * 128:(t + 1) * 128], oE[:, t * 128:(t + 1) * 128], ident[:])
                    ins.then_inc(m_done, 1)

                for g in range(NG):
                    for n in range(MICRO):
                        if g < NG - 1:
                            scores(PER_S * b + MICRO * (g + 1) + n, k, g + 1, n)
                        elif not last:
                            if n == 0:
                                pe.wait_ge(stacked, 16 * NSTACK * (b + 2))
                            scores(PER_S * b + MICRO * (g + 1) + n, 1 - k, 0, n)
                        shifted(g, n)
                        if n % GH == GH - 1 and n > GH:
                            weighted(g, n // GH - 1)
                        if g and n == GH - 1:
                            weighted(g - 1, NT - 1)
                        if g and n == 9:
                            turn_out(g - 1)
                        if g == 0 and not last:
                            if n == 1:
                                turn_in(b + 1, m_use(b, 0))
                            if n in (4, 6, 8, 10):
                                project(n // 2 - 2, m_use(b, n // 2 - 1))
                            if n == 13:
                                project_v(m_use(b, 5))
                weighted(NG - 1, NT - 1)
                turn_out(NG - 1)
                use = m_use(b, pre + NG)
                m_ready(use)
                pe.wait_ge(post_step, 13 * b + 12)
                for t in range(NT):
                    ins = nc.tensor.transpose(m_ps[:, t * 128:(t + 1) * 128], att[:, t, :], ident[:])
                ins.then_inc(m_done, 1)
                m_ready(use + 1)
                for t in range(NT):
                    ins = nc.tensor.matmul(m_ps[:, t * C:(t + 1) * C], attT[:, t * 128:(t + 1) * 128], wo[:],
                                           start=True, stop=True)
                ins.then_inc(m_done, 1)

            with pe.Fori(0, NB // 2 - 1) as i:
                for k in range(2):
                    batch(2 * i + k, k, False)
            batch(NB - 2, 0, False)
            batch(NB - 1, 1, True)


def l1_ffn(nc, x, mean, rstd, w1_d, b1_d, phase_d, real_d, imag_d, w2_d, b2_d, ident_in, out):
    _, TILES, C = x.shape
    NT = 4
    CH = NT * 128
    NCH = TILES // NT
    F = w1_d.shape[1]
    NF = F // 128
    U = 2
    TURNS = NCH // U
    INV = 1.0 / (2 * np.pi)
    MAGIC = 1.5 * 2.0 ** 23
    P1 = 6.28125
    P2 = float(np.float32(int((2 * np.pi - P1) * 2 ** 21) / 2 ** 21))
    P3 = float(np.float32(2 * np.pi - P1 - P2))
    TURN = 6.283185
    out_v = out.rearrange("(n t p) c -> n p t c", p=128, t=NT)

    with ExitStack() as ctx:
        def sb(name, shape, dt=F32):
            return ctx.enter_context(nc.sbuf_tensor("e_" + name + "_", shape, dt))

        def ps(name, shape):
            return ctx.enter_context(nc.psum_tensor("e_" + name + "_", shape, F32))

        def sem(name):
            return ctx.enter_context(nc.semaphore("e_" + name))

        w1 = sb("w1", [128, F])
        w2 = sb("w2", [128, NF, C])
        b1 = sb("b1", [128, NF])
        b2 = sb("b2", [128, 1])
        phase = sb("phase", [128, NF])
        real = sb("real", [128, NF])
        imag = sb("imag", [128, NF])
        ident = sb("ident", [128, 128])
        kk = sb("kk", [128, NF])
        red = [sb(f"red{k}", [128, NF]) for k in range(2)]
        theta = sb("theta", [128, NF])
        quarter = sb("quarter", [128, NF])
        whole = sb("whole", [128, NF])
        cosine = sb("cosine", [128, NF])
        sine = sb("sine", [128, NF])
        qa = sb("qa", [128, NF])
        qb = sb("qb", [128, NF])
        gain = sb("gain", [128, NF])
        offset = sb("offset", [128, NF])
        zz = [sb(f"zz{k}", [128, NT, C]) for k in range(U)]
        zT = [sb(f"zT{k}", [128, CH]) for k in range(U)]
        turns = [sb(f"turns{k}", [128, CH]) for k in range(2)]
        near = [sb(f"near{k}", [128, CH]) for k in range(2)]
        frac = [sb(f"frac{k}", [128, CH]) for k in range(2)]
        sn = [sb(f"sn{k}", [128, CH]) for k in range(2)]
        pre = [sb(f"pre{k}", [128, CH]) for k in range(2)]
        gT = sb("gT", [128, NF, CH])
        yT = sb("yT", [128, CH])
        yn = sb("yn", [128, NT, C])
        xo = [sb(f"xo{k}", [128, NT, C]) for k in range(U)]
        st2 = sb("st2", [128, NT, 6])
        mv2 = sb("mv2", [128, NT, 2])
        ve2 = sb("ve2", [128, NT])
        rstd2 = sb("rstd2", [128, NT])
        neg_half = sb("neg_half", [128, NT])
        mark = sb("mark", [128, 1])

        in_ps = ps("in", [128, CH])
        h_ps = [ps(f"h{k}", [128, CH]) for k in range(NF)]
        y_ps = ps("y", [128, CH])
        back_ps = ps("back", [128, CH])

        loaded = sem("loaded")
        const_set = sem("const_set")
        chain = sem("chain")
        angles = sem("angles")
        sines = sem("sines")
        factors = sem("factors")
        zz_ready = sem("zz_ready")
        turned = sem("turned")
        zT_ready = sem("zT_ready")
        h_done = sem("h_done")
        turns_ready = sem("turns_ready")
        near_ready = sem("near_ready")
        frac_ready = sem("frac_ready")
        sin_ready = sem("sin_ready")
        pre_ready = sem("pre_ready")
        relu_done = sem("relu_done")
        y_done = sem("y_done")
        yT_ready = sem("yT_ready")
        back_done = sem("back_done")
        post_step = sem("post_step")
        var2_ready = sem("var2_ready")
        rstd2_ready = sem("rstd2_ready")
        x_ready = sem("x_ready")
        stored = sem("stored")
        NLOADS = 8

        block = ctx.enter_context(nc.Block())

        @block.sync
        def _(sp):
            for dst, src in ((ident, ident_in), (w1, w1_d), (phase, phase_d), (b1, b1_d), (real, real_d), (imag, imag_d),
                             (b2, b2_d), (w2, w2_d.rearrange("(f p) c -> p f c", p=128))):
                sp.dma_start(dst[:], src).then_inc(loaded, 16)
            with sp.Fori(0, TURNS) as i:
                for u in range(U):
                    c = U * i + u
                    sp.wait_ge(x_ready, c + 1)
                    sp.dma_start(out_v[c], xo[u][:]).then_inc(stored, 16)
            sp.wait_ge(stored, 16 * NCH + 1)

        @block.gpsimd
        def _(pool):
            nc.gpsimd.memset(neg_half[:], -0.5).then_inc(const_set, 1)
            nc.gpsimd.memset(mark[:], 0.0).then_inc(stored, 1)
            pool.wait_ge(const_set, 1)
            with pool.Fori(0, NCH) as c:
                pool.wait_ge(var2_ready, c + 1)
                nc.gpsimd.tensor_tensor(rstd2[:], ve2[:], neg_half[:], ALU.pow).then_inc(rstd2_ready, 1)

        @block.scalar
        def _(act):
            act.wait_ge(angles, 1)
            nc.scalar.activation(sine[:], theta[:], ACT.Sin, scale=TURN)
            nc.scalar.activation(cosine[:], quarter[:], ACT.Sin, scale=TURN).then_inc(sines, 1)

            def turn_in(c, k):
                act.wait_ge(turned, c + 1)
                nc.scalar.activation(zT[k][:], in_ps[:], ACT.Copy).then_inc(zT_ready, 1)

            turn_in(0, 0)
            act.wait_ge(factors, 1)

            def turn(i, last):
                for u in range(U):
                    c = U * i + u

                    def angle(f):
                        act.wait_ge(h_done, NF * c + f + 1)
                        nc.scalar.activation(turns[f % 2][:], h_ps[f][:], ACT.Identity, bias=offset[:, f:f + 1],
                                             scale=0.1 * INV).then_inc(turns_ready, 1)

                    def sin(f):
                        act.wait_ge(frac_ready, NF * c + f + 1)
                        nc.scalar.activation(sn[f % 2][:], frac[f % 2][:], ACT.Sin, scale=TURN).then_inc(sin_ready, 1)

                    def relu(f):
                        act.wait_ge(pre_ready, NF * c + f + 1)
                        nc.scalar.activation(gT[:, f, :], pre[f % 2][:], ACT.Relu, bias=b1[:, f:f + 1]).then_inc(relu_done, 1)

                    for f in range(NF + 2):
                        if f < NF:
                            angle(f)
                        if 1 <= f <= NF:
                            sin(f - 1)
                        if f >= 2:
                            relu(f - 2)
                        if f == NF and not (last and u == U - 1):
                            turn_in(c + 1, 1 - u)
                    act.wait_ge(y_done, c + 1)
                    nc.scalar.activation(yT[:], y_ps[:], ACT.Identity, bias=b2[:]).then_inc(yT_ready, 1)

            with act.Fori(0, TURNS - 1) as i:
                turn(i, False)
            turn(TURNS - 1, True)

        @block.vector
        def _(dve):
            chained = [0]

            def link(ins):
                chained[0] += 1
                ins.then_inc(chain, 1)
                dve.wait_ge(chain, chained[0])

            def normalised(c, k):
                for t in range(NT):
                    n = NT * c + t
                    ins = nc.vector.tensor_scalar(zz[k][:, t, :], x[:, n, :], mean[:, bass.ds(n, 1)],
                                                  rstd[:, bass.ds(n, 1)], ALU.subtract, ALU.mult)
                ins.then_inc(zz_ready, 1)

            nc.vector.memset(whole[:], 0.0).then_inc(post_step, 1)
            normalised(0, 0)
            dve.wait_ge(loaded, 16 * NLOADS)
            link(nc.vector.tensor_scalar(kk[:], phase[:], INV, MAGIC, ALU.mult, ALU.add))
            link(nc.vector.tensor_scalar(kk[:], kk[:], MAGIC, None, ALU.subtract))
            link(nc.vector.scalar_tensor_tensor(red[0][:], kk[:], -P1, phase[:], ALU.mult, ALU.add))
            link(nc.vector.scalar_tensor_tensor(red[1][:], kk[:], -P2, red[0][:], ALU.mult, ALU.add))
            link(nc.vector.scalar_tensor_tensor(red[0][:], kk[:], -P3, red[1][:], ALU.mult, ALU.add))
            link(nc.vector.tensor_scalar(red[1][:], red[0][:], INV, None, ALU.mult))
            link(nc.vector.tensor_scalar(kk[:], red[1][:], MAGIC, MAGIC, ALU.add, ALU.subtract))
            link(nc.vector.tensor_tensor(theta[:], red[1][:], kk[:], ALU.subtract))
            link(nc.vector.tensor_scalar(quarter[:], theta[:], 0.25, None, ALU.add))
            link(nc.vector.tensor_scalar(whole[:], quarter[:], MAGIC, MAGIC, ALU.add, ALU.subtract))
            nc.vector.tensor_tensor(quarter[:], quarter[:], whole[:], ALU.subtract).then_inc(angles, 1)
            dve.wait_ge(sines, 1)
            nc.vector.tensor_tensor(qa[:], cosine[:], real[:], ALU.mult)
            link(nc.vector.tensor_tensor(qb[:], sine[:], imag[:], ALU.mult))
            link(nc.vector.tensor_tensor(qa[:], qa[:], qb[:], ALU.add))
            link(nc.vector.scalar_tensor_tensor(gain[:], qa[:], 0.1, imag[:], ALU.mult, ALU.mult))
            nc.vector.scalar_tensor_tensor(offset[:], b1[:], 0.1 * INV, theta[:], ALU.mult, ALU.add).then_inc(factors, 1)
            dve.wait_ge(factors, 1)

            def turn(i, last):
                for u in range(U):
                    c = U * i + u
                    if not (last and u == U - 1):
                        normalised(c + 1, 1 - u)

                    def fraction(f):
                        k = f % 2
                        dve.wait_ge(turns_ready, NF * c + f + 1)
                        nc.vector.tensor_scalar(near[k][:], turns[k][:], MAGIC, MAGIC, ALU.add,
                                                ALU.subtract).then_inc(near_ready, 1)
                        dve.wait_ge(near_ready, NF * c + f + 1)
                        nc.vector.tensor_tensor(frac[k][:], turns[k][:], near[k][:], ALU.subtract).then_inc(frac_ready, 1)

                    def combine(f):
                        dve.wait_ge(sin_ready, NF * c + f + 1)
                        nc.vector.scalar_tensor_tensor(pre[f % 2][:], sn[f % 2][:], gain[:, f:f + 1], h_ps[f][:],
                                                       ALU.mult, ALU.add).then_inc(pre_ready, 1)

                    for f in range(NF + 1):
                        if f < NF:
                            fraction(f)
                        if f:
                            combine(f - 1)

                    n = 3 * c
                    dve.wait_ge(back_done, c + 1)
                    for t in range(NT):
                        ins = nc.vector.bn_stats(st2[:, t, :], back_ps[:, t * 128:(t + 1) * 128])
                    ins.then_inc(post_step, 1)
                    dve.wait_ge(post_step, n + 2)
                    nc.vector.memset(kk[:], 0.0)
                    for t in range(NT):
                        ins = nc.vector.bn_aggr(mv2[:, t, :], st2[:, t, :])
                    ins.then_inc(post_step, 1)
                    dve.wait_ge(post_step, n + 3)
                    nc.vector.tensor_scalar(ve2[:], mv2[:, :, 1], 1e-5, None, ALU.add).then_inc(var2_ready, 1)
                    dve.wait_ge(rstd2_ready, c + 1)
                    for t in range(NT):
                        ins = nc.vector.tensor_scalar(yn[:, t, :], back_ps[:, t * 128:(t + 1) * 128], mv2[:, t, 0:1],
                                                      rstd2[:, t:t + 1], ALU.subtract, ALU.mult)
                    ins.then_inc(post_step, 1)
                    dve.wait_ge(post_step, n + 4)
                    dve.wait_ge(stored, 16 * c + 1)
                    nc.vector.tensor_tensor(xo[u][:], yn[:], x[:, bass.ds(NT * c, NT), :], ALU.add).then_inc(x_ready, 1)

            with dve.Fori(0, TURNS - 1) as i:
                turn(i, False)
            turn(TURNS - 1, True)

        @block.tensor
        def _(pe):
            def turn_in(c, k):
                pe.wait_ge(zz_ready, c + 1)
                for t in range(NT):
                    ins = nc.tensor.transpose(in_ps[:, t * 128:(t + 1) * 128], zz[k][:, t, :], ident[:])
                ins.then_inc(turned, 1)

            pe.wait_ge(loaded, 16 * NLOADS)
            turn_in(0, 0)

            def turn(i, last):
                for u in range(U):
                    c = U * i + u
                    pe.wait_ge(zT_ready, c + 1)
                    for f in range(NF):
                        nc.tensor.matmul(h_ps[f][:], w1[:, f * 128:(f + 1) * 128], zT[u][:],
                                         start=True, stop=True).then_inc(h_done, 1)
                    if not (last and u == U - 1):
                        turn_in(c + 1, 1 - u)
                    for f in range(NF):
                        pe.wait_ge(relu_done, NF * c + f + 1)
                        ins = nc.tensor.matmul(y_ps[:], w2[:, f, :], gT[:, f, :], start=f == 0, stop=f == NF - 1)
                    ins.then_inc(y_done, 1)
                    pe.wait_ge(yT_ready, c + 1)
                    pe.wait_ge(post_step, 3 * c + 1)
                    for t in range(NT):
                        ins = nc.tensor.transpose(back_ps[:, t * 128:(t + 1) * 128], yT[:, t * 128:(t + 1) * 128], ident[:])
                    ins.then_inc(back_done, 1)

            with pe.Fori(0, TURNS - 1) as i:
                turn(i, False)
            turn(TURNS - 1, True)


def gather_rows(nc, x, pos, rows):
    _, TILES, _ = x.shape
    with nc.semaphore("g_gathered") as gathered, nc.Block() as block:
        @block.gpsimd
        def _(pool):
            for t in range(TILES):
                pool.indirect_dma_start(out=x[:, t, :], out_offset=None, in_=rows,
                                        in_offset=bass.IndirectOffsetOnAxis(ap=pos[:, t:t + 1], axis=0)).then_inc(gathered, 16)
            pool.wait_ge(gathered, 16 * TILES)


def program(nc, a, out, B, T, C):
    TILES = B * T // 128
    sorted_x = nc.dram_tensor("sorted_x", (B * T, C), F32).ap()
    sorted_x2 = nc.dram_tensor("sorted_x2", (B * T, C), F32).ap()
    q_parts = nc.dram_tensor("q_parts", (2, 3, C, T), BF16).ap()
    k_parts = nc.dram_tensor("k_parts", (2, 3, C, T), BF16).ap()
    with ExitStack() as ctx:
        x = ctx.enter_context(nc.sbuf_tensor("x_tokens", [128, TILES, C], F32))
        pos = ctx.enter_context(nc.sbuf_tensor("pos", [128, TILES], I32))
        mean = ctx.enter_context(nc.sbuf_tensor("mean", [128, TILES], F32))
        rstd = ctx.enter_context(nc.sbuf_tensor("rstd", [128, TILES], F32))
        l0_attention(nc, a["x"], a["l0_w"], a["l0_wo"], a["l0_rope"], a["l0_masks_q"], a["l0_masks_k"], a["ident"], x)
        routing(nc, x, pos, mean, rstd, a["centroids"], a["ln_g"], a["ln_b"], a["ident"], a["ones"], a["before"], sorted_x)
        expert_ffn(nc, sorted_x, a["e_w1"], a["e_b1"], a["e_w2"], a["e_b2"], a["ln_g"], a["ln_b"], a["ident"], sorted_x2)
        gather_rows(nc, x, pos, sorted_x2)
        row_statistics(nc, "r1", x, mean, rstd)
        l1_attention(nc, x, mean, rstd, a["l1_wqk"], a["l1_wv"], a["l1_bqk"], a["l1_bv"], a["l1_wo"], a["l1_bo"],
                     a["l1_rope"], a["ident"], (q_parts, k_parts))
        row_statistics(nc, "r2", x, mean, rstd)
        l1_ffn(nc, x, mean, rstd, a["f_w1"], a["f_b1"], a["f_phase"], a["f_real"], a["f_imag"], a["f_w2"], a["f_b2"],
               a["ident"], out)


def l0_constants(T, head_dim, window):
    half = head_dim // 2
    inv_freq = np.float32(1.0) / np.power(np.float32(10000.0), np.arange(0, head_dim, 2, dtype=np.float32) / np.float32(head_dim))
    freqs = np.outer(np.arange(T, dtype=np.float32), inv_freq.astype(np.float32))
    cos, sin = np.cos(freqs).T, np.sin(freqs).T
    cos2 = np.concatenate([cos, cos] * 2)
    sin2 = np.concatenate([-sin, sin] * 2)
    scale = head_dim ** -0.5
    rope = np.stack([cos2 * scale, sin2 * scale, cos2, sin2], axis=1).astype(np.float32)
    tiles, band = T // 128, 128 + window
    qry = np.arange(128)[:, None, None]
    tile = np.arange(tiles)[None, :, None]
    key = np.arange(band)[None, None, :]
    seen_q = (qry <= key) & (key <= qry + window) & (key + 128 * tile >= window)
    masks_q = np.where(seen_q, 0.0, MASKED).astype(np.float32).reshape(128, tiles * band)
    ahead = np.arange(band)[None, :] - np.arange(128)[:, None]
    seen_k = (ahead >= 0) & (ahead <= window)
    masks_k = np.tile(np.where(seen_k, 0.0, MASKED).astype(np.float32), (1, tiles // 2))
    return np.ascontiguousarray(rope), masks_q, masks_k


def partner(w, head_dim):
    half = head_dim // 2
    n, c = w.shape
    return w.reshape(n // head_dim, 2, half, c)[:, ::-1].reshape(n, c)


def l1_constants(T, heads, head_dim):
    inv_freq = np.float32(1.0) / np.power(np.float32(10000.0), np.arange(0, head_dim, 2, dtype=np.float32) / np.float32(head_dim))
    freqs = np.outer(np.arange(T, dtype=np.float32), inv_freq.astype(np.float32))
    cos, sin = np.cos(freqs).T, np.sin(freqs).T
    cos2 = np.repeat(np.concatenate([cos, cos]), heads, axis=0)
    sin2 = np.repeat(np.concatenate([-sin, sin]), heads, axis=0)
    scale = head_dim ** -0.5
    return np.stack([cos2 * scale, sin2 * scale, cos2, sin2], axis=1).astype(np.float32)


def by_dimension(w, heads, head_dim, swapped):
    w = w.reshape(*w.shape[:-1], heads, head_dim)
    if swapped:
        w = np.roll(w, head_dim // 2, axis=-1)
    return np.swapaxes(w, -1, -2).reshape(*w.shape[:-2], heads * head_dim)


def l1_weights(wqkv, bqkv, heads):
    c = wqkv.shape[0]
    d = c // heads
    q, k, v = (wqkv[:, n * c:(n + 1) * c] for n in range(3))
    bq, bk, bv = (bqkv[n * c:(n + 1) * c] for n in range(3))
    w = np.stack([by_dimension(a, heads, d, s) for a in (q, k) for s in (False, True)], axis=1)
    b = np.stack([by_dimension(a, heads, d, s) for a in (bq, bk) for s in (False, True)], axis=1)
    return w, b, v, bv.reshape(1, c)


def kernel(L0_attn_x, L0_attn_w_qkv, L0_attn_w_out, L0_ffn_centroids, L0_ffn_ln_g, L0_ffn_ln_b, L0_ffn_w1, L0_ffn_b1,
           L0_ffn_w2, L0_ffn_b2, L1_attn_Wqkv, L1_attn_bqkv, L1_attn_Wout, L1_attn_bout, L1_ffn_W1, L1_ffn_b1,
           L1_ffn_quantum_phases, L1_ffn_quantum_weights_real, L1_ffn_quantum_weights_imag, L1_ffn_W2, L1_ffn_b2):
    import ml_dtypes
    import concourse.bacc as _bacc
    from concourse.bass_utils import run_bass_kernel_spmd as _run

    nc = _bacc.Bacc("TRN2", target_bir_lowering=False, num_devices=1)
    arrays, a = {}, {}

    def give(name, array):
        array = np.ascontiguousarray(array)
        arrays[name] = array
        a[name] = nc.dram_tensor(name, array.shape, mybir.dt.from_np(array.dtype), kind="ExternalInput").ap()

    def columns(v):
        return np.asarray(v).reshape(-1, 128).T

    x = np.asarray(L0_attn_x)
    B, T, C = x.shape
    bf = ml_dtypes.bfloat16
    give("x", x)
    give("ident", np.eye(128, dtype=np.float32))
    give("ones", np.ones((128, 128), bf))
    give("before", np.triu(np.ones((128, 128)), 1).astype(bf))
    q, k, v = np.split(np.asarray(L0_attn_w_qkv), 3)
    give("l0_w", np.concatenate([q, partner(q, L0_HEAD), k, partner(k, L0_HEAD), v]).T)
    give("l0_wo", np.asarray(L0_attn_w_out).T)
    rope, masks_q, masks_k = l0_constants(T, L0_HEAD, L0_WINDOW)
    give("l0_rope", rope)
    give("l0_masks_q", masks_q.astype(bf))
    give("l0_masks_k", masks_k.astype(bf))
    E, _, F = np.asarray(L0_ffn_w1).shape
    give("centroids", np.asarray(L0_ffn_centroids).T)
    give("ln_g", columns(L0_ffn_ln_g))
    give("ln_b", columns(L0_ffn_ln_b))
    give("e_w1", np.asarray(L0_ffn_w1))
    give("e_b1", np.asarray(L0_ffn_b1).reshape(E, F // 128, 128).transpose(0, 2, 1))
    give("e_w2", np.asarray(L0_ffn_w2))
    give("e_b2", np.asarray(L0_ffn_b2).reshape(E, C, 1))
    wqk, bqk, wv, bv = l1_weights(np.asarray(L1_attn_Wqkv), np.asarray(L1_attn_bqkv), L1_HEADS)
    give("l1_wqk", wqk)
    give("l1_bqk", bqk)
    give("l1_wv", wv)
    give("l1_bv", bv)
    give("l1_wo", np.asarray(L1_attn_Wout))
    give("l1_bo", np.asarray(L1_attn_bout).reshape(1, C))
    give("l1_rope", l1_constants(T, L1_HEADS, C // L1_HEADS))
    give("f_w1", np.asarray(L1_ffn_W1))
    give("f_b1", columns(L1_ffn_b1))
    give("f_phase", columns(L1_ffn_quantum_phases))
    give("f_real", columns(L1_ffn_quantum_weights_real))
    give("f_imag", columns(L1_ffn_quantum_weights_imag))
    give("f_w2", np.asarray(L1_ffn_W2))
    give("f_b2", columns(L1_ffn_b2))

    out = nc.dram_tensor("out_0_dram", x.shape, F32, kind="ExternalOutput").ap()
    program(nc, a, out.rearrange("b t c -> (b t) c"), B, T, C)
    return _run(nc, [arrays], core_ids=[0]).results[0]["out_0_dram"]
```

```python
from contextlib import ExitStack

import numpy as np

import concourse.bass as bass
from concourse import mybir

F32 = mybir.dt.float32
F32R = mybir.dt.float32r
BF16 = mybir.dt.bfloat16
I32 = mybir.dt.int32
ALU = mybir.AluOpType
ACT = mybir.ActivationFunctionType
AX_X = mybir.AxisListType.X
MASKED = -1e30
L0_HEAD = 64
L0_WINDOW = 32
L1_HEADS = 16


def l0_attention(nc, x_in, w_l0, wo_l0, rope_l0, masks_q, masks_k, ident_in, x1, mean, comb1):
    NB, T, C = x_in.shape
    NT = T // 128
    HD = 64
    PAIRS = wo_l0.shape[0] // 128
    HALF = 4 * 128
    WIN = 32
    BAND = 128 + WIN
    widths = [min(BAND, T - 128 * t) for t in range(NT)]
    GT = NT // 2
    PW = BAND * (NT - 1) + widths[-1]
    VH = w_l0.shape[1] // 3
    NV = NT * (VH // HALF)

    x_v = x_in.rearrange("b (t p) c -> b p t c", p=128)

    with ExitStack() as ctx:
        def sb(name, shape, dt=F32):
            return ctx.enter_context(nc.sbuf_tensor("a_" + name, shape, dt))

        def ps(name, shape):
            return ctx.enter_context(nc.psum_tensor("a_" + name, shape, F32))

        def sem(name):
            return ctx.enter_context(nc.semaphore("a_" + name))

        w_hi = sb("w_hi", [128, 3 * VH], F32R)
        w_lo = sb("w_lo", [128, 3 * VH], F32R)
        wo_sb = sb("wo", [128, PAIRS, C])
        rope = sb("rope", [128, 4, T])
        mq = sb("mq", [128, NT * BAND], BF16)
        mk = sb("mk", [128, GT * BAND], BF16)
        ident = sb("ident", [128, 128])
        identx = sb("identx", [128, WIN + 128], BF16)
        ones = sb("ones", [128, HD])
        xpre = sb("xpre", [128, NT, C])
        xres = sb("xres", [128, NT, C])
        xn = sb("xn", [128, NT, C])
        xnT_hi = [sb(f"xnT_hi{k}", [128, T], F32R) for k in range(2)]
        xnT_lo = [sb(f"xnT_lo{k}", [128, T], F32R) for k in range(2)]
        v_sb = [sb(f"v{k}", [128, NT, VH]) for k in range(2)]
        other = [sb(f"other{k}", [128, 2, T]) for k in range(2)]
        prod = [sb(f"prod{k}", [128, 4, T]) for k in range(2)]
        qT = [sb(f"qT{k}", [128, T]) for k in range(4)]
        kT = [sb(f"kT{k}", [128, T]) for k in range(4)]
        qB = [sb(f"qB{k}", [128, T], BF16) for k in range(2)]
        kB = [sb(f"kB{k}", [128, WIN + T], BF16) for k in range(2)]
        nmax = [sb(f"nmax{k}", [128, 2, NT], BF16) for k in range(2)]
        pT = [[sb(f"pT{k}{h}", [128, PW]) for h in range(2)] for k in range(2)]
        rden = sb("rden", [128, T])
        oT = sb("oT", [128, PAIRS, T])
        w_whole = oT[:].rearrange("p a t -> p (a t)")[:, 0:3 * VH]
        ynorm = sb("ynorm", [128, NT, C])
        st1 = sb("st1", [128, NT, 6])
        mv1 = sb("mv1", [128, NT, 2])
        st2 = sb("st2", [128, NT, 6])
        mv2 = sb("mv2", [128, NT, 2])
        neg_half = sb("neg_half", [128, NT])
        ve = sb("ve", [128, NT])
        rstd = sb("rstd", [128, NT])
        ms = sb("ms", [128, NT])
        ms2 = sb("ms2", [128, NT])
        rr = sb("rr", [128, NT])
        comb = sb("comb", [128, NT])
        st3 = sb("st3", [128, NT, 6])
        mv3 = sb("mv3", [128, NT, 2])
        ve3 = sb("ve3", [128, NT])
        rstd3 = sb("rstd3", [128, NT])
        ms3 = sb("ms3", [128, NT])
        ms4 = sb("ms4", [128, NT])
        rr3 = sb("rr3", [128, NT])
        eps5 = sb("eps5", [128, NT])
        eps6 = sb("eps6", [128, NT])
        mark = sb("mark", [128, 1])
        ve2 = sb("ve2", [128, NT])
        rstd2 = sb("rstd2", [128, NT])

        proj = [ps(f"proj{k}", [128, HALF]) for k in range(2)]
        s_ps = [ps(f"s{k}", [128, HALF]) for k in range(2)]
        t_ps = [ps(f"t{k}", [128, HALF]) for k in range(2)]
        o_ps = ps("o", [128, HALF])
        d_ps = ps("d", [128, HALF])

        loaded = sem("loaded")
        ident_loaded = sem("ident_loaded")
        w_loaded = sem("w_loaded")
        const_set = sem("const_set")
        identx_ready = sem("identx_ready")
        xpre_in = sem("xpre_in")
        xres_in = sem("xres_in")
        stats1 = sem("stats1")
        pool_step = sem("pool_step")
        comb_ready = sem("comb_ready")
        xn_ready = sem("xn_ready")
        xn_transposed = sem("xn_transposed")
        w_hi_ready = sem("w_hi_ready")
        w_ready = sem("w_ready")
        xnT_hi_ready = sem("xnT_hi_ready")
        xnT_ready = sem("xnT_ready")
        v_done = sem("v_done")
        v_evac = sem("v_evac")
        qk_done = sem("qk_done")
        swap_done = sem("swap_done")
        rope_done = sem("rope_done")
        rope2_done = sem("rope2_done")
        add_done = sem("add_done")
        round_done = sem("round_done")
        s_done = sem("s_done")
        max_done = sem("max_done")
        st_done = sem("st_done")
        exp_done = sem("exp_done")
        av_done = sem("av_done")
        rden_done = sem("rden_done")
        norm_done = sem("norm_done")
        y_done = sem("y_done")
        stats2 = sem("stats2")
        x_stat = sem("x_stat")
        y_stat = sem("y_stat")
        rstd2_ready = sem("rstd2_ready")
        ynorm_done = sem("ynorm_done")
        x1_ready = sem("x1_ready")
        sum_stat = sem("sum_stat")
        sum_stats = sem("sum_stats")
        sum_step = sem("sum_step")
        NCONST = 6
        NLOADS = 4

        LAG_MAX, LAG_EXP, LAG_VAL = 2, 3, 4
        OUT_STEP, XN_STEP, V_STEP = 4, 5, 6
        SUM_STEP = 6
        V_EACH = -(-NV // (PAIRS - V_STEP))

        uses = []
        for s in range(PAIRS):
            uses += [("qk", s, c) for c in range(2)]
            if s == OUT_STEP:
                uses += [("y", s, 0)]
            if s == XN_STEP:
                uses += [("xn", s, 0)]
            if s >= V_STEP:
                uses += [("v", s, n) for n in range(V_EACH * (s - V_STEP), min(NV, V_EACH * (s - V_STEP + 1)))]

        def program(engine, step):
            many = 10 * PAIRS
            for r in range(2 * PAIRS):
                step(r // PAIRS, r // PAIRS, r % PAIRS, r, many)
            with engine.Fori(1, NB // 2 - 1) as i:
                for r in range(2 * PAIRS):
                    step(2 * i + r // PAIRS, r // PAIRS, r % PAIRS, many, many)
            for r in range(2 * PAIRS + SUM_STEP + 1):
                step(NB - 2 + r // PAIRS, r // PAIRS % 2, r % PAIRS, many, 2 * PAIRS - r)

        def alive(lag, before, left):
            return before >= lag and left + lag > 0

        def bank_of(what):
            return proj[uses.index((what, {"y": OUT_STEP, "xn": XN_STEP}[what], 0)) % 2]

        block = ctx.enter_context(nc.Block())

        @block.sync
        def _(sp):
            sp.dma_start(xpre[:], x_v[0]).then_inc(xpre_in, 16)
            sp.dma_start(ident[:], ident_in).then_inc(ident_loaded, 16)
            sp.dma_start(w_whole, w_l0).then_inc(w_loaded, 16)
            sp.dma_start(rope[:], rope_l0).then_inc(loaded, 16)
            sp.dma_start(mq[:], masks_q).then_inc(loaded, 16)
            sp.dma_start(mk[:], masks_k).then_inc(loaded, 16)
            sp.dma_start(wo_sb[:], wo_l0.rearrange("(k p) c -> p k c", p=128)).then_inc(loaded, 16)
            sp.wait_ge(xn_ready, 1)
            sp.dma_start(xpre[:], x_v[1]).then_inc(xpre_in, 16)
            sp.dma_start(xres[:], x_v[0]).then_inc(xres_in, 16)

            with sp.Fori(1, NB - 1) as i:
                sp.wait_ge(xn_ready, i + 1)
                sp.dma_start(xpre[:], x_v[i + 1]).then_inc(xpre_in, 16)
                sp.wait_ge(x1_ready, i)
                sp.dma_start(xres[:], x_v[i]).then_inc(xres_in, 16)
            sp.wait_ge(x1_ready, NB - 1)
            sp.dma_start(xres[:], x_v[NB - 1]).then_inc(xres_in, 16)

        @block.gpsimd
        def _(pool):
            nc.gpsimd.memset(neg_half[:], -0.5).then_inc(const_set, 1)
            nc.gpsimd.memset(eps5[:], 1e-5).then_inc(const_set, 1)
            nc.gpsimd.memset(eps6[:], 1e-6).then_inc(const_set, 1)
            nc.gpsimd.memset(ones[:], 1.0).then_inc(const_set, 1)
            for k in range(2):
                nc.gpsimd.memset(kB[k][:, 0:WIN], 0.0).then_inc(const_set, 1)

            def factors(b):
                n = 6 * b
                pool.wait_ge(stats1, b + 1)
                nc.gpsimd.tensor_tensor(ve[:], mv1[:, :, 1], eps5[:], ALU.add).then_inc(pool_step, 1)
                pool.wait_ge(pool_step, n + 1)
                nc.gpsimd.tensor_tensor(rstd[:], ve[:], neg_half[:], ALU.pow).then_inc(pool_step, 1)
                pool.wait_ge(pool_step, n + 2)
                nc.gpsimd.tensor_tensor(ms[:], rstd[:], rstd[:], ALU.mult).then_inc(pool_step, 1)
                pool.wait_ge(pool_step, n + 3)
                nc.gpsimd.tensor_tensor(ms2[:], ms[:], mv1[:, :, 1], ALU.mult).then_inc(pool_step, 1)
                pool.wait_ge(pool_step, n + 4)
                nc.gpsimd.tensor_tensor(ms[:], ms2[:], eps6[:], ALU.add).then_inc(pool_step, 1)
                pool.wait_ge(pool_step, n + 5)
                nc.gpsimd.tensor_tensor(rr[:], ms[:], neg_half[:], ALU.pow).then_inc(pool_step, 1)
                pool.wait_ge(pool_step, n + 6)
                nc.gpsimd.tensor_tensor(comb[:], rr[:], rstd[:], ALU.mult).then_inc(comb_ready, 1)

            def sum_factors(b):
                n = 7 * b
                pool.wait_ge(sum_stats, b + 1)
                nc.gpsimd.tensor_tensor(ve3[:], mv3[:, :, 1], eps5[:], ALU.add).then_inc(sum_step, 1)
                pool.wait_ge(sum_step, n + 1)
                nc.gpsimd.tensor_tensor(rstd3[:], ve3[:], neg_half[:], ALU.pow).then_inc(sum_step, 1)
                pool.wait_ge(sum_step, n + 2)
                nc.gpsimd.tensor_tensor(ms3[:], rstd3[:], rstd3[:], ALU.mult).then_inc(sum_step, 1)
                pool.wait_ge(sum_step, n + 3)
                nc.gpsimd.tensor_tensor(ms4[:], ms3[:], mv3[:, :, 1], ALU.mult).then_inc(sum_step, 1)
                pool.wait_ge(sum_step, n + 4)
                nc.gpsimd.tensor_tensor(ms3[:], ms4[:], eps5[:], ALU.add).then_inc(sum_step, 1)
                pool.wait_ge(sum_step, n + 5)
                nc.gpsimd.tensor_tensor(rr3[:], ms3[:], neg_half[:], ALU.pow).then_inc(sum_step, 1)
                pool.wait_ge(sum_step, n + 6)
                nc.gpsimd.tensor_tensor(comb1[:, bass.ds(NT * b, NT)], rr3[:], rstd3[:], ALU.mult).then_inc(sum_step, 1)

            pool.wait_ge(const_set, NCONST)
            factors(0)

            pool.wait_ge(loaded, 16 * NLOADS)

            def step(b, k, s, before, left):
                n = PAIRS * b + s
                if alive(0, before, left):
                    for side, dst in ((0, qT[s % 4][:]), (1, kT[s % 4][:])):
                        pool.wait_ge(swap_done, 2 * n + side + 1)
                        nc.gpsimd.tensor_tensor(prod[s % 2][:, 2 * side + 1, :], other[s % 2][:, side, :],
                                                rope[:, 2 * side + 1, :], ALU.mult).then_inc(rope2_done, 1)
                        pool.wait_ge(rope_done, 2 * n + side + 1)
                        pool.wait_ge(rope2_done, 2 * n + side + 1)
                        if before >= 4 and side == 0:
                            pool.wait_ge(st_done, 4 * (n - 3))
                        nc.gpsimd.tensor_tensor(dst, prod[s % 2][:, 2 * side, :], prod[s % 2][:, 2 * side + 1, :],
                                                ALU.add).then_inc(add_done, 1)
                if s == 1 and left > PAIRS:
                    factors(b + 1)
                if s == OUT_STEP and before >= PAIRS:
                    pool.wait_ge(stats2, b)
                    nc.gpsimd.tensor_tensor(rstd2[:], ve2[:], neg_half[:], ALU.pow).then_inc(rstd2_ready, 1)
                if s == SUM_STEP and before >= PAIRS:
                    sum_factors(b - 1)

            program(pool, step)
            pool.wait_ge(sum_step, 7 * NB)

        @block.scalar
        def _(act):
            def turned(b, k):
                act.wait_ge(xn_transposed, b + 1)
                nc.scalar.copy(xnT_hi[k][:], bank_of("xn")[:, 0:T]).then_inc(xnT_hi_ready, 1)

            def v_copy(b, k, n, bank):
                t, half = divmod(n, VH // HALF)
                act.wait_ge(v_done, NV * b + n + 1)
                nc.scalar.copy(v_sb[k][:, t, half * HALF:(half + 1) * HALF], proj[bank][:]).then_inc(v_evac, 1)

            act.wait_ge(ident_loaded, 16)
            nc.scalar.copy(identx[:, 0:WIN], ident[:, 0:WIN])
            nc.scalar.copy(identx[:, WIN:BAND], ident[:]).then_inc(identx_ready, 1)
            turned(0, 0)
            act.wait_ge(w_loaded, 16)
            nc.scalar.copy(w_hi[:], w_whole).then_inc(w_hi_ready, 1)
            for n in range(NV):
                v_copy(0, 0, n, n % 2)

            def exchanged(n, s, side, before):
                act.wait_ge(qk_done, 2 * n + side + 1)
                if before >= 2:
                    act.wait_ge(rope2_done, 2 * (n - 2) + side + 1)
                bank = uses.index(("qk", s, side)) % 2
                for part in range(4):
                    src = part ^ 1
                    ins = nc.scalar.copy(other[s % 2][32 * part:32 * (part + 1), side, :],
                                         proj[bank][32 * src:32 * (src + 1), 0:T])
                ins.then_inc(swap_done, 1)

            def exponentials(m, s, h, av_before):
                for g in range(2):
                    if av_before and h == 0 and g == 0:
                        act.wait_ge(av_done, m - 1)
                    cols = slice(BAND * GT * g, min(BAND * GT * (g + 1), PW))
                    act.wait_ge(st_done, 4 * m + 2 * h + g + 1)
                    nc.scalar.activation(pT[s % 2][h][:, cols], t_ps[g][:, 0:cols.stop - cols.start],
                                         ACT.Exp).then_inc(exp_done, 1)

            def step(b, k, s, before, left):
                n = PAIRS * b + s
                m = n - LAG_EXP
                if alive(0, before, left):
                    exchanged(n, s, 0, before)
                    exchanged(n, s, 1, before)
                if alive(LAG_EXP, before, left):
                    exponentials(m, (s - LAG_EXP) % PAIRS, 0, before >= LAG_EXP + 2)
                if alive(0, before, left):
                    if before >= 2:
                        act.wait_ge(s_done, 4 * (n - 1))
                    act.wait_ge(add_done, 2 * n + 1)
                    nc.scalar.copy(qB[s % 2][:], qT[s % 4][:]).then_inc(round_done, 1)
                    if left > PAIRS:
                        for u, (what, at, i) in enumerate(uses):
                            if (what, at) == ("v", s):
                                v_copy(b + 1, 1 - k, i, u % 2)
                if s == XN_STEP and left > PAIRS:
                    turned(b + 1, 1 - k)
                if alive(LAG_EXP, before, left):
                    exponentials(m, (s - LAG_EXP) % PAIRS, 1, False)
                if alive(0, before, left):
                    act.wait_ge(add_done, 2 * n + 2)
                    nc.scalar.copy(kB[s % 2][:, WIN:WIN + T], kT[s % 4][:]).then_inc(round_done, 1)

            program(act, step)

        @block.vector
        def _(dve):
            def statistics(b):
                dve.wait_ge(xpre_in, 16 * (b + 1))
                for t in range(NT):
                    ins = nc.vector.bn_stats(st1[:, t, :], xpre[:, t, :])
                ins.then_inc(x_stat, 1)
                dve.wait_ge(x_stat, b + 1)
                nc.vector.memset(mark[:], 0.0)
                for t in range(NT):
                    ins = nc.vector.bn_aggr(mv1[:, t, :], st1[:, t, :])
                ins.then_inc(stats1, 1)

            def normalised(b):
                dve.wait_ge(comb_ready, b + 1)
                for t in range(NT):
                    ins = nc.vector.tensor_scalar(xn[:, t, :], xpre[:, t, :], mv1[:, t, 0:1], comb[:, t:t + 1],
                                                  ALU.subtract, ALU.mult)
                ins.then_inc(xn_ready, 1)

            statistics(0)
            normalised(0)
            def turned_low(b, k):
                dve.wait_ge(xnT_hi_ready, b + 1)
                nc.vector.tensor_tensor(xnT_lo[k][:], bank_of("xn")[:, 0:T], xnT_hi[k][:],
                                        ALU.subtract).then_inc(xnT_ready, 1)

            turned_low(0, 0)
            dve.wait_ge(w_hi_ready, 1)
            nc.vector.tensor_tensor(w_lo[:], w_whole, w_hi[:], ALU.subtract).then_inc(w_ready, 1)
            dve.wait_ge(loaded, 16 * NLOADS)

            def output_statistics(b):
                dve.wait_ge(y_done, b + 1)
                for t in range(NT):
                    ins = nc.vector.bn_stats(st2[:, t, :], bank_of("y")[:, t * 128:(t + 1) * 128])
                ins.then_inc(y_stat, 1)
                dve.wait_ge(y_stat, b + 1)
                nc.vector.memset(mark[:], 0.0)
                for t in range(NT):
                    ins = nc.vector.bn_aggr(mv2[:, t, :], st2[:, t, :])
                ins.then_inc(ynorm_done, 1)
                dve.wait_ge(ynorm_done, 3 * b + 1)
                nc.vector.tensor_scalar(ve2[:], mv2[:, :, 1], 1e-5, None, ALU.add).then_inc(stats2, 1)

            def output(b):
                dve.wait_ge(rstd2_ready, b + 1)
                for t in range(NT):
                    ins = nc.vector.tensor_scalar(ynorm[:, t, :], bank_of("y")[:, t * 128:(t + 1) * 128], mv2[:, t, 0:1],
                                                  rstd2[:, t:t + 1], ALU.subtract, ALU.mult)
                ins.then_inc(ynorm_done, 2)
                dve.wait_ge(ynorm_done, 3 * b + 3)
                dve.wait_ge(xres_in, 16 * (b + 1))
                nc.vector.tensor_tensor(x1[:, bass.ds(NT * b, NT), :], ynorm[:], xres[:], ALU.add).then_inc(x1_ready, 1)

            def sum_statistics(b):
                if not (isinstance(b, int) and b == 0):
                    dve.wait_ge(sum_step, 7 * b)
                dve.wait_ge(x1_ready, b + 1)
                nc.vector.memset(mark[:], 0.0)
                for t in range(NT):
                    ins = nc.vector.bn_stats(st3[:, t, :], x1[:, NT * b + t, :])
                ins.then_inc(sum_stat, 1)
                dve.wait_ge(sum_stat, 2 * b + 1)
                nc.vector.memset(mark[:], 0.0)
                for t in range(NT):
                    ins = nc.vector.bn_aggr(mv3[:, t, :], st3[:, t, :])
                ins.then_inc(sum_stats, 1)
                dve.wait_ge(sum_stats, b + 1)
                nc.vector.tensor_scalar(mean[:, bass.ds(NT * b, NT)], mv3[:, :, 0], 1.0, None,
                                        ALU.mult).then_inc(sum_stat, 1)

            def step(b, k, s, before, left):
                n = PAIRS * b + s

                def rope_product(side):
                    if not alive(0, before, left):
                        return
                    dve.wait_ge(swap_done, 2 * n + side + 1)
                    if before >= 2:
                        dve.wait_ge(add_done, 2 * (n - 2) + side + 1)
                    bank = uses.index(("qk", s, side)) % 2
                    nc.vector.tensor_tensor(prod[s % 2][:, 2 * side, :], proj[bank][:, 0:T], rope[:, 2 * side, :],
                                            ALU.mult).then_inc(rope_done, 1)

                def maxima(h):
                    if not alive(LAG_MAX, before, left):
                        return
                    m = n - LAG_MAX
                    for g in range(2):
                        if before >= LAG_MAX + 2 and h == 0 and g == 0:
                            dve.wait_ge(st_done, 4 * (m - 1))
                        dve.wait_ge(s_done, 4 * m + 2 * h + g + 1)
                        scores = s_ps[g][:, 0:GT * BAND].rearrange("p (j k) -> p j k", k=BAND)
                        nc.vector.reduce_max(nmax[(s - LAG_MAX) % 2][:, h, GT * g:GT * (g + 1)], scores, AX_X,
                                             negate=True).then_inc(max_done, 1)

                maxima(0)
                rope_product(0)
                maxima(1)
                rope_product(1)
                if s == 1 and left > PAIRS:
                    statistics(b + 1)
                if s == OUT_STEP and left > PAIRS:
                    dve.wait_ge(xn_transposed, b + 1)
                    normalised(b + 1)
                if s == XN_STEP and left > PAIRS:
                    turned_low(b + 1, 1 - k)
                if s == OUT_STEP and before >= PAIRS:
                    output_statistics(b - 1)
                    output(b - 1)
                if s == SUM_STEP and before >= PAIRS:
                    sum_statistics(b - 1)
                if alive(LAG_VAL, before, left):
                    m = n - LAG_VAL
                    dve.wait_ge(av_done, m + 1)
                    nc.vector.reciprocal(rden[:], d_ps[:, 0:T]).then_inc(rden_done, 1)
                    dve.wait_ge(rden_done, m + 1)
                    nc.vector.tensor_tensor(oT[:, (s - LAG_VAL) % PAIRS, :], o_ps[:, 0:T], rden[:],
                                            ALU.mult).then_inc(norm_done, 1)

            program(dve, step)

        @block.tensor
        def _(pe):
            def transposes(b):
                pe.wait_ge(xn_ready, b + 1)
                for t in range(NT):
                    ins = nc.tensor.transpose(bank_of("xn")[:, t * 128:(t + 1) * 128], xn[:, t, :], ident[:])
                ins.then_inc(xn_transposed, 1)

            def value(k, n, bank):
                t, half = divmod(n, VH // HALF)
                for part, (x_part, w_part) in enumerate(((xnT_hi, w_lo), (xnT_lo, w_hi), (xnT_hi, w_hi))):
                    ins = nc.tensor.matmul(proj[bank][:], x_part[k][:, 128 * t:128 * (t + 1)],
                                           w_part[:, 2 * VH + half * HALF:2 * VH + (half + 1) * HALF],
                                           start=part == 0, stop=part == 2)
                ins.then_inc(v_done, 1)

            def formed(what, before, left):
                return {"qk": left > 0, "v": left > PAIRS, "xn": left > PAIRS, "y": before >= PAIRS}[what]

            def bank_free(b, u, before, left):
                before, left = before - uses[u][1], left + uses[u][1]
                u -= 2
                while u < 0 or not formed(uses[u][0], before, left):
                    if u < 0:
                        b, u, before, left = b - 1, u + len(uses), before - PAIRS, left + PAIRS
                    else:
                        u -= 2
                what, s, m = uses[u]
                if what == "qk":
                    pe.wait_ge(rope_done, 2 * (PAIRS * b + s) + m + 1)
                elif what == "v":
                    pe.wait_ge(v_evac, NV * (b + 1) + m + 1)
                elif what == "xn":
                    pe.wait_ge(xnT_ready, b + 2)
                else:
                    pe.wait_ge(ynorm_done, 3 * b)

            pe.wait_ge(ident_loaded, 16)
            transposes(0)
            pe.wait_ge(const_set, NCONST)
            pe.wait_ge(loaded, 16 * NLOADS)
            pe.wait_ge(xnT_ready, 1)
            pe.wait_ge(w_ready, 1)
            for n in range(NV):
                if n >= 2:
                    pe.wait_ge(v_evac, n - 1)
                value(0, n, n % 2)
            pe.wait_ge(identx_ready, 1)

            def max_scores(m, s, h):
                pe.wait_ge(round_done, 2 * m + 2)
                rows = slice(HD * h, HD * h + HD)
                for g in range(2):
                    use = 4 * m + 2 * h + g
                    if not (isinstance(m, int) and use < 2):
                        pe.wait_ge(max_done, use - 1)
                    nc.tensor.matmul(s_ps[g][:, 0:GT * BAND], identx[:, WIN:BAND],
                                     mq[:, GT * BAND * g:GT * BAND * (g + 1)], start=True, stop=False)
                    for i in range(GT):
                        t = GT * g + i
                        ins = nc.tensor.matmul(s_ps[g][:, BAND * i:BAND * (i + 1)],
                                               qB[s % 2][rows, 128 * t:128 * (t + 1)],
                                               kB[s % 2][rows, 128 * t:128 * t + BAND],
                                               start=False, stop=i == GT - 1)
                    ins.then_inc(s_done, 1)

            def shifted_scores(m, s, h):
                rows = slice(HD * h, HD * h + HD)
                pe.wait_ge(max_done, 4 * m + 2 * h + 2)
                for g in range(2):
                    use = 4 * m + 2 * h + g
                    if not (isinstance(m, int) and use < 2):
                        pe.wait_ge(exp_done, use - 1)
                    width = sum(widths[GT * g:GT * (g + 1)])
                    nc.tensor.matmul(t_ps[g][:, 0:width], identx[:, WIN:BAND], mk[:, 0:width], start=True, stop=False)
                    for i in range(GT):
                        t = GT * g + i
                        nc.tensor.matmul(t_ps[g][:, BAND * i:BAND * i + widths[t]],
                                         kT[s % 4][rows, 128 * t:128 * (t + 1)],
                                         qT[s % 4][rows, 128 * t:128 * t + widths[t]], start=False, stop=False)
                    for t in range(GT * g, min(GT * (g + 1) + 1, NT)):
                        first = BAND * (t - GT * g) - (WIN if t > GT * g else 0)
                        last = min(BAND * (t - GT * g) + 128, width)
                        skip = WIN if t == GT * g else 0
                        ins = nc.tensor.matmul(t_ps[g][:, first:last], nmax[s % 2][:, h, t:t + 1].to_broadcast([128, 128]),
                                               identx[:, skip:skip + last - first], start=False,
                                               stop=last == width)
                    ins.then_inc(st_done, 1)

            def weighted_values(m, k, s):
                for t in range(NT):
                    for h in range(2):
                        col = (2 * s + h) * HD
                        nc.tensor.matmul(o_ps[HD * h:HD * h + HD, 128 * t:128 * t + widths[t]],
                                         v_sb[k][:, t, col:col + HD],
                                         pT[s % 2][h][:, BAND * t:BAND * t + widths[t]], start=t == 0,
                                         stop=t == NT - 1, skip_group_check=True)
                for t in range(NT):
                    for h in range(2):
                        ins = nc.tensor.matmul(d_ps[HD * h:HD * h + HD, 128 * t:128 * t + widths[t]], ones[:],
                                               pT[s % 2][h][:, BAND * t:BAND * t + widths[t]], start=t == 0,
                                               stop=t == NT - 1, skip_group_check=True)
                ins.then_inc(av_done, 1)

            def step(b, k, s, before, left):
                n = PAIRS * b + s

                def projections(kind, which=None):
                    for u, (what, at, i) in enumerate(uses):
                        if (what, at) != (kind, s) or which not in (None, i):
                            continue
                        if kind == "qk" and alive(0, before, left):
                            bank_free(b, u, before, left)
                            rows = slice(i * VH + s * 128, i * VH + (s + 1) * 128)
                            for part, (w_part, x_part) in enumerate(((w_lo, xnT_hi), (w_hi, xnT_lo), (w_hi, xnT_hi))):
                                ins = nc.tensor.matmul(proj[u % 2][:, 0:T], w_part[:, rows], x_part[k][:],
                                                       start=part == 0, stop=part == 2)
                            ins.then_inc(qk_done, 1)
                        if kind == "v" and left > PAIRS:
                            bank_free(b, u, before, left)
                            value(1 - k, i, u % 2)
                        if kind == "xn" and left > PAIRS:
                            bank_free(b, u, before, left)
                            transposes(b + 1)
                        if kind == "y" and before >= PAIRS:
                            bank_free(b, u, before, left)
                            pe.wait_ge(norm_done, PAIRS * b)
                            for t in range(NT):
                                for p in range(PAIRS):
                                    ins = nc.tensor.matmul(proj[u % 2][:, t * 128:(t + 1) * 128],
                                                           oT[:, p, t * 128:(t + 1) * 128], wo_sb[:, p, :],
                                                           start=p == 0, stop=p == PAIRS - 1)
                            ins.then_inc(y_done, 1)

                def maxima(h):
                    if alive(LAG_MAX, before, left):
                        max_scores(n - LAG_MAX, (s - LAG_MAX) % PAIRS, h)

                def shifted(h):
                    if alive(LAG_EXP, before, left):
                        shifted_scores(n - LAG_EXP, (s - LAG_EXP) % PAIRS, h)

                projections("qk", 0)
                maxima(0)
                projections("qk", 1)
                shifted(0)
                maxima(1)
                projections("xn")
                projections("y")
                if alive(LAG_VAL, before, left):
                    m = n - LAG_VAL
                    pe.wait_ge(exp_done, 4 * m + 4)
                    if before > LAG_VAL:
                        pe.wait_ge(norm_done, m)
                    weighted_values(m, k if s >= LAG_VAL else 1 - k, (s - LAG_VAL) % PAIRS)
                if s == V_STEP and left > PAIRS:
                    pe.wait_ge(xnT_ready, b + 2)
                projections("v")
                shifted(1)

            program(pe, step)


def routing(nc, x1, pos, mean, comb, cent_t, ln_g, ln_b, ident_in, ones_in, before_in, sorted_x):
    _, TILES, C = x1.shape
    E = cent_t.shape[1]
    CAP = TILES * 128 // E
    G4 = 4
    DIGITS = 8
    TIES = 3

    with ExitStack() as ctx:
        def sb(name, shape, dt=F32):
            return ctx.enter_context(nc.sbuf_tensor("b_" + name, shape, dt))

        def ps(name, shape):
            return ctx.enter_context(nc.psum_tensor("b_" + name, shape, F32))

        def sem(name):
            return ctx.enter_context(nc.semaphore("b_" + name))

        cent = sb("cent", [128, E])
        gamma = sb("gamma", [128, 1])
        beta = sb("beta", [128, 1])
        ident = sb("ident", [128, 128])
        ones = sb("ones", [128, 128], BF16)
        before = sb("before", [128, 128], BF16)
        zz = [sb(f"zz{k}", [128, G4, C]) for k in range(2)]
        nT = [sb(f"nT{k}", [128, G4 * 128]) for k in range(2)]
        score = sb("score", [128, E, TILES])
        sign = sb("sign", [128, E, TILES], I32)
        key = sb("key", [128, E, TILES], I32)
        half_i = sb("half_i", [128, E, TILES], I32)
        half_j = sb("half_j", [128, E, TILES], I32)
        hi1 = sb("hi1", [128, E, TILES])
        lo1 = sb("lo1", [128, E, TILES])
        free = sb("free", [128, TILES])
        place = sb("place", [128, TILES])
        a1 = sb("a1", [128, TILES])
        b1 = sb("b1", [128, TILES])
        eq = sb("eq", [128, TILES])
        above = sb("above", [128, TILES])
        above2 = sb("above2", [128, TILES])
        tied = sb("tied", [128, TILES], BF16)
        taken = sb("taken", [128, TILES], BF16)
        run = sb("run", [128, TILES])
        rank = sb("rank", [128, TILES])
        junk = sb("junk", [128, TIES, TILES])
        junk3 = sb("junk3", [128, TIES])
        steps = sb("steps", [128, DIGITS, TIES])
        first = sb("first", [128, TIES])
        base = sb("base", [128, 1])
        thr = [sb(f"thr{k}", [128, 1]) for k in range(2)]
        tries = sb("tries", [128, TIES])
        tries_base = sb("tries_base", [128, TIES])
        count = sb("count", [128, TIES], BF16)
        digit = sb("digit", [128, 1])
        need = [sb(f"need{k}", [128, 1]) for k in range(3)]
        one_col = sb("one_col", [128, TILES])

        tp = [ps(f"tp{k}", [128, 512]) for k in range(2)]
        sp_ps = [ps(f"sp{k}", [128, 512]) for k in range(2)]
        tot = ps("tot", [128, 512])
        pre_ps = ps("pre", [128, 512])
        all_ps = ps("all", [128, 512])

        loaded = sem("loaded")
        zz_ready = sem("zz_ready")
        zz_turned = sem("zz_turned")
        nT_ready = sem("nT_ready")
        sc_done = sem("sc_done")
        sc_kept = sem("sc_kept")
        chain = sem("chain")
        cnt_ready = sem("cnt_ready")
        tot_ready = sem("tot_ready")
        tied_ready = sem("tied_ready")
        rank_ready = sem("rank_ready")
        pos_ready = sem("pos_ready")
        scattered = sem("scattered")
        NLOADS = 6

        CNT = 2 * DIGITS + 2

        GROUPS = TILES // G4

        def groups(engine, one):
            for m in range(4):
                one(m, m % 2)
            with engine.Fori(2, GROUPS // 2) as i:
                for k in range(2):
                    one(2 * i + k, k)

        def at_least(m, n):
            return not isinstance(m, int) or m >= n

        block = ctx.enter_context(nc.Block())

        @block.sync
        def _(sp):
            sp.dma_start(cent[:], cent_t).then_inc(loaded, 16)
            sp.dma_start(gamma[:], ln_g).then_inc(loaded, 16)
            sp.dma_start(beta[:], ln_b).then_inc(loaded, 16)
            sp.dma_start(ident[:], ident_in).then_inc(loaded, 16)
            sp.dma_start(ones[:], ones_in).then_inc(loaded, 16)
            sp.dma_start(before[:], before_in).then_inc(loaded, 16)

        @block.gpsimd
        def _(pool):
            pool.wait_ge(pos_ready, 1)
            for t in range(TILES):
                pool.indirect_dma_start(out=sorted_x, out_offset=bass.IndirectOffsetOnAxis(ap=pos[:, t:t + 1], axis=0),
                                        in_=x1[:, t, :], in_offset=None).then_inc(scattered, 16)
            pool.wait_ge(scattered, 16 * TILES)

        @block.scalar
        def _(act):
            act.wait_ge(loaded, 16 * NLOADS)

            def one(m, k):
                act.wait_ge(zz_turned, m + 1)
                if at_least(m, 2):
                    act.wait_ge(sc_done, m - 1)
                nc.scalar.activation(nT[k][:], tp[k][:], ACT.Identity, bias=beta[:], scale=gamma[:]).then_inc(nT_ready, 1)

            groups(act, one)

        @block.tensor
        def _(pe):
            pe.wait_ge(loaded, 16 * NLOADS)

            def scores(m, k):
                pe.wait_ge(nT_ready, m + 1)
                if at_least(m, 2):
                    pe.wait_ge(sc_kept, m - 1)
                for t in range(G4):
                    ins = nc.tensor.matmul(sp_ps[k][:, t * E:(t + 1) * E], nT[k][:, t * 128:(t + 1) * 128], cent[:],
                                           start=True, stop=True)
                ins.then_inc(sc_done, 1)

            def one(m, k):
                pe.wait_ge(zz_ready, m + 1)
                if at_least(m, 2):
                    pe.wait_ge(nT_ready, m - 1)
                for t in range(G4):
                    ins = nc.tensor.transpose(tp[k][:, t * 128:(t + 1) * 128], zz[k][:, t, :], ident[:])
                ins.then_inc(zz_turned, 1)
                if at_least(m, 1):
                    scores(m - 1, 1 - k)

            groups(pe, one)
            scores(GROUPS - 1, 1)

            def ranks(flags, n):
                pe.wait_ge(tied_ready, n)
                nc.tensor.matmul(pre_ps[:, 0:TILES], before[:], flags[:], start=True, stop=True)
                nc.tensor.matmul(all_ps[:, 0:TILES], ones[:], flags[:], start=True, stop=True).then_inc(rank_ready, 1)

            with pe.Fori(0, E - 1) as e:
                for n in range(CNT):
                    pe.wait_ge(cnt_ready, CNT * e + n + 1)
                    nc.tensor.matmul(tot[:, 0:TIES], ones[:], count[:], start=True, stop=True).then_inc(tot_ready, 1)
                ranks(tied, 2 * e + 1)
                ranks(taken, 2 * e + 2)
            ranks(taken, 2 * (E - 1) + 1)

        @block.vector
        def _(dve):
            chained = [0]

            def link(ins):
                chained[0] += 1
                ins.then_inc(chain, 1)
                dve.wait_ge(chain, chained[0])

            link(nc.vector.memset(base[:], 0.0))
            nc.vector.memset(free[:], 1.0)
            nc.vector.memset(place[:], 0.0)
            nc.vector.memset(one_col[:], 1.0)
            nc.vector.memset(need[0][:], float(CAP))
            nc.vector.memset(count[:], 0.0)
            for d in range(DIGITS):
                for k in range(TIES):
                    nc.vector.memset(steps[:, d, k:k + 1], float((k + 1) * 4 ** d))
            for k in range(TIES):
                nc.vector.memset(first[:, k:k + 1], float((k + 1) * 4 ** (DIGITS - 1) + 1))


            def kept(m, k):
                dve.wait_ge(sc_done, m + 1)
                nc.vector.tensor_copy(score[:, :, bass.ds(m * G4, G4)],
                                      sp_ps[k][:, 0:G4 * E].rearrange("p (t e) -> p e t", e=E)).then_inc(sc_kept, 1)

            def one(m, k):
                if at_least(m, 2):
                    dve.wait_ge(zz_turned, m - 1)
                for u in range(G4):
                    t = m * G4 + u
                    ins = nc.vector.tensor_scalar(zz[k][:, u, :], x1[:, t, :], mean[:, bass.ds(t, 1)],
                                                  comb[:, bass.ds(t, 1)], ALU.subtract, ALU.mult)
                ins.then_inc(zz_ready, 1)
                if at_least(m, 2):
                    kept(m - 2, k)

            groups(dve, one)
            for m in range(GROUPS - 2, GROUPS):
                kept(m, m % 2)
            dve.wait_ge(sc_kept, GROUPS)
            bits = score[:].bitcast(I32)
            link(nc.vector.tensor_scalar(sign[:], bits, 31, -2 ** 31, ALU.arith_shift_right, ALU.bitwise_or))
            link(nc.vector.tensor_tensor(key[:], bits, sign[:], ALU.bitwise_xor))
            nc.vector.tensor_scalar(half_i[:], key[:], 16, 0xffff, ALU.arith_shift_right, ALU.bitwise_and)
            link(nc.vector.tensor_scalar(half_j[:], key[:], 0xffff, None, ALU.bitwise_and))
            nc.vector.tensor_scalar(hi1[:], half_i[:], 1.0, None, ALU.add)
            link(nc.vector.tensor_scalar(lo1[:], half_j[:], 1.0, None, ALU.add))
            done = chained[0]

            def expert(e, last):
                step = [0]

                def link(ins):
                    step[0] += 1
                    ins.then_inc(chain, 1)
                    dve.wait_ge(chain, PER * e + done + step[0])

                totals = [0]

                def total(ins):
                    totals[0] += 1
                    ins.then_inc(cnt_ready, 1)
                    return lambda: dve.wait_ge(tot_ready, CNT * e + totals[0])

                def search(values, needed, thr):
                    nc.vector.memset(thr[:], 1.0)
                    link(nc.vector.tensor_copy(tries[:], first[:]))
                    for d in reversed(range(DIGITS)):
                        for k in range(TIES):
                            ins = nc.vector.tensor_scalar(junk[:, k, :], values, tries[:, k:k + 1], None, ALU.is_ge,
                                                          ALU.add, accum_out=count[:, k:k + 1])
                        wait_total = total(ins)
                        dve.wait_ge(chain, PER * e + done + step[0])
                        if d:
                            nc.vector.tensor_scalar(tries_base[:], steps[:, d - 1, :], thr[:], None, ALU.add)
                        wait_total()
                        link(nc.vector.tensor_scalar(junk3[:], tot[:, 0:TIES], needed[:], None, ALU.is_ge,
                                                     ALU.add, accum_out=digit[:]))
                        if d:
                            ins = nc.vector.scalar_tensor_tensor(tries[:], digit[:].to_broadcast([128, TIES]),
                                                                 float(4 ** d), tries_base[:], ALU.mult, ALU.add)
                            step[0] += 2
                            ins.then_inc(chain, 1)
                            nc.vector.scalar_tensor_tensor(thr[:], digit[:], float(4 ** d), thr[:],
                                                           ALU.mult, ALU.add).then_inc(chain, 1)
                            dve.wait_ge(chain, PER * e + done + step[0] - 1)
                        else:
                            link(nc.vector.scalar_tensor_tensor(thr[:], digit[:], 1.0, thr[:], ALU.mult, ALU.add))

                def ranked(flags_done, n):
                    flags_done.then_inc(tied_ready, 1)
                    dve.wait_ge(rank_ready, n)
                    link(nc.vector.tensor_tensor_scan(run[:], one_col[:], all_ps[:, 0:TILES], 0.0, ALU.mult, ALU.add))
                    link(nc.vector.tensor_tensor(run[:], run[:], all_ps[:, 0:TILES], ALU.subtract))
                    link(nc.vector.tensor_tensor(rank[:], run[:], pre_ps[:, 0:TILES], ALU.add))

                if last:
                    ins = nc.vector.tensor_copy(taken[:], free[:])
                    ranked(ins, 2 * e + 1)
                else:
                    link(nc.vector.tensor_tensor(a1[:], hi1[:, e, :], free[:], ALU.mult))
                    search(a1[:], need[0], thr[0])
                    total(nc.vector.tensor_scalar(above[:], a1[:], thr[0][:], None, ALU.is_gt, ALU.add,
                                                  accum_out=count[:, 0:1]))()
                    nc.vector.tensor_scalar(eq[:], a1[:], thr[0][:], None, ALU.is_equal)
                    link(nc.vector.tensor_tensor(need[1][:], need[0][:], tot[:, 0:1], ALU.subtract))
                    link(nc.vector.tensor_tensor(b1[:], eq[:], lo1[:, e, :], ALU.mult))
                    search(b1[:], need[1], thr[1])
                    total(nc.vector.tensor_scalar(above2[:], b1[:], thr[1][:], None, ALU.is_gt, ALU.add,
                                                  accum_out=count[:, 0:1]))()
                    nc.vector.tensor_tensor(need[2][:], need[1][:], tot[:, 0:1], ALU.subtract)
                    ins = nc.vector.tensor_scalar(tied[:], b1[:], thr[1][:], None, ALU.is_equal)
                    ranked(ins, 2 * e + 1)
                    link(nc.vector.scalar_tensor_tensor(eq[:], rank[:], need[2][:], tied[:], ALU.is_lt, ALU.mult))
                    link(nc.vector.tensor_tensor(above[:], above[:], above2[:], ALU.add))
                    link(nc.vector.tensor_tensor(eq[:], eq[:], above[:], ALU.add))
                    ins = nc.vector.tensor_copy(taken[:], eq[:])
                    ranked(ins, 2 * e + 2)
                link(nc.vector.scalar_tensor_tensor(run[:], rank[:], base[:], taken[:], ALU.add, ALU.mult))
                nc.vector.tensor_tensor(place[:], place[:], run[:], ALU.add)
                nc.vector.tensor_tensor(free[:], free[:], taken[:], ALU.subtract)
                link(nc.vector.tensor_scalar(base[:], base[:], float(CAP), None, ALU.add))
                assert last or (step[0] == PER and totals[0] == CNT)

            PER = 6 * DIGITS + 14
            with dve.Fori(0, E - 1) as e:
                expert(e, False)
            expert(E - 1, True)
            nc.vector.tensor_copy(pos[:], place[:]).then_inc(pos_ready, 1)


def expert_ffn(nc, sorted_x, w1_d, b1_d, w2_d, b2_d, ln_g, ln_b, ident_in, sorted_out):
    N, C = sorted_x.shape
    E, _, F = w1_d.shape
    CH = 512
    NT = CH // 128
    NF = F // 128
    U = 4
    TURNS = N // CH // U
    assert N // E == 2 * CH
    x_v = sorted_x.rearrange("(n p t) c -> n p t c", p=128, t=NT)
    o_v = sorted_out.rearrange("(n p t) c -> n p t c", p=128, t=NT)

    with ExitStack() as ctx:
        def sb(name, shape, dt=F32):
            return ctx.enter_context(nc.sbuf_tensor("c_" + name + "_", shape, dt))

        def ps(name, shape):
            return ctx.enter_context(nc.psum_tensor("c_" + name + "_", shape, F32))

        def sem(name):
            return ctx.enter_context(nc.semaphore("c_" + name))

        gamma = sb("gamma", [128, 1])
        beta = sb("beta", [128, 1])
        ident = sb("ident", [128, 128])
        w1 = [sb(f"w1_{k}", [128, F]) for k in range(2)]
        w2 = [sb(f"w2_{k}", [128, NF, C]) for k in range(2)]
        b1 = [sb(f"b1_{k}", [128, NF]) for k in range(2)]
        b2 = [sb(f"b2_{k}", [128, 1]) for k in range(2)]
        xs = [sb(f"xs_{k}", [128, NT, C]) for k in range(U)]
        mv = [sb(f"mv_{k}", [128, NT, 2]) for k in range(U)]
        st = [sb(f"st_{k}", [128, NT, 6]) for k in range(2)]
        rstd = [sb(f"rstd_{k}", [128, NT]) for k in range(U)]
        comb = [sb(f"comb_{k}", [128, NT]) for k in range(U)]
        va = sb("va", [128, NT])
        vb = sb("vb", [128, NT])
        neg_half = sb("neg_half", [128, NT])
        zz = [sb(f"zz_{k}", [128, NT, C]) for k in range(2)]
        z = [sb(f"z_{k}", [128, NT, C]) for k in range(U)]
        hT = [sb(f"hT_{k}", [128, CH]) for k in range(2)]
        gT = [sb(f"gT_{k}", [128, NF, CH]) for k in range(2)]
        yT = sb("yT", [128, CH])
        res = sb("res", [128, NT, C])
        resn = sb("resn", [128, NT, C])
        st2 = sb("st2", [128, NT, 6])
        mv2 = sb("mv2", [128, NT, 2])
        ve2 = sb("ve2", [128, NT])
        rstd2 = sb("rstd2", [128, NT])
        mark = sb("mark", [128, 1])

        in_ps = [ps(f"in_{k}", [128, CH]) for k in range(2)]
        h_ps = [ps(f"h_{k}", [128, CH]) for k in range(2)]
        y_ps = [ps(f"y_{k}", [128, CH]) for k in range(2)]
        back_ps = [ps(f"back_{k}", [128, CH]) for k in range(2)]

        loaded = sem("loaded")
        w_in = [sem(f"w_in{k}") for k in range(2)]
        xs_in = [sem(f"xs_in{k}") for k in range(U)]
        const_set = sem("const_set")
        stat_step = sem("stat_step")
        stats = sem("stats")
        rstd_ready = sem("rstd_ready")
        comb_ready = sem("comb_ready")
        zz_ready = sem("zz_ready")
        turned = sem("turned")
        hT_ready = sem("hT_ready")
        h_done = sem("h_done")
        gelu_done = sem("gelu_done")
        y_done = sem("y_done")
        yT_ready = sem("yT_ready")
        back_done = sem("back_done")
        post_step = sem("post_step")
        var2_ready = sem("var2_ready")
        rstd2_ready = sem("rstd2_ready")
        x2_ready = sem("x2_ready")
        stored = sem("stored")

        def chunks(engine, one):
            for u in range(U):
                one(0, u, u == 0, False)
            with engine.Fori(1, TURNS - 1) as i:
                for u in range(U):
                    one(i, u, False, False)
            for u in range(U):
                one(TURNS - 1, u, False, True)

        block = ctx.enter_context(nc.Block())

        @block.sync
        def _(sp):
            def weights(e, k):
                sp.dma_start(w1[k][:], w1_d[e]).then_inc(w_in[k], 16)
                sp.dma_start(w2[k][:], w2_d[e].rearrange("(f p) c -> p f c", p=128)).then_inc(w_in[k], 16)
                sp.dma_start(b1[k][:], b1_d[e]).then_inc(w_in[k], 16)
                sp.dma_start(b2[k][:], b2_d[e]).then_inc(w_in[k], 16)

            sp.dma_start(xs[0][:], x_v[0]).then_inc(xs_in[0], 16)
            sp.dma_start(xs[1][:], x_v[1]).then_inc(xs_in[1], 16)
            sp.dma_start(gamma[:], ln_g).then_inc(loaded, 16)
            sp.dma_start(beta[:], ln_b).then_inc(loaded, 16)
            sp.dma_start(ident[:], ident_in).then_inc(loaded, 16)
            weights(0, 0)
            for u in range(2, U):
                sp.dma_start(xs[u][:], x_v[u]).then_inc(xs_in[u], 16)
            weights(1, 1)

            def turn(i, last):
                for u in range(U):
                    c = U * i + u
                    if u % 2 and not last:
                        sp.wait_ge(yT_ready, c + 1)
                        weights(2 * (i + 1) + u // 2, u // 2)
                    sp.wait_ge(x2_ready, c + 1)
                    sp.dma_start(o_v[c], xs[u][:]).then_inc(stored, 16)
                    if not last:
                        sp.wait_ge(stored, 16 * (c + 1))
                        sp.dma_start(xs[u][:], x_v[c + U]).then_inc(xs_in[u], 16)

            with sp.Fori(0, TURNS - 1) as i:
                turn(i, False)
            turn(TURNS - 1, True)
            sp.wait_ge(stored, 16 * U * TURNS)

        @block.gpsimd
        def _(pool):
            nc.gpsimd.memset(neg_half[:], -0.5).then_inc(const_set, 1)
            pool.wait_ge(const_set, 1)

            def factors(c, k):
                pool.wait_ge(stats, c + 1)
                nc.gpsimd.tensor_tensor(comb[k][:], vb[:], neg_half[:], ALU.pow).then_inc(comb_ready, 1)
                nc.gpsimd.tensor_tensor(rstd[k][:], va[:], neg_half[:], ALU.pow).then_inc(rstd_ready, 1)

            def factor_of_output(c):
                pool.wait_ge(var2_ready, c + 1)
                nc.gpsimd.tensor_tensor(rstd2[:], ve2[:], neg_half[:], ALU.pow).then_inc(rstd2_ready, 1)

            factors(0, 0)
            factors(1, 1)

            def one(i, u, first, last):
                c = U * i + u
                if not first:
                    factor_of_output(c - 1)
                if not (last and u >= U - 2):
                    factors(c + 2, (u + 2) % U)

            chunks(pool, one)
            factor_of_output(U * TURNS - 1)

        @block.scalar
        def _(act):
            def turn_in(c, k):
                act.wait_ge(turned, c + 1)
                nc.scalar.activation(hT[k % 2][:], in_ps[k % 2][:], ACT.Identity, bias=beta[:],
                                     scale=gamma[:]).then_inc(hT_ready, 1)

            act.wait_ge(loaded, 16 * 3)
            turn_in(0, 0)

            def second(c, u):
                act.wait_ge(y_done, c + 1)
                nc.scalar.activation(yT[:], y_ps[u % 2][:], ACT.Identity, bias=b2[u // 2][:]).then_inc(yT_ready, 1)

            def one(i, u, first, last):
                c = U * i + u
                w = u // 2
                if u % 2 == 0:
                    act.wait_ge(w_in[w], 64 * (i + 1))
                for f in range(NF):
                    act.wait_ge(h_done, NF * c + f + 1)
                    nc.scalar.activation(gT[u % 2][:, f, :], h_ps[f % 2][:], ACT.Gelu_apprx_tanh,
                                         bias=b1[w][:, f:f + 1]).then_inc(gelu_done, 1)
                    if f == 1 and not first:
                        second(c - 1, (u - 1) % U)
                    if f == 2 and not (last and u == U - 1):
                        turn_in(c + 1, u + 1)

            chunks(act, one)
            second(U * TURNS - 1, U - 1)

        @block.vector
        def _(dve):
            def statistics(c, i, k):
                dve.wait_ge(xs_in[k], 16 * (i + 1))
                for t in range(NT):
                    last = nc.vector.bn_stats(st[k % 2][:, t, :], xs[k][:, t, :])
                last.then_inc(stat_step, 1)
                dve.wait_ge(stat_step, 3 * c + 1)
                nc.vector.memset(mark[:], 0.0)
                for t in range(NT):
                    last = nc.vector.bn_aggr(mv[k][:, t, :], st[k % 2][:, t, :])
                last.then_inc(stat_step, 1)
                dve.wait_ge(stat_step, 3 * c + 2)
                if not (isinstance(c, int) and c == 0):
                    dve.wait_ge(rstd_ready, c)
                nc.vector.tensor_scalar(va[:], mv[k][:, :, 1], 1e-5, None, ALU.add).then_inc(stat_step, 1)
                dve.wait_ge(stat_step, 3 * c + 3)
                nc.vector.scalar_tensor_tensor(vb[:], va[:], 1e-5, mv[k][:, :, 1], ALU.mult, ALU.add).then_inc(stats, 1)

            def normalised(c, k):
                dve.wait_ge(comb_ready, c + 1)
                for t in range(NT):
                    last = nc.vector.tensor_scalar(zz[k % 2][:, t, :], xs[k][:, t, :], mv[k][:, t, 0:1],
                                                   comb[k][:, t:t + 1], ALU.subtract, ALU.mult)
                last.then_inc(zz_ready, 1)

            def plain(c, k):
                dve.wait_ge(rstd_ready, c + 1)
                for t in range(NT):
                    nc.vector.tensor_scalar(z[k][:, t, :], xs[k][:, t, :], mv[k][:, t, 0:1],
                                            rstd[k][:, t:t + 1], ALU.subtract, ALU.mult)

            statistics(0, 0, 0)
            statistics(1, 0, 1)
            normalised(0, 0)
            plain(0, 0)
            normalised(1, 1)

            def link(c, k, ins):
                ins.then_inc(post_step, 1)
                dve.wait_ge(post_step, 5 * c + k)

            def output_statistics(c, u):
                dve.wait_ge(back_done, c + 1)
                link(c, 1, nc.vector.tensor_tensor(res[:], z[u][:], back_ps[u % 2][:].rearrange("p (t c) -> p t c", c=C),
                                                   ALU.add))
                for t in range(NT):
                    ins = nc.vector.bn_stats(st2[:, t, :], res[:, t, :])
                link(c, 2, ins)
                nc.vector.memset(mark[:], 0.0)
                for t in range(NT):
                    ins = nc.vector.bn_aggr(mv2[:, t, :], st2[:, t, :])
                link(c, 3, ins)
                nc.vector.tensor_scalar(ve2[:], mv2[:, :, 1], 1e-5, None, ALU.add).then_inc(var2_ready, 1)

            def output(c, u):
                dve.wait_ge(rstd2_ready, c + 1)
                for t in range(NT):
                    ins = nc.vector.tensor_scalar(resn[:, t, :], res[:, t, :], mv2[:, t, 0:1], rstd2[:, t:t + 1],
                                                  ALU.subtract, ALU.mult)
                link(c, 4, ins)
                link(c, 5, nc.vector.tensor_tensor(xs[u][:], resn[:], xs[u][:], ALU.add))
                nc.vector.memset(mark[:], 0.0).then_inc(x2_ready, 1)

            def one(i, u, first, last):
                c = U * i + u
                if not first:
                    output_statistics(c - 1, (u - 1) % U)
                if not (last and u >= U - 2):
                    statistics(c + 2, i + (u + 2) // U, (u + 2) % U)
                if not first:
                    output(c - 1, (u - 1) % U)
                if not (last and u >= U - 2):
                    dve.wait_ge(turned, c + 1)
                    normalised(c + 2, (u + 2) % U)
                if not (last and u == U - 1):
                    plain(c + 1, (u + 1) % U)

            chunks(dve, one)
            output_statistics(U * TURNS - 1, U - 1)
            output(U * TURNS - 1, U - 1)

        @block.tensor
        def _(pe):
            def turn_in(c, k):
                pe.wait_ge(zz_ready, c + 1)
                for t in range(NT):
                    last = nc.tensor.transpose(in_ps[k % 2][:, t * 128:(t + 1) * 128], zz[k % 2][:, t, :], ident[:])
                last.then_inc(turned, 1)

            pe.wait_ge(loaded, 16 * 3)
            turn_in(0, 0)

            def second(c, u):
                for f in range(NF):
                    pe.wait_ge(gelu_done, NF * c + f + 1)
                    ins = nc.tensor.matmul(y_ps[u % 2][:], w2[u // 2][:, f, :], gT[u % 2][:, f, :],
                                           start=f == 0, stop=f == NF - 1)
                ins.then_inc(y_done, 1)

            def turn_back(c, u):
                pe.wait_ge(yT_ready, c + 1)
                if not (isinstance(c, int) and c < 2):
                    pe.wait_ge(post_step, 5 * (c - 2) + 1)
                for t in range(NT):
                    ins = nc.tensor.transpose(back_ps[u % 2][:, t * 128:(t + 1) * 128],
                                              yT[:, t * 128:(t + 1) * 128], ident[:])
                ins.then_inc(back_done, 1)

            def one(i, u, first, last):
                c = U * i + u
                w = u // 2
                if u % 2 == 0:
                    pe.wait_ge(w_in[w], 64 * (i + 1))
                pe.wait_ge(hT_ready, c + 1)
                for f in range(NF):
                    if f >= 2 or not first:
                        pe.wait_ge(gelu_done, NF * c + f - 1)
                    nc.tensor.matmul(h_ps[f % 2][:], w1[w][:, f * 128:(f + 1) * 128], hT[u % 2][:],
                                     start=True, stop=True).then_inc(h_done, 1)
                    if f == 1 and not first:
                        second(c - 1, (u - 1) % U)
                    if f == 2 and not first:
                        turn_back(c - 1, (u - 1) % U)
                    if f == 2 and not (last and u == U - 1):
                        turn_in(c + 1, u + 1)

            chunks(pe, one)
            second(U * TURNS - 1, U - 1)
            turn_back(U * TURNS - 1, U - 1)


def l1_attention(nc, x, pos, sorted_rows, mean, rstd, wqk_d, wv_d, bqk_d, bv_d, wo_d, bo_d, rope_d, ident_in, parts):
    _, TILES, C = x.shape
    NT = 4
    T = NT * 128
    NB = TILES // NT
    HD = 8
    H = C // HD
    GH = 4
    NG = H // GH
    NP = 3
    ROWS = NP * NP * HD
    HC = 32
    MICRO = GH * NT
    PER_S = NG * MICRO
    SHIFT = ROWS
    LEAD = 6
    LAST = NG - 1
    NS = 4
    qp_d, kp_d = parts

    with ExitStack() as ctx:
        def sb(name, shape, dt=F32):
            return ctx.enter_context(nc.sbuf_tensor("d_" + name + "_", shape, dt))

        def ps(name, shape):
            return ctx.enter_context(nc.psum_tensor("d_" + name + "_", shape, F32))

        def sem(name):
            return ctx.enter_context(nc.semaphore("d_" + name))

        wqk = sb("wqk", [128, 4, C])
        wv = sb("wv", [128, C])
        wo = sb("wo", [128, C])
        ones = sb("ones", [H, T], BF16)
        bqk = sb("bqk", [128, 4])
        bv = sb("bv", [128, C])
        bo = sb("bo", [128, C])
        rope = sb("rope", [128, 4, T])
        ident = sb("ident", [128, 128])
        zz = sb("zz", [128, NT, C])
        zT = sb("zT", [128, T])
        prod = sb("prod", [128, 4, T])
        whole = [sb(f"whole{k}", [128, T]) for k in range(2)]
        rest = [sb(f"rest{k}", [128, T]) for k in range(2)]
        part = [sb(f"part{k}", [128, NP, T], BF16) for k in range(2)]
        qs = [sb(f"qs{k}", [SHIFT + 1, H, T], BF16) for k in range(2)]
        ks = [sb(f"ks{k}", [SHIFT + 1, H, T], BF16) for k in range(2)]
        v = [sb(f"v{k}", [128, NT, H, HC]) for k in range(2)]
        nmax = [sb(f"nmax{k}", [128, 32], BF16) for k in range(2)]
        nmaxT = [sb(f"nmaxT{k}", [128, 32], BF16) for k in range(2)]
        pT = [[sb(f"pT{k}_{h}", [128, T]) for h in range(GH)] for k in range(2)]
        oE = sb("oE", [128, T])
        rden = sb("rden", [128, NT, GH])
        quot = sb("quot", [128, NT, C])
        plus = sb("plus", [128, NT, C])
        att = sb("att", [128, NT, C])
        attT = sb("attT", [128, T])
        yb = sb("yb", [128, NT, C])
        yn = sb("yn", [128, NT, C])
        st2 = sb("st2", [128, NT, 6])
        mv2 = sb("mv2", [128, NT, 2])
        ve2 = sb("ve2", [128, NT])
        rstd2 = sb("rstd2", [128, NT])
        neg_half = sb("neg_half", [128, NT])
        st1 = sb("st1", [128, NT, 6])
        mv1 = [sb(f"mv1_{k}", [128, NT, 2]) for k in range(2)]
        ve1 = sb("ve1", [128, NT])
        rstd1 = [sb(f"rstd1_{k}", [128, NT]) for k in range(2)]
        st3 = sb("st3", [128, NT, 6])
        mv3 = sb("mv3", [128, NT, 2])
        ve3 = sb("ve3", [128, NT])
        mark = sb("mark", [128, 1])

        s_ps = [ps(f"s{k}", [128, T]) for k in range(NS)]
        t_ps = [ps(f"t{k}", [128, T]) for k in range(2)]
        o_ps = ps("o", [128, T])
        m_ps = ps("m", [128, T])
        m3 = m_ps[:].rearrange("p (t c) -> p t c", c=C)

        loaded = sem("loaded")
        gather_groups = [range(0, 1), range(1, 2), range(2, NB // 2 + 1), range(NB // 2 + 1, NB)]
        gathered = [sem(f"gathered{k}") for k in range(len(gather_groups))]
        in_step = sem("in_step")
        var1_ready = sem("var1_ready")
        rstd1_ready = sem("rstd1_ready")
        end_step = sem("end_step")
        var3_ready = sem("var3_ready")
        rstd3_ready = sem("rstd3_ready")
        const_set = sem("const_set")
        zz_ready = sem("zz_ready")
        m_done = sem("m_done")
        m_free = sem("m_free")
        whole_ready = sem("whole_ready")
        part1 = sem("part1")
        rest_ready = sem("rest_ready")
        part2 = sem("part2")
        part3 = sem("part3")
        parts_out = sem("parts_out")
        stack_set = sem("stack_set")
        stacked = sem("stacked")
        s_done = sem("s_done")
        max_done = sem("max_done")
        nmaxT_ready = sem("nmaxT_ready")
        shifts_in = sem("shifts_in")
        st_done = sem("st_done")
        exp_done = sem("exp_done")
        av_done = sem("av_done")
        oe_done = sem("oe_done")
        post_step = sem("post_step")
        var2_step = sem("var2_step")
        var2_ready = sem("var2_ready")
        rstd2_ready = sem("rstd2_ready")
        x_done = sem("x_done")
        NLOADS = 8
        NSTACK = NP * NP + NP

        USES = [("turn_in", 0, 0), ("q0", 0, 2), ("q1", 0, 4), ("q2", 0, 6), ("q3", 0, 8), ("out3", 0, 10),
                ("v", 0, 12), ("att", 1, 1), ("y", 1, 5), ("out0", 1, 9), ("out1", 2, 9), ("out2", 3, 9)]
        NEXT, BEFORE = ("turn_in", "q0", "q1", "q2", "q3", "v"), ("out3", "att", "y")

        def m_use(b, what, first=False, last=False):
            used = [u for u, _, _ in USES if not (first and u in BEFORE) and not (last and u in NEXT)]
            return (len(NEXT) if first else len(USES) * b + len(NEXT) - len(BEFORE)) + used.index(what)

        def at(what, g, n):
            return (what, g, n) in USES

        def turns(engine, batch):
            batch(0, 0, True, False)
            batch(1, 1, False, False)
            with engine.Fori(1, NB // 2 - 1) as i:
                for k in range(2):
                    batch(2 * i + k, k, False, False)
            batch(NB - 2, 0, False, False)
            batch(NB - 1, 1, False, True)

        def two_more(b, last):
            return not last and not (isinstance(b, int) and b == NB - 2)

        def ahead(g, n):
            return divmod(MICRO * (g + 1) + n + LEAD, MICRO)

        block = ctx.enter_context(nc.Block())

        @block.sync
        def _(sp):
            for dst, src in ((ident, ident_in), (wqk, wqk_d), (bqk, bqk_d), (rope, rope_d), (wv, wv_d),
                             (wo, wo_d), (bv, bv_d.to_broadcast([128, C])), (bo, bo_d.to_broadcast([128, C]))):
                sp.dma_start(dst[:], src).then_inc(loaded, 16)

            def parts_to_dram(b, k):
                for side, dst in ((0, qp_d), (1, kp_d)):
                    sp.wait_ge(part3, 2 * b + side + 1)
                    sp.dma_start(dst[k].rearrange("n p t -> p n t"), part[side][:]).then_inc(parts_out, 16)

            def stack(b, k):
                sp.wait_ge(parts_out, 32 * (b + 1))
                for a in range(NP):
                    for c in range(NP):
                        r = (NP * a + c) * HD
                        sp.dma_start(qs[k][r:r + HD, :, :],
                                     qp_d[k, a].rearrange("(d h) t -> d h t", h=H)).then_inc(stacked, 16)
                    sp.dma_start(ks[k][NP * HD * a:NP * HD * (a + 1), :, :],
                                 kp_d[k].rearrange("n (d h) t -> (n d) h t", h=H)).then_inc(stacked, 16)

            def shifts(b, k, g):
                sp.wait_ge(nmaxT_ready, NG * b + g + 1)
                for a in range(4):
                    dst = qs[k][SHIFT:SHIFT + 1, GH * g:GH * (g + 1), :].rearrange("o h (t a i) -> o a (h t) i", t=NT, a=4)
                    sp.dma_start(dst[:, a], nmaxT[g % 2][32 * a:32 * a + MICRO, :]).then_inc(shifts_in, 16)

            sp.wait_ge(const_set, 8)
            for k in range(2):
                sp.dma_start(ks[k][SHIFT:SHIFT + 1, :, :], ones[:]).then_inc(stack_set, 16)
            parts_to_dram(0, 0)
            stack(0, 0)
            shifts(0, 0, 0)

            def batch(b, k, first, last):
                shifts(b, k, 1)
                if not last:
                    parts_to_dram(b + 1, 1 - k)
                shifts(b, k, 2)
                if not last:
                    stack(b + 1, 1 - k)
                shifts(b, k, 3)
                if not last:
                    shifts(b + 1, 1 - k, 0)

            turns(sp, batch)

        @block.gpsimd
        def _(pool):
            for t in range(NT):
                pool.indirect_dma_start(out=x[:, t, :], out_offset=None, in_=sorted_rows,
                                        in_offset=bass.IndirectOffsetOnAxis(ap=pos[:, t:t + 1], axis=0)
                                        ).then_inc(gathered[0], 16)
            nc.gpsimd.memset(neg_half[:], -0.5).then_inc(const_set, 1)
            for k in range(2):
                nc.gpsimd.memset(nmax[k][:], 0.0).then_inc(const_set, 1)
                nc.gpsimd.memset(v[k][:], 0.0).then_inc(const_set, 1)
            nc.gpsimd.memset(ones[:], 1.0).then_inc(const_set, 1)
            pool.wait_ge(const_set, 6)
            for k in range(2):
                nc.gpsimd.memset(v[k][:, :, :, HD:HD + 1], 1.0).then_inc(const_set, 1)

            def wholes(b, use):
                for side in range(2):
                    pool.wait_ge(m_free, use + 2 * side + 2)
                    nc.gpsimd.tensor_tensor(whole[side][:], prod[:, 2 * side, :], prod[:, 2 * side + 1, :],
                                            ALU.add).then_inc(whole_ready, 1)

            def rest_parts(b, side):
                pool.wait_ge(part1, 2 * b + side + 1)
                nc.gpsimd.tensor_tensor(rest[side][:], whole[side][:], part[side][:, 0, :],
                                        ALU.subtract).then_inc(rest_ready, 1)
                pool.wait_ge(part2, 2 * b + side + 1)
                nc.gpsimd.tensor_tensor(part[side][:, 2, :], rest[side][:], part[side][:, 1, :],
                                        ALU.subtract).then_inc(part3, 1)

            def wholes_and_parts(b, use):
                wholes(b, use)
                for side in range(2):
                    rest_parts(b, side)

            def sum_of_output(b):
                pool.wait_ge(post_step, 13 * b + 13)
                rows = x[:, bass.ds(NT * b, NT), :]
                nc.gpsimd.tensor_tensor(rows, yn[:], rows, ALU.add).then_inc(x_done, 1)

            def rsqrt_of_output(b):
                pool.wait_ge(var2_ready, b + 1)
                nc.gpsimd.tensor_tensor(rstd2[:], ve2[:], neg_half[:], ALU.pow).then_inc(rstd2_ready, 1)

            def gather(n):
                for t in range(NT * gather_groups[n].start, NT * gather_groups[n].stop):
                    pool.indirect_dma_start(out=x[:, t, :], out_offset=None, in_=sorted_rows,
                                            in_offset=bass.IndirectOffsetOnAxis(ap=pos[:, t:t + 1], axis=0)
                                            ).then_inc(gathered[n], 16)

            def rsqrt_of_input(b, k):
                pool.wait_ge(var1_ready, b + 1)
                nc.gpsimd.tensor_tensor(rstd1[k][:], ve1[:], neg_half[:], ALU.pow).then_inc(rstd1_ready, 1)

            def rsqrt_of_sum(b):
                pool.wait_ge(var3_ready, b + 1)
                nc.gpsimd.tensor_tensor(rstd[:, bass.ds(NT * b, NT)], ve3[:], neg_half[:], ALU.pow).then_inc(rstd3_ready, 1)

            rsqrt_of_input(0, 0)
            gather(1)
            wholes(0, 1)
            rsqrt_of_input(1, 1)

            def batch(b, k, first, last):
                if not last:
                    wholes_and_parts(b + 1, m_use(b, "q0", first))
                if not first:
                    rsqrt_of_output(b - 1)
                    sum_of_output(b - 1)
                if isinstance(b, int) and b < 2:
                    gather(b + 2)
                if not first:
                    rsqrt_of_sum(b - 1)
                if two_more(b, last):
                    rsqrt_of_input(b + 2, k)

            turns(pool, batch)
            rsqrt_of_output(NB - 1)
            sum_of_output(NB - 1)
            rsqrt_of_sum(NB - 1)
            pool.wait_ge(rstd3_ready, NB)

        @block.scalar
        def _(act):
            act.wait_ge(loaded, 16 * NLOADS)

            def turned(use):
                act.wait_ge(m_done, use + 1)
                nc.scalar.copy(zT[:], m_ps[:]).then_inc(m_free, 1)

            def first_part(b, side):
                act.wait_ge(whole_ready, 2 * b + side + 1)
                nc.scalar.copy(part[side][:, 0, :], whole[side][:]).then_inc(part1, 1)

            def second_part(b, side):
                act.wait_ge(rest_ready, 2 * b + side + 1)
                nc.scalar.copy(part[side][:, 1, :], rest[side][:]).then_inc(part2, 1)

            turned(0)
            for side in range(2):
                first_part(0, side)
                second_part(0, side)

            def out_copy(b, g, free):
                act.wait_ge(av_done, NG * NT * b + NT * (g + 1))
                if free is not None:
                    act.wait_ge(m_done, free + 1)
                nc.scalar.copy(oE[:], o_ps[:]).then_inc(oe_done, 1)

            def output_turned(use):
                act.wait_ge(m_done, use + 1)
                nc.scalar.copy(attT[:], m_ps[:]).then_inc(m_free, 1)

            def batch(b, k, first, last):
                use = lambda what: m_use(b, what, first, last)
                for g in range(NG):
                    for n in range(MICRO):
                        kt, h = divmod(n, GH)
                        if h == 0 and not (first and (g, kt) < (0, 2)):
                            act.wait_ge(av_done, NG * NT * b + NT * g + kt - 1)
                        act.wait_ge(st_done, PER_S * b + MICRO * g + n + 1)
                        nc.scalar.activation(pT[kt % 2][h][:], t_ps[n % 2][:], ACT.Exp).then_inc(exp_done, 1)
                        if n == 4 and g == 0 and not first:
                            out_copy(b - 1, LAST, use("turn_in") - 1 if not last else use("out3") - 1)
                        if n == 4 and g:
                            free = use(f"out{(g - 2) % NG}") if g > 1 or not first else None
                            out_copy(b, g - 1, free)
                        if at("att", g, n - 1) and not first:
                            output_turned(use("att"))
                        if not last:
                            if at("turn_in", g, n - 1):
                                turned(use("turn_in"))
                            if (g, n) == (0, 8):
                                first_part(b + 1, 0)
                            if (g, n) == (0, 10):
                                second_part(b + 1, 0)
                            if (g, n) == (0, 13):
                                first_part(b + 1, 1)
                            if (g, n) == (1, 0):
                                second_part(b + 1, 1)

            turns(act, batch)
            over = m_use(NB - 1, "out2", last=True) + 1
            out_copy(NB - 1, LAST, over - 1)
            output_turned(over + 1)

        @block.vector
        def _(dve):
            def statistics_of(rows, st, mv, ve, step, done, n):
                for t in range(NT):
                    ins = nc.vector.bn_stats(st[:, t, :], rows(t))
                ins.then_inc(step, 1)
                dve.wait_ge(step, 2 * n + 1)
                nc.vector.memset(mark[:], 0.0)
                for t in range(NT):
                    ins = nc.vector.bn_aggr(mv[:, t, :], st[:, t, :])
                ins.then_inc(step, 1)
                dve.wait_ge(step, 2 * n + 2)
                nc.vector.tensor_scalar(ve[:], mv[:, :, 1], 1e-5, None, ALU.add).then_inc(done, 1)

            def input_statistics(b, k):
                if not (isinstance(b, int) and b == 0):
                    dve.wait_ge(rstd1_ready, b)
                statistics_of(lambda t: x[:, NT * b + t, :], st1, mv1[k], ve1, in_step, var1_ready, b)

            def sum_statistics(b):
                dve.wait_ge(x_done, b + 1)
                if not (isinstance(b, int) and b == 0):
                    dve.wait_ge(rstd3_ready, b)
                statistics_of(lambda t: x[:, NT * b + t, :], st3, mv3, ve3, end_step, var3_ready, b)
                nc.vector.tensor_scalar(mean[:, bass.ds(NT * b, NT)], mv3[:, :, 0], 1.0, None, ALU.mult)

            def normalised(b, k):
                dve.wait_ge(rstd1_ready, b + 1)
                for t in range(NT):
                    last = nc.vector.tensor_scalar(zz[:, t, :], x[:, NT * b + t, :], mv1[k][:, t, 0:1],
                                                   rstd1[k][:, t:t + 1], ALU.subtract, ALU.mult)
                last.then_inc(zz_ready, 1)

            def rotary(b, c, use, bank):
                dve.wait_ge(m_done, use + 1)
                nc.vector.scalar_tensor_tensor(prod[:, c, :], bank[:], bqk[:, c:c + 1], rope[:, c, :],
                                               ALU.add, ALU.mult).then_inc(m_free, 1)

            def values(b, k, use):
                dve.wait_ge(m_done, use + 1)
                nc.vector.tensor_tensor(v[k][:, :, :, 0:HD], m_ps[:].rearrange("p (t h d) -> p t h d", t=NT, h=H),
                                        bv[:].rearrange("p (o h d) -> p o h d", o=1, h=H).to_broadcast([128, NT, H, HD]),
                                        ALU.add).then_inc(m_free, 1)

            def maximum(b, g, n):
                h, qt = divmod(n, NT)
                dve.wait_ge(s_done, PER_S * b + MICRO * g + n + 1)
                nc.vector.reduce_max(nmax[g % 2][:, n:n + 1], s_ps[n % NS][:], AX_X, negate=True).then_inc(max_done, 1)
                if n == MICRO - 1:
                    if not (isinstance(b, int) and NG * b + g < 2):
                        dve.wait_ge(shifts_in, 64 * (NG * b + g - 1))
                    dve.wait_ge(max_done, PER_S * b + MICRO * (g + 1))
                    nc.vector.transpose(nmaxT[g % 2][:], nmax[g % 2][:]).then_inc(nmaxT_ready, 1)

            def quotients(b, g, use):
                dve.wait_ge(m_done, use + 1)
                got = m_ps[:].rearrange("p (t h c) -> p t h c", t=NT, c=HC)
                cols = slice(g * GH * HD, (g + 1) * GH * HD)
                nc.vector.reciprocal(rden[:], got[:, :, :, HD]).then_inc(post_step, 1)
                dve.wait_ge(post_step, 13 * b + 3 * g + 1)
                nc.vector.tensor_tensor(quot[:, :, cols].rearrange("p t (h d) -> p t h d", d=HD), got[:, :, :, 0:HD],
                                        rden[:].rearrange("p t (h o) -> p t h o", o=1).to_broadcast([128, NT, GH, HD]),
                                        ALU.mult).then_inc(m_free, 1)
                dve.wait_ge(m_free, use + 1)
                nc.vector.tensor_scalar(plus[:, :, cols], quot[:, :, cols], 0.0, None, ALU.max).then_inc(post_step, 1)
                dve.wait_ge(post_step, 13 * b + 3 * g + 2)
                nc.vector.scalar_tensor_tensor(att[:, :, cols], quot[:, :, cols], 0.0, plus[:, :, cols],
                                               ALU.min, ALU.add).then_inc(post_step, 1)

            def output_statistics(b, use):
                dve.wait_ge(m_done, use + 1)
                nc.vector.tensor_tensor(yb[:], m3, bo[:].rearrange("p (o c) -> p o c", o=1).to_broadcast([128, NT, C]),
                                        ALU.add).then_inc(m_free, 1)
                dve.wait_ge(m_free, use + 1)
                for t in range(NT):
                    ins = nc.vector.bn_stats(st2[:, t, :], yb[:, t, :])
                ins.then_inc(var2_step, 1)
                dve.wait_ge(var2_step, 2 * b + 1)
                nc.vector.memset(mark[:], 0.0)
                for t in range(NT):
                    ins = nc.vector.bn_aggr(mv2[:, t, :], st2[:, t, :])
                ins.then_inc(var2_step, 1)
                dve.wait_ge(var2_step, 2 * b + 2)
                nc.vector.tensor_scalar(ve2[:], mv2[:, :, 1], 1e-5, None, ALU.add).then_inc(var2_ready, 1)

            def output(b):
                if not (isinstance(b, int) and b == 0):
                    dve.wait_ge(x_done, b)
                dve.wait_ge(rstd2_ready, b + 1)
                for t in range(NT):
                    ins = nc.vector.tensor_scalar(yn[:, t, :], yb[:, t, :], mv2[:, t, 0:1], rstd2[:, t:t + 1],
                                                  ALU.subtract, ALU.mult)
                ins.then_inc(post_step, 1)

            dve.wait_ge(loaded, 16 * NLOADS)
            dve.wait_ge(gathered[0], 16 * NT)
            input_statistics(0, 0)
            normalised(0, 0)
            for c in range(4):
                rotary(0, c, 1 + c, s_ps[c])
            for side in range(2):
                dve.wait_ge(part1, side + 1)
                nc.vector.tensor_tensor(rest[side][:], whole[side][:], part[side][:, 0, :],
                                        ALU.subtract).then_inc(rest_ready, 1)
                dve.wait_ge(part2, side + 1)
                nc.vector.tensor_tensor(part[side][:, 2, :], rest[side][:], part[side][:, 1, :],
                                        ALU.subtract).then_inc(part3, 1)
            dve.wait_ge(const_set, 8)
            values(0, 0, 5)
            dve.wait_ge(gathered[1], 16 * NT)
            input_statistics(1, 1)
            dve.wait_ge(m_done, 1)
            normalised(1, 1)
            for n in range(MICRO + LEAD):
                maximum(0, n // MICRO, n % MICRO)

            def batch(b, k, first, last):
                use = lambda what: m_use(b, what, first, last)
                for g in range(NG):
                    for n in range(MICRO):
                        g1, n1 = ahead(g, n)
                        if g1 < NG:
                            maximum(b, g1, n1)
                        elif not last:
                            maximum(b + 1, g1 - NG, n1)
                        if g and at(f"out{g - 1}", g, n):
                            quotients(b, g - 1, use(f"out{g - 1}"))
                        if not first:
                            if at("out3", g, n):
                                quotients(b - 1, LAST, use("out3"))
                            if at("y", g, n):
                                output_statistics(b - 1, use("y"))
                            if at("y", g, n - 3):
                                output(b - 1)
                            if (g, n) == (2, 3):
                                sum_statistics(b - 1)
                        if (g, n) == (3, 4) and two_more(b, last):
                            if isinstance(b, int) and b < 2:
                                dve.wait_ge(gathered[b + 2], 16 * NT * len(gather_groups[b + 2]))
                            input_statistics(b + 2, k)
                        if (g, n) == (3, 9) and two_more(b, last):
                            normalised(b + 2, k)
                        if not last:
                            for c in range(4):
                                if at(f"q{c}", g, n):
                                    rotary(b + 1, c, use(f"q{c}"), m_ps)
                            if at("v", g, n):
                                values(b + 1, 1 - k, use("v"))

            turns(dve, batch)
            over = m_use(NB - 1, "out2", last=True) + 1
            quotients(NB - 1, LAST, over)
            output_statistics(NB - 1, over + 2)
            output(NB - 1)
            sum_statistics(NB - 1)

        @block.tensor
        def _(pe):
            def m_ready(use):
                if not (isinstance(use, int) and use == 0):
                    pe.wait_ge(m_free, use)

            def turn_in(b, use):
                pe.wait_ge(zz_ready, b + 1)
                m_ready(use)
                for t in range(NT):
                    ins = nc.tensor.transpose(m_ps[:, t * 128:(t + 1) * 128], zz[:, t, :], ident[:])
                ins.then_inc(m_done, 1)

            def project(c, use):
                m_ready(use)
                nc.tensor.matmul(m_ps[:], wqk[:, c, :], zT[:], start=True, stop=True).then_inc(m_done, 1)

            def project_v(use):
                m_ready(use)
                for t in range(NT):
                    ins = nc.tensor.matmul(m_ps[:, t * C:(t + 1) * C], zT[:, t * 128:(t + 1) * 128], wv[:],
                                           start=True, stop=True)
                ins.then_inc(m_done, 1)

            def scores(b, k, g, n):
                h, qt = divmod(n, NT)
                h += g * GH
                step = PER_S * b + MICRO * g + n
                if not (isinstance(step, int) and step < NS):
                    pe.wait_ge(max_done, step - NS + 1)
                nc.tensor.matmul(s_ps[n % NS][:], qs[k][0:ROWS, h, qt * 128:(qt + 1) * 128], ks[k][0:ROWS, h, :],
                                 start=True, stop=True).then_inc(s_done, 1)

            def shifted(b, k, g, n, first):
                kt, h = divmod(n, GH)
                if not (first and (g, n) < (0, 2)):
                    pe.wait_ge(exp_done, PER_S * b + MICRO * g + n - 1)
                if n == 0:
                    pe.wait_ge(shifts_in, 64 * (NG * b + g + 1))
                hh = g * GH + h
                nc.tensor.matmul(t_ps[n % 2][:], ks[k][:, hh, kt * 128:(kt + 1) * 128], qs[k][:, hh, :],
                                 start=True, stop=True).then_inc(st_done, 1)

            def weighted(b, k, g, kt, first):
                pe.wait_ge(exp_done, PER_S * b + MICRO * g + GH * (kt + 1))
                if kt == 0 and not (first and g == 0):
                    pe.wait_ge(oe_done, NG * b + g)
                for h in range(GH):
                    ins = nc.tensor.matmul(o_ps[HC * h:HC * (h + 1), :], v[k][:, kt, g * GH + h, :], pT[kt % 2][h][:],
                                           start=kt == 0, stop=kt == NT - 1)
                ins.then_inc(av_done, 1)

            def turn_out(b, g, use):
                m_ready(use)
                pe.wait_ge(oe_done, NG * b + g + 1)
                for t in range(NT):
                    ins = nc.tensor.transpose(m_ps[:, t * 128:(t + 1) * 128], oE[:, t * 128:(t + 1) * 128], ident[:])
                ins.then_inc(m_done, 1)

            def turn_attention(b, use):
                m_ready(use)
                pe.wait_ge(post_step, 13 * b + 12)
                for t in range(NT):
                    ins = nc.tensor.transpose(m_ps[:, t * 128:(t + 1) * 128], att[:, t, :], ident[:])
                ins.then_inc(m_done, 1)

            def project_out(use):
                m_ready(use)
                for t in range(NT):
                    ins = nc.tensor.matmul(m_ps[:, t * C:(t + 1) * C], attT[:, t * 128:(t + 1) * 128], wo[:],
                                           start=True, stop=True)
                ins.then_inc(m_done, 1)

            pe.wait_ge(loaded, 16 * NLOADS)
            turn_in(0, 0)
            pe.wait_ge(m_free, 1)
            for c in range(4):
                nc.tensor.matmul(s_ps[c][:], wqk[:, c, :], zT[:], start=True, stop=True).then_inc(m_done, 1)
            project_v(5)
            pe.wait_ge(const_set, 8)
            pe.wait_ge(stack_set, 32)
            pe.wait_ge(stacked, 16 * NSTACK)
            for n in range(MICRO + LEAD):
                scores(0, 0, n // MICRO, n % MICRO)

            def batch(b, k, first, last):
                use = lambda what: m_use(b, what, first, last)
                for g in range(NG):
                    for n in range(MICRO):
                        g1, n1 = ahead(g, n)
                        if g1 < NG:
                            scores(b, k, g1, n1)
                        elif not last:
                            if (g1, n1) == (NG, 0):
                                pe.wait_ge(stacked, 16 * NSTACK * (b + 2))
                            scores(b + 1, 1 - k, g1 - NG, n1)
                        shifted(b, k, g, n, first)
                        if n % GH == GH - 1 and n > GH:
                            weighted(b, k, g, n // GH - 1, first)
                        if n == GH - 1 and g:
                            weighted(b, k, g - 1, NT - 1, first)
                        if n == GH - 1 and g == 0 and not first:
                            weighted(b - 1, 1 - k, LAST, NT - 1, False)
                        if g and at(f"out{g - 1}", g, n):
                            turn_out(b, g - 1, use(f"out{g - 1}"))
                        if not first:
                            if at("out3", g, n):
                                turn_out(b - 1, LAST, use("out3"))
                            if at("att", g, n):
                                turn_attention(b - 1, use("att"))
                            if at("y", g, n):
                                project_out(use("y"))
                        if not last:
                            if at("turn_in", g, n):
                                turn_in(b + 1, use("turn_in"))
                            for c in range(4):
                                if at(f"q{c}", g, n):
                                    project(c, use(f"q{c}"))
                            if at("v", g, n):
                                project_v(use("v"))

            turns(pe, batch)
            over = m_use(NB - 1, "out2", last=True) + 1
            weighted(NB - 1, 1, LAST, NT - 1, False)
            turn_out(NB - 1, LAST, over)
            turn_attention(NB - 1, over + 1)
            project_out(over + 2)


def l1_ffn(nc, x, mean, rstd, w1_d, b1_d, phase_d, real_d, imag_d, w2_d, b2_d, ident_in, out):
    _, TILES, C = x.shape
    NT = 4
    CH = NT * 128
    NCH = TILES // NT
    F = w1_d.shape[1]
    NF = F // 128
    U = 2
    TURNS = NCH // U
    INV = 1.0 / (2 * np.pi)
    MAGIC = 1.5 * 2.0 ** 23
    P1 = 6.28125
    P2 = float(np.float32(int((2 * np.pi - P1) * 2 ** 21) / 2 ** 21))
    P3 = float(np.float32(2 * np.pi - P1 - P2))
    TURN = 6.283185
    out_v = out.rearrange("(n t p) c -> n p t c", p=128, t=NT)

    with ExitStack() as ctx:
        def sb(name, shape, dt=F32):
            return ctx.enter_context(nc.sbuf_tensor("e_" + name + "_", shape, dt))

        def ps(name, shape):
            return ctx.enter_context(nc.psum_tensor("e_" + name + "_", shape, F32))

        def sem(name):
            return ctx.enter_context(nc.semaphore("e_" + name))

        w1 = sb("w1", [128, F])
        w2 = sb("w2", [128, NF, C])
        b1 = sb("b1", [128, NF])
        b2 = sb("b2", [128, 1])
        phase = sb("phase", [128, NF])
        real = sb("real", [128, NF])
        imag = sb("imag", [128, NF])
        ident = sb("ident", [128, 128])
        kk = sb("kk", [128, NF])
        red = [sb(f"red{k}", [128, NF]) for k in range(2)]
        theta = sb("theta", [128, NF])
        quarter = sb("quarter", [128, NF])
        whole = sb("whole", [128, NF])
        cosine = sb("cosine", [128, NF])
        sine = sb("sine", [128, NF])
        qa = sb("qa", [128, NF])
        qb = sb("qb", [128, NF])
        gain = sb("gain", [128, NF])
        offset = sb("offset", [128, NF])
        zz = [sb(f"zz{k}", [128, NT, C]) for k in range(U)]
        zT = [sb(f"zT{k}", [128, CH]) for k in range(U)]
        turns = [sb(f"turns{k}", [128, CH]) for k in range(NF)]
        near = [sb(f"near{k}", [128, CH]) for k in range(2)]
        frac = [sb(f"frac{k}", [128, CH]) for k in range(2)]
        sn = [sb(f"sn{k}", [128, CH]) for k in range(2)]
        pre = [sb(f"pre{k}", [128, CH]) for k in range(2)]
        gT = [sb(f"gT{k}", [128, NF, CH]) for k in range(2)]
        yT = sb("yT", [128, CH])
        yn = [sb(f"yn{k}", [128, NT, C]) for k in range(U)]
        xo = [sb(f"xo{k}", [128, NT, C]) for k in range(U)]
        st2 = sb("st2", [128, NT, 6])
        mv2 = sb("mv2", [128, NT, 2])
        ve2 = sb("ve2", [128, NT])
        rstd2 = sb("rstd2", [128, NT])
        neg_half = sb("neg_half", [128, NT])
        mark = sb("mark", [128, 1])

        in_ps = ps("in", [128, CH])
        h_ps = [ps(f"h{k}", [128, CH]) for k in range(NF)]
        y_ps = ps("y", [128, CH])
        back_ps = ps("back", [128, CH])

        loaded = sem("loaded")
        const_set = sem("const_set")
        chain = sem("chain")
        angles = sem("angles")
        sines = sem("sines")
        factors = sem("factors")
        zz_ready = sem("zz_ready")
        turned = sem("turned")
        zT_ready = sem("zT_ready")
        h_done = sem("h_done")
        turns_ready = sem("turns_ready")
        near_ready = sem("near_ready")
        frac_ready = sem("frac_ready")
        sin_ready = sem("sin_ready")
        pre_ready = sem("pre_ready")
        relu_done = sem("relu_done")
        y_done = sem("y_done")
        yT_ready = sem("yT_ready")
        back_done = sem("back_done")
        post_step = sem("post_step")
        var2_ready = sem("var2_ready")
        rstd2_ready = sem("rstd2_ready")
        x_ready = sem("x_ready")
        stored = [sem(f"stored{k}") for k in range(U)]
        NLOADS = 8

        def chunks(engine, one):
            for u in range(U):
                one(0, u, u == 0, False)
            with engine.Fori(1, TURNS - 1) as i:
                for u in range(U):
                    one(i, u, False, False)
            for u in range(U):
                one(TURNS - 1, u, False, u == U - 1)

        block = ctx.enter_context(nc.Block())

        @block.sync
        def _(sp):
            for dst, src in ((ident, ident_in), (w1, w1_d), (phase, phase_d), (b1, b1_d), (real, real_d), (imag, imag_d),
                             (b2, b2_d), (w2, w2_d.rearrange("(f p) c -> p f c", p=128))):
                sp.dma_start(dst[:], src).then_inc(loaded, 16)
            with sp.Fori(0, TURNS) as i:
                for u in range(U):
                    c = U * i + u
                    sp.wait_ge(x_ready, c + 1)
                    sp.dma_start(out_v[c], xo[u][:]).then_inc(stored[u], 16)
            for u in range(U):
                sp.wait_ge(stored[u], 16 * TURNS)

        @block.gpsimd
        def _(pool):
            nc.gpsimd.memset(neg_half[:], -0.5).then_inc(const_set, 1)
            pool.wait_ge(const_set, 1)
            def one(i, u, first, last):
                c = U * i + u
                pool.wait_ge(var2_ready, c + 1)
                nc.gpsimd.tensor_tensor(rstd2[:], ve2[:], neg_half[:], ALU.pow).then_inc(rstd2_ready, 1)
                if not (isinstance(i, int) and i == 0):
                    pool.wait_ge(stored[u], 16 * i)
                pool.wait_ge(post_step, 3 * c + 4)
                nc.gpsimd.tensor_tensor(xo[u][:], yn[u][:], x[:, bass.ds(NT * c, NT), :], ALU.add).then_inc(x_ready, 1)

            chunks(pool, one)

        @block.scalar
        def _(act):
            act.wait_ge(angles, 1)
            nc.scalar.activation(sine[:], theta[:], ACT.Sin, scale=TURN)
            nc.scalar.activation(cosine[:], quarter[:], ACT.Sin, scale=TURN).then_inc(sines, 1)

            def turn_in(c, k):
                act.wait_ge(turned, c + 1)
                nc.scalar.activation(zT[k][:], in_ps[:], ACT.Copy).then_inc(zT_ready, 1)

            turn_in(0, 0)
            act.wait_ge(factors, 1)

            def second(c):
                act.wait_ge(y_done, c + 1)
                nc.scalar.activation(yT[:], y_ps[:], ACT.Identity, bias=b2[:]).then_inc(yT_ready, 1)

            def one(i, u, first, last):
                c = U * i + u

                def angle(f):
                    act.wait_ge(h_done, NF * c + f + 1)
                    nc.scalar.activation(turns[f][:], h_ps[f][:], ACT.Identity, bias=offset[:, f:f + 1],
                                         scale=0.1 * INV).then_inc(turns_ready, 1)

                def sin(f):
                    act.wait_ge(frac_ready, NF * c + f + 1)
                    nc.scalar.activation(sn[f % 2][:], frac[f % 2][:], ACT.Sin, scale=TURN).then_inc(sin_ready, 1)

                def relu(f):
                    act.wait_ge(pre_ready, NF * c + f + 1)
                    nc.scalar.activation(gT[u][:, f, :], pre[f % 2][:], ACT.Relu, bias=b1[:, f:f + 1]).then_inc(relu_done, 1)

                angle(0)
                for f in range(NF + 2):
                    if f + 1 < NF:
                        angle(f + 1)
                    if 1 <= f <= NF:
                        sin(f - 1)
                    if f >= 2:
                        relu(f - 2)
                    if f == NF - 1 and not first:
                        second(c - 1)
                    if f == NF and not last:
                        turn_in(c + 1, 1 - u)

            chunks(act, one)
            second(NCH - 1)

        @block.vector
        def _(dve):
            chained = [0]

            def link(ins):
                chained[0] += 1
                ins.then_inc(chain, 1)
                dve.wait_ge(chain, chained[0])

            def normalised(c, k):
                for t in range(NT):
                    n = NT * c + t
                    ins = nc.vector.tensor_scalar(zz[k][:, t, :], x[:, n, :], mean[:, bass.ds(n, 1)],
                                                  rstd[:, bass.ds(n, 1)], ALU.subtract, ALU.mult)
                ins.then_inc(zz_ready, 1)

            nc.vector.memset(whole[:], 0.0).then_inc(post_step, 1)
            normalised(0, 0)
            dve.wait_ge(loaded, 16 * NLOADS)
            link(nc.vector.tensor_scalar(kk[:], phase[:], INV, MAGIC, ALU.mult, ALU.add))
            link(nc.vector.tensor_scalar(kk[:], kk[:], MAGIC, None, ALU.subtract))
            link(nc.vector.scalar_tensor_tensor(red[0][:], kk[:], -P1, phase[:], ALU.mult, ALU.add))
            link(nc.vector.scalar_tensor_tensor(red[1][:], kk[:], -P2, red[0][:], ALU.mult, ALU.add))
            link(nc.vector.scalar_tensor_tensor(red[0][:], kk[:], -P3, red[1][:], ALU.mult, ALU.add))
            link(nc.vector.tensor_scalar(red[1][:], red[0][:], INV, None, ALU.mult))
            link(nc.vector.tensor_scalar(kk[:], red[1][:], MAGIC, MAGIC, ALU.add, ALU.subtract))
            link(nc.vector.tensor_tensor(theta[:], red[1][:], kk[:], ALU.subtract))
            link(nc.vector.tensor_scalar(quarter[:], theta[:], 0.25, None, ALU.add))
            link(nc.vector.tensor_scalar(whole[:], quarter[:], MAGIC, MAGIC, ALU.add, ALU.subtract))
            nc.vector.tensor_tensor(quarter[:], quarter[:], whole[:], ALU.subtract).then_inc(angles, 1)
            dve.wait_ge(sines, 1)
            nc.vector.tensor_tensor(qa[:], cosine[:], real[:], ALU.mult)
            link(nc.vector.tensor_tensor(qb[:], sine[:], imag[:], ALU.mult))
            link(nc.vector.tensor_tensor(qa[:], qa[:], qb[:], ALU.add))
            link(nc.vector.scalar_tensor_tensor(gain[:], qa[:], 0.1, imag[:], ALU.mult, ALU.mult))
            nc.vector.scalar_tensor_tensor(offset[:], b1[:], 0.1 * INV, theta[:], ALU.mult, ALU.add).then_inc(factors, 1)
            dve.wait_ge(factors, 1)

            def output_statistics(c):
                dve.wait_ge(back_done, c + 1)
                for t in range(NT):
                    ins = nc.vector.bn_stats(st2[:, t, :], back_ps[:, t * 128:(t + 1) * 128])
                ins.then_inc(post_step, 1)
                dve.wait_ge(post_step, 3 * c + 2)
                nc.vector.memset(kk[:], 0.0)
                for t in range(NT):
                    ins = nc.vector.bn_aggr(mv2[:, t, :], st2[:, t, :])
                ins.then_inc(post_step, 1)
                dve.wait_ge(post_step, 3 * c + 3)
                nc.vector.tensor_scalar(ve2[:], mv2[:, :, 1], 1e-5, None, ALU.add).then_inc(var2_ready, 1)

            def output(c, u):
                if not (isinstance(c, int) and c < 2):
                    dve.wait_ge(x_ready, c - 1)
                dve.wait_ge(rstd2_ready, c + 1)
                for t in range(NT):
                    ins = nc.vector.tensor_scalar(yn[u][:, t, :], back_ps[:, t * 128:(t + 1) * 128], mv2[:, t, 0:1],
                                                  rstd2[:, t:t + 1], ALU.subtract, ALU.mult)
                ins.then_inc(post_step, 1)

            def one(i, u, first, last):
                c = U * i + u

                def fraction(f):
                    k = f % 2
                    dve.wait_ge(turns_ready, NF * c + f + 1)
                    nc.vector.tensor_scalar(near[k][:], turns[f][:], MAGIC, MAGIC, ALU.add,
                                            ALU.subtract).then_inc(near_ready, 1)
                    dve.wait_ge(near_ready, NF * c + f + 1)
                    nc.vector.tensor_tensor(frac[k][:], turns[f][:], near[k][:], ALU.subtract).then_inc(frac_ready, 1)

                def combine(f):
                    dve.wait_ge(sin_ready, NF * c + f + 1)
                    nc.vector.scalar_tensor_tensor(pre[f % 2][:], sn[f % 2][:], gain[:, f:f + 1], h_ps[f][:],
                                                   ALU.mult, ALU.add).then_inc(pre_ready, 1)

                if not last:
                    normalised(c + 1, 1 - u)
                for f in range(NF + 1):
                    if f < NF:
                        fraction(f)
                    if f:
                        combine(f - 1)
                if not first:
                    output_statistics(c - 1)
                if not first:
                    output(c - 1, 1 - u)

            chunks(dve, one)
            output_statistics(NCH - 1)
            output(NCH - 1, 1)

        @block.tensor
        def _(pe):
            def turn_in(c, k):
                pe.wait_ge(zz_ready, c + 1)
                for t in range(NT):
                    ins = nc.tensor.transpose(in_ps[:, t * 128:(t + 1) * 128], zz[k][:, t, :], ident[:])
                ins.then_inc(turned, 1)

            pe.wait_ge(loaded, 16 * NLOADS)
            turn_in(0, 0)

            def second(c, u):
                if not (isinstance(c, int) and c == 0):
                    pe.wait_ge(yT_ready, c)
                for f in range(NF):
                    pe.wait_ge(relu_done, NF * c + f + 1)
                    ins = nc.tensor.matmul(y_ps[:], w2[:, f, :], gT[u][:, f, :], start=f == 0, stop=f == NF - 1)
                ins.then_inc(y_done, 1)

            def turn_back(c):
                pe.wait_ge(yT_ready, c + 1)
                pe.wait_ge(post_step, 3 * c + 1)
                for t in range(NT):
                    ins = nc.tensor.transpose(back_ps[:, t * 128:(t + 1) * 128], yT[:, t * 128:(t + 1) * 128], ident[:])
                ins.then_inc(back_done, 1)

            def one(i, u, first, last):
                c = U * i + u

                pe.wait_ge(zT_ready, c + 1)
                for f in range(NF):
                    if not first:
                        pe.wait_ge(pre_ready, NF * (c - 1) + f + 1)
                    nc.tensor.matmul(h_ps[f][:], w1[:, f * 128:(f + 1) * 128], zT[u][:],
                                     start=True, stop=True).then_inc(h_done, 1)
                if not first:
                    second(c - 1, 1 - u)
                if not last:
                    turn_in(c + 1, 1 - u)
                if not first:
                    turn_back(c - 1)

            chunks(pe, one)
            second(NCH - 1, 1)
            turn_back(NCH - 1)


def program(nc, a, out, B, T, C):
    TILES = B * T // 128
    sorted_x = nc.dram_tensor("sorted_x", (B * T, C), F32).ap()
    sorted_x2 = nc.dram_tensor("sorted_x2", (B * T, C), F32).ap()
    q_parts = nc.dram_tensor("q_parts", (2, 3, C, T), BF16).ap()
    k_parts = nc.dram_tensor("k_parts", (2, 3, C, T), BF16).ap()
    with ExitStack() as ctx:
        x = ctx.enter_context(nc.sbuf_tensor("x_tokens", [128, TILES, C], F32))
        pos = ctx.enter_context(nc.sbuf_tensor("pos", [128, TILES], I32))
        mean = ctx.enter_context(nc.sbuf_tensor("mean", [128, TILES], F32))
        comb = ctx.enter_context(nc.sbuf_tensor("comb", [128, TILES], F32))
        rstd = ctx.enter_context(nc.sbuf_tensor("rstd", [128, TILES], F32))
        l0_attention(nc, a["x"], a["l0_w"], a["l0_wo"], a["l0_rope"], a["l0_masks_q"], a["l0_masks_k"], a["ident"], x,
                     mean, comb)
        routing(nc, x, pos, mean, comb, a["centroids"], a["ln_g"], a["ln_b"], a["ident"], a["ones"], a["before"], sorted_x)
        expert_ffn(nc, sorted_x, a["e_w1"], a["e_b1"], a["e_w2"], a["e_b2"], a["ln_g"], a["ln_b"], a["ident"], sorted_x2)
        l1_attention(nc, x, pos, sorted_x2, mean, rstd, a["l1_wqk"], a["l1_wv"], a["l1_bqk"], a["l1_bv"], a["l1_wo"], a["l1_bo"],
                     a["l1_rope"], a["ident"], (q_parts, k_parts))
        l1_ffn(nc, x, mean, rstd, a["f_w1"], a["f_b1"], a["f_phase"], a["f_real"], a["f_imag"], a["f_w2"], a["f_b2"],
               a["ident"], out)


def l0_constants(T, head_dim, window):
    half = head_dim // 2
    inv_freq = np.float32(1.0) / np.power(np.float32(10000.0), np.arange(0, head_dim, 2, dtype=np.float32) / np.float32(head_dim))
    freqs = np.outer(np.arange(T, dtype=np.float32), inv_freq.astype(np.float32))
    cos, sin = np.cos(freqs).T, np.sin(freqs).T
    cos2 = np.concatenate([cos, cos] * 2)
    sin2 = np.concatenate([-sin, sin] * 2)
    scale = head_dim ** -0.5
    rope = np.stack([cos2 * scale, sin2 * scale, cos2, sin2], axis=1).astype(np.float32)
    tiles, band = T // 128, 128 + window
    qry = np.arange(128)[:, None, None]
    tile = np.arange(tiles)[None, :, None]
    key = np.arange(band)[None, None, :]
    seen_q = (qry <= key) & (key <= qry + window) & (key + 128 * tile >= window)
    masks_q = np.where(seen_q, 0.0, MASKED).astype(np.float32).reshape(128, tiles * band)
    ahead = np.arange(band)[None, :] - np.arange(128)[:, None]
    seen_k = (ahead >= 0) & (ahead <= window)
    masks_k = np.tile(np.where(seen_k, 0.0, MASKED).astype(np.float32), (1, tiles // 2))
    return np.ascontiguousarray(rope), masks_q, masks_k


def l1_constants(T, heads, head_dim):
    inv_freq = np.float32(1.0) / np.power(np.float32(10000.0), np.arange(0, head_dim, 2, dtype=np.float32) / np.float32(head_dim))
    freqs = np.outer(np.arange(T, dtype=np.float32), inv_freq.astype(np.float32))
    cos, sin = np.cos(freqs).T, np.sin(freqs).T
    cos2 = np.repeat(np.concatenate([cos, cos]), heads, axis=0)
    sin2 = np.repeat(np.concatenate([-sin, sin]), heads, axis=0)
    scale = head_dim ** -0.5
    return np.stack([cos2 * scale, sin2 * scale, cos2, sin2], axis=1).astype(np.float32)


def by_dimension(w, heads, head_dim, swapped):
    w = w.reshape(*w.shape[:-1], heads, head_dim)
    if swapped:
        w = np.roll(w, head_dim // 2, axis=-1)
    return np.swapaxes(w, -1, -2).reshape(*w.shape[:-2], heads * head_dim)


def l1_weights(wqkv, bqkv, heads):
    c = wqkv.shape[0]
    d = c // heads
    q, k, v = (wqkv[:, n * c:(n + 1) * c] for n in range(3))
    bq, bk, bv = (bqkv[n * c:(n + 1) * c] for n in range(3))
    w = np.stack([by_dimension(a, heads, d, s) for a in (q, k) for s in (False, True)], axis=1)
    b = np.stack([by_dimension(a, heads, d, s) for a in (bq, bk) for s in (False, True)], axis=1)
    return w, b, v, bv.reshape(1, c)


def kernel(L0_attn_x, L0_attn_w_qkv, L0_attn_w_out, L0_ffn_centroids, L0_ffn_ln_g, L0_ffn_ln_b, L0_ffn_w1, L0_ffn_b1,
           L0_ffn_w2, L0_ffn_b2, L1_attn_Wqkv, L1_attn_bqkv, L1_attn_Wout, L1_attn_bout, L1_ffn_W1, L1_ffn_b1,
           L1_ffn_quantum_phases, L1_ffn_quantum_weights_real, L1_ffn_quantum_weights_imag, L1_ffn_W2, L1_ffn_b2):
    import ml_dtypes
    import concourse.bacc as _bacc
    from concourse.bass_utils import run_bass_kernel_spmd as _run

    nc = _bacc.Bacc("TRN2", target_bir_lowering=False, num_devices=1)
    arrays, a = {}, {}

    def give(name, array):
        array = np.ascontiguousarray(array)
        arrays[name] = array
        a[name] = nc.dram_tensor(name, array.shape, mybir.dt.from_np(array.dtype), kind="ExternalInput").ap()

    def columns(v):
        return np.asarray(v).reshape(-1, 128).T

    x = np.asarray(L0_attn_x)
    B, T, C = x.shape
    bf = ml_dtypes.bfloat16
    give("x", x)
    give("ident", np.eye(128, dtype=np.float32))
    give("ones", np.ones((128, 128), bf))
    give("before", np.triu(np.ones((128, 128)), 1).astype(bf))
    give("l0_w", np.asarray(L0_attn_w_qkv).T)
    give("l0_wo", np.asarray(L0_attn_w_out).T)
    rope, masks_q, masks_k = l0_constants(T, L0_HEAD, L0_WINDOW)
    give("l0_rope", rope)
    give("l0_masks_q", masks_q.astype(bf))
    give("l0_masks_k", masks_k.astype(bf))
    E, _, F = np.asarray(L0_ffn_w1).shape
    give("centroids", np.asarray(L0_ffn_centroids).T)
    give("ln_g", columns(L0_ffn_ln_g))
    give("ln_b", columns(L0_ffn_ln_b))
    give("e_w1", np.asarray(L0_ffn_w1))
    give("e_b1", np.asarray(L0_ffn_b1).reshape(E, F // 128, 128).transpose(0, 2, 1))
    give("e_w2", np.asarray(L0_ffn_w2))
    give("e_b2", np.asarray(L0_ffn_b2).reshape(E, C, 1))
    wqk, bqk, wv, bv = l1_weights(np.asarray(L1_attn_Wqkv), np.asarray(L1_attn_bqkv), L1_HEADS)
    give("l1_wqk", wqk)
    give("l1_bqk", bqk)
    give("l1_wv", wv)
    give("l1_bv", bv)
    give("l1_wo", np.asarray(L1_attn_Wout))
    give("l1_bo", np.asarray(L1_attn_bout).reshape(1, C))
    give("l1_rope", l1_constants(T, L1_HEADS, C // L1_HEADS))
    give("f_w1", np.asarray(L1_ffn_W1))
    give("f_b1", columns(L1_ffn_b1))
    give("f_phase", columns(L1_ffn_quantum_phases))
    give("f_real", columns(L1_ffn_quantum_weights_real))
    give("f_imag", columns(L1_ffn_quantum_weights_imag))
    give("f_w2", np.asarray(L1_ffn_W2))
    give("f_b2", columns(L1_ffn_b2))

    out = nc.dram_tensor("out_0_dram", x.shape, F32, kind="ExternalOutput").ap()
    program(nc, a, out.rearrange("b t c -> (b t) c"), B, T, C)
    return _run(nc, [arrays], core_ids=[0]).results[0]["out_0_dram"]
```
